# Optimizing a Trainium2 kernel written in Bass

```python
import numpy as np
import jax
import jax.numpy as jnp

def _softmax(x, axis=-1):
    return jax.nn.softmax(x, axis=axis)

def _gelu(x):
    return jax.nn.gelu(x, approximate=True)

def _silu(x):
    return jax.nn.silu(x)

def _sigmoid(x):
    return jax.nn.sigmoid(x)

def _layernorm(x, axis=-1, eps=1e-05):
    m = jnp.mean(x, axis=axis, keepdims=True)
    v = jnp.var(x, axis=axis, keepdims=True)
    return (x - m) / jnp.sqrt(v + eps)

def _scatter_add(tgt, idx, src, axis=0):
    return tgt.at[idx].add(src)

def _segment_sum(src, seg, n):
    return jax.ops.segment_sum(src, seg, n)
kernel_name = 'mk_gps_d2_gnn_r32_2279ad'

def setup_inputs(seed: int=0):
    np.random.seed(seed)
    _w = jnp.asarray

    def _rec_inputs():
        import jax
        import jax.numpy as jnp
        _gk = jax.random.key(seed)
        x = -0.0003713 + 1 * jax.random.normal(jax.random.fold_in(_gk, 1), (3125, 256), jnp.float32)
        src = jax.random.randint(jax.random.fold_in(_gk, 2), (50000,), 0, 3125, jnp.int32)
        dst = jax.random.randint(jax.random.fold_in(_gk, 3), (50000,), 0, 3125, jnp.int32)
        _o = jnp.argsort(dst, stable=True)
        src = src[_o]
        dst = dst[_o]
        return (x, src, dst)
    x, src, dst = _rec_inputs()

    def _L0_gnn_setup():
        import jax, jax.numpy as jnp
        import numpy as np
        N = 50000
        NEG_SLOPE = 0.2

        def _gat_conv(x, src, dst, W, a_src, a_dst, b, heads, out_c):
            n = x.shape[0]
            h = (x @ W).reshape(n, heads, out_c)
            s = jnp.einsum('nhc,hc->nh', h, a_src)
            d = jnp.einsum('nhc,hc->nh', h, a_dst)
            e = jax.nn.leaky_relu(s[src] + d[dst], NEG_SLOPE)
            e_max = jax.ops.segment_max(e, dst, num_segments=n)
            e = jnp.exp(e - e_max[dst])
            denom = jax.ops.segment_sum(e, dst, num_segments=n)
            alpha = e / (denom[dst] + 1e-16)
            msg = h[src] * alpha[:, :, None]
            out = jax.ops.segment_sum(msg, dst, num_segments=n)
            return out.reshape(n, heads * out_c) + b
        key = jax.random.key(seed)
        ks = jax.random.split(key, 11)
        E = 25000
        return {'x': jax.random.normal(ks[0], (N, 256), jnp.float32), 'edge_index': jax.random.randint(ks[1], (2, E), 0, N, jnp.int32), 'W1': jax.random.normal(ks[2], (256, 256), jnp.float32) * 0.06, 'att_src1': jax.random.normal(ks[3], (8, 32), jnp.float32) * 0.1, 'att_dst1': jax.random.normal(ks[4], (8, 32), jnp.float32) * 0.1, 'b1': jax.random.normal(ks[5], (256,), jnp.float32) * 0.02, 'W2': jax.random.normal(ks[6], (256, 256), jnp.float32) * 0.06, 'att_src2': jax.random.normal(ks[7], (1, 256), jnp.float32) * 0.05, 'att_dst2': jax.random.normal(ks[8], (1, 256), jnp.float32) * 0.05, 'b2': jax.random.normal(ks[9], (256,), jnp.float32) * 0.02}
    _L0_gnn_all = _L0_gnn_setup()
    _L0_gnn_in = {k: v for k, v in _L0_gnn_all.items() if k in ('W1', 'att_src1', 'att_dst1', 'b1', 'W2', 'att_src2', 'att_dst2', 'b2')}
    del _L0_gnn_all

    def _L0_mix_setup():
        import jax, jax.numpy as jnp
        import numpy as np
        NUM_HEADS = 8
        key = jax.random.key(seed)
        ks = jax.random.split(key, 5)
        B, N, C = (8, 512, 256)
        x = jax.random.normal(ks[0], (B, N, C), dtype=jnp.float32)
        Wq = jax.random.normal(ks[1], (C, C), dtype=jnp.float32) * 0.02
        Wkv = jax.random.normal(ks[2], (2 * C, C), dtype=jnp.float32) * 0.02
        Wproj = jax.random.normal(ks[3], (C, C), dtype=jnp.float32) * 0.02
        bproj = jnp.zeros((C,), dtype=jnp.float32)
        return {'x': x, 'Wq': Wq, 'Wkv': Wkv, 'Wproj': Wproj, 'bproj': bproj}
    _L0_mix_all = _L0_mix_setup()
    _L0_mix_in = {k: v for k, v in _L0_mix_all.items() if k in ('Wq', 'Wkv', 'Wproj', 'bproj')}
    del _L0_mix_all

    def _L0_ffn_setup():
        import jax, jax.numpy as jnp
        import numpy as np
        B, N, D = (16, 128, 256)
        NUM_EXPERTS, TOP_K, HEADS = (4, 2, 4)
        N_EDGES = 32768
        LN_EPS = 1e-05

        def _layernorm(x, g, b):
            mu = x.mean(-1, keepdims=True)
            var = ((x - mu) ** 2).mean(-1, keepdims=True)
            return (x - mu) * jax.lax.rsqrt(var + LN_EPS) * g + b

        def _forward(x, edge_index, W_gat, att_src, att_dst, b_gat, ln_gamma, ln_beta, W1, b1, W2, b2):
            Bc, Nc, Dc = x.shape
            M = Bc * Nc
            x_flat = x.reshape(M, Dc)
            h = (x_flat @ W_gat).reshape(M, HEADS, NUM_EXPERTS)
            loops = jnp.arange(M, dtype=edge_index.dtype)
            src = jnp.concatenate([edge_index[0], loops])
            dst = jnp.concatenate([edge_index[1], loops])
            a_src = (h * att_src).sum(-1)
            a_dst = (h * att_dst).sum(-1)
            e = jax.nn.leaky_relu(a_src[src] + a_dst[dst], negative_slope=0.2)
            e_max = jax.ops.segment_max(e, dst, num_segments=M)
            ee = jnp.exp(e - e_max[dst])
            denom = jax.ops.segment_sum(ee, dst, num_segments=M)
            alpha = ee / (denom[dst] + 1e-16)
            msg = h[src] * alpha[:, :, None]
            agg = jax.ops.segment_sum(msg, dst, num_segments=M).reshape(M, HEADS * NUM_EXPERTS) + b_gat
            scores = _layernorm(agg, ln_gamma, ln_beta).reshape(M, HEADS, NUM_EXPERTS).mean(1)
            scores = scores.reshape(Bc, Nc, NUM_EXPERTS)
            topk_s, topk_i = jax.lax.top_k(scores, TOP_K)
            w = jax.nn.softmax(topk_s, axis=-1)
            out = jnp.zeros_like(x)
            for ei in range(NUM_EXPERTS):
                g = jnp.where(topk_i == ei, w, 0.0).sum(-1)
                hh = jax.nn.gelu(x @ W1[ei] + b1[ei], approximate=False)
                out = out + g[..., None] * (hh @ W2[ei] + b2[ei])
            return out
        key = jax.random.key(seed)
        ks = jax.random.split(key, 8)
        s = 0.05
        return {'x': jax.random.normal(ks[0], (B, N, D), jnp.float32), 'W_gat': jax.random.normal(ks[1], (D, HEADS * NUM_EXPERTS), jnp.float32) * s, 'att_src': jax.random.normal(ks[2], (HEADS, NUM_EXPERTS), jnp.float32) * s, 'att_dst': jax.random.normal(ks[3], (HEADS, NUM_EXPERTS), jnp.float32) * s, 'b_gat': jnp.zeros((HEADS * NUM_EXPERTS,), jnp.float32), 'ln_gamma': jnp.ones((HEADS * NUM_EXPERTS,), jnp.float32), 'ln_beta': jnp.zeros((HEADS * NUM_EXPERTS,), jnp.float32), 'W1': jax.random.normal(ks[4], (NUM_EXPERTS, D, 2 * D), jnp.float32) * s, 'b1': jnp.zeros((NUM_EXPERTS, 2 * D), jnp.float32), 'W2': jax.random.normal(ks[5], (NUM_EXPERTS, 2 * D, D), jnp.float32) * s, 'b2': jnp.zeros((NUM_EXPERTS, D), jnp.float32), 'edge_index': jax.random.randint(ks[6], (2, N_EDGES), 0, B * N, jnp.int32)}
    _L0_ffn_all = _L0_ffn_setup()
    _L0_ffn_in = {k: v for k, v in _L0_ffn_all.items() if k in ('W_gat', 'att_src', 'att_dst', 'b_gat', 'ln_gamma', 'ln_beta', 'W1', 'b1', 'W2', 'b2', 'edge_index')}
    del _L0_ffn_all

    def _L1_gnn_setup():
        import jax, jax.numpy as jnp
        import numpy as np
        N_NODES = 3125
        N_EDGES = 50000
        D_IN = 256
        HEADS = 8
        D_HEAD = 32
        NEG_SLOPE = 0.2
        BN_EPS = 1e-05
        key = jax.random.key(seed)
        ks = jax.random.split(key, 8)
        x = jax.random.normal(ks[0], (N_NODES, D_IN), dtype=jnp.float32)
        edge_index = jax.random.randint(ks[1], (2, N_EDGES), 0, N_NODES, dtype=jnp.int32)
        W = jax.random.normal(ks[2], (D_IN, HEADS * D_HEAD), dtype=jnp.float32) / np.sqrt(D_IN)
        att_src = jax.random.normal(ks[3], (HEADS, D_HEAD), dtype=jnp.float32) / np.sqrt(D_HEAD)
        att_dst = jax.random.normal(ks[4], (HEADS, D_HEAD), dtype=jnp.float32) / np.sqrt(D_HEAD)
        bias = jax.random.normal(ks[5], (HEADS * D_HEAD,), dtype=jnp.float32) * 0.01
        gamma = jnp.ones((HEADS * D_HEAD,), dtype=jnp.float32)
        beta = jnp.zeros((HEADS * D_HEAD,), dtype=jnp.float32)
        return {'x': x, 'edge_index': edge_index, 'W': W, 'att_src': att_src, 'att_dst': att_dst, 'bias': bias, 'gamma': gamma, 'beta': beta}
    _L1_gnn_all = _L1_gnn_setup()
    _L1_gnn_in = {k: v for k, v in _L1_gnn_all.items() if k in ('W', 'att_src', 'att_dst', 'bias', 'gamma', 'beta')}
    del _L1_gnn_all

    def _L1_mix_setup():
        import jax, jax.numpy as jnp
        import numpy as np
        HEADS = 8
        EPS = 1e-05

        def _ln(t, w, b, headc):
            m = jnp.mean(t, axis=-1, keepdims=True)
            d = t - m
            std = jnp.sqrt(jnp.sum(d * d, axis=-1, keepdims=True) / (headc - 1))
            return w * (d / (std + EPS)) + b
        key = jax.random.key(seed)
        B, N, C = (32, 128, 256)
        headc = C // HEADS
        x = jax.random.normal(key, (B, N, C), dtype=jnp.float32)
        return {'x': x, 'kln_weight': jnp.ones((HEADS, 1, headc), dtype=jnp.float32), 'kln_bias': jnp.zeros((HEADS, 1, headc), dtype=jnp.float32), 'vln_weight': jnp.ones((HEADS, 1, headc), dtype=jnp.float32), 'vln_bias': jnp.zeros((HEADS, 1, headc), dtype=jnp.float32)}
    _L1_mix_all = _L1_mix_setup()
    _L1_mix_in = {k: v for k, v in _L1_mix_all.items() if k in ('kln_weight', 'kln_bias', 'vln_weight', 'vln_bias')}
    del _L1_mix_all

    def _L1_ffn_setup():
        import jax, jax.numpy as jnp
        import numpy as np
        B, K, D = (512, 16, 256)
        E = 32
        H = int(D * 0.25)
        key = jax.random.key(seed)
        ks = jax.random.split(key, 7)
        d_rs = D ** (-0.5)
        h_rs = H ** (-0.5)
        x = jax.random.normal(ks[0], (B, K, D), dtype=jnp.float32)
        router_w = jax.random.uniform(ks[1], (E, D), jnp.float32, -d_rs, d_rs)
        router_b = jax.random.uniform(ks[2], (E,), jnp.float32, -d_rs, d_rs)
        W1 = jax.random.uniform(ks[3], (E, D, H), jnp.float32, -h_rs, h_rs)
        b1 = jax.random.uniform(ks[4], (E, H), jnp.float32, -h_rs, h_rs)
        W2 = jax.random.uniform(ks[5], (E, H, D), jnp.float32, -d_rs, d_rs)
        b2 = jax.random.uniform(ks[6], (E, D), jnp.float32, -d_rs, d_rs)
        return {'x': x, 'router_w': router_w, 'router_b': router_b, 'W1': W1, 'b1': b1, 'W2': W2, 'b2': b2}
    _L1_ffn_all = _L1_ffn_setup()
    _L1_ffn_in = {k: v for k, v in _L1_ffn_all.items() if k in ('router_w', 'router_b', 'W1', 'b1', 'W2', 'b2')}
    del _L1_ffn_all
    return {'x': x, 'src': src, 'dst': dst, 'L0_gnn_W1': _L0_gnn_in['W1'], 'L0_gnn_att_src1': _L0_gnn_in['att_src1'], 'L0_gnn_att_dst1': _L0_gnn_in['att_dst1'], 'L0_gnn_b1': _L0_gnn_in['b1'], 'L0_gnn_W2': _L0_gnn_in['W2'], 'L0_gnn_att_src2': _L0_gnn_in['att_src2'], 'L0_gnn_att_dst2': _L0_gnn_in['att_dst2'], 'L0_gnn_b2': _L0_gnn_in['b2'], 'L0_mix_Wq': _L0_mix_in['Wq'], 'L0_mix_Wkv': _L0_mix_in['Wkv'], 'L0_mix_Wproj': _L0_mix_in['Wproj'], 'L0_mix_bproj': _L0_mix_in['bproj'], 'L0_ffn_W_gat': _L0_ffn_in['W_gat'], 'L0_ffn_att_src': _L0_ffn_in['att_src'], 'L0_ffn_att_dst': _L0_ffn_in['att_dst'], 'L0_ffn_b_gat': _L0_ffn_in['b_gat'], 'L0_ffn_ln_gamma': _L0_ffn_in['ln_gamma'], 'L0_ffn_ln_beta': _L0_ffn_in['ln_beta'], 'L0_ffn_W1': _L0_ffn_in['W1'], 'L0_ffn_b1': _L0_ffn_in['b1'], 'L0_ffn_W2': _L0_ffn_in['W2'], 'L0_ffn_b2': _L0_ffn_in['b2'], 'L0_ffn_edge_index': _L0_ffn_in['edge_index'], 'L1_gnn_W': _L1_gnn_in['W'], 'L1_gnn_att_src': _L1_gnn_in['att_src'], 'L1_gnn_att_dst': _L1_gnn_in['att_dst'], 'L1_gnn_bias': _L1_gnn_in['bias'], 'L1_gnn_gamma': _L1_gnn_in['gamma'], 'L1_gnn_beta': _L1_gnn_in['beta'], 'L1_mix_kln_weight': _L1_mix_in['kln_weight'], 'L1_mix_kln_bias': _L1_mix_in['kln_bias'], 'L1_mix_vln_weight': _L1_mix_in['vln_weight'], 'L1_mix_vln_bias': _L1_mix_in['vln_bias'], 'L1_ffn_router_w': _L1_ffn_in['router_w'], 'L1_ffn_router_b': _L1_ffn_in['router_b'], 'L1_ffn_W1': _L1_ffn_in['W1'], 'L1_ffn_b1': _L1_ffn_in['b1'], 'L1_ffn_W2': _L1_ffn_in['W2'], 'L1_ffn_b2': _L1_ffn_in['b2']}

def reference(x, src, dst, L0_gnn_W1, L0_gnn_att_src1, L0_gnn_att_dst1, L0_gnn_b1, L0_gnn_W2, L0_gnn_att_src2, L0_gnn_att_dst2, L0_gnn_b2, L0_mix_Wq, L0_mix_Wkv, L0_mix_Wproj, L0_mix_bproj, L0_ffn_W_gat, L0_ffn_att_src, L0_ffn_att_dst, L0_ffn_b_gat, L0_ffn_ln_gamma, L0_ffn_ln_beta, L0_ffn_W1, L0_ffn_b1, L0_ffn_W2, L0_ffn_b2, L0_ffn_edge_index, L1_gnn_W, L1_gnn_att_src, L1_gnn_att_dst, L1_gnn_bias, L1_gnn_gamma, L1_gnn_beta, L1_mix_kln_weight, L1_mix_kln_bias, L1_mix_vln_weight, L1_mix_vln_bias, L1_ffn_router_w, L1_ffn_router_b, L1_ffn_W1, L1_ffn_b1, L1_ffn_W2, L1_ffn_b2):
    import jax
    import jax.numpy as jnp

    def _L0_gnn_ref(x, edge_index, W1, att_src1, att_dst1, b1, W2, att_src2, att_dst2, b2):
        import jax, jax.numpy as jnp
        import numpy as np
        N = 50000
        NEG_SLOPE = 0.2

        def _gat_conv(x, src, dst, W, a_src, a_dst, b, heads, out_c):
            n = x.shape[0]
            h = (x @ W).reshape(n, heads, out_c)
            s = jnp.einsum('nhc,hc->nh', h, a_src)
            d = jnp.einsum('nhc,hc->nh', h, a_dst)
            e = jax.nn.leaky_relu(s[src] + d[dst], NEG_SLOPE)
            e_max = jax.ops.segment_max(e, dst, num_segments=n)
            e = jnp.exp(e - e_max[dst])
            denom = jax.ops.segment_sum(e, dst, num_segments=n)
            alpha = e / (denom[dst] + 1e-16)
            msg = h[src] * alpha[:, :, None]
            out = jax.ops.segment_sum(msg, dst, num_segments=n)
            return out.reshape(n, heads * out_c) + b
        n = x.shape[0]
        loop = jnp.arange(n, dtype=edge_index.dtype)
        src = jnp.concatenate([edge_index[0], loop])
        dst = jnp.concatenate([edge_index[1], loop])
        h = _gat_conv(x, src, dst, W1, att_src1, att_dst1, b1, heads=8, out_c=32)
        h = jax.nn.relu(h)
        out = _gat_conv(h, src, dst, W2, att_src2, att_dst2, b2, heads=1, out_c=256)
        return out

    def _L0_mix_ref(x, Wq, Wkv, Wproj, bproj):
        import jax, jax.numpy as jnp
        import numpy as np
        NUM_HEADS = 8
        B, N, C = x.shape
        h = NUM_HEADS
        d = C // h
        q = jnp.einsum('bnc,oc->bno', x, Wq).reshape(B, N, h, d).transpose(0, 2, 1, 3)
        kv = jnp.einsum('bnc,oc->bno', x, Wkv).reshape(B, N, 2, h, d)
        k = kv[:, :, 0].transpose(0, 2, 1, 3)
        v = kv[:, :, 1].transpose(0, 2, 1, 3)
        q = jax.nn.elu(q) + 1.0
        k = jax.nn.elu(k) + 1.0
        k_sum = k.sum(axis=2)
        D_inv = 1.0 / jnp.maximum(jnp.einsum('bhnd,bhd->bhn', q, k_sum), 1e-06)
        context = jnp.einsum('bhnd,bhne->bhde', k, v)
        attn = jnp.einsum('bhnd,bhde->bhne', q, context) * D_inv[..., None]
        out = attn.transpose(0, 2, 1, 3).reshape(B, N, C)
        out = jnp.einsum('bnc,oc->bno', out, Wproj) + bproj
        return out

    def _L0_ffn_ref(x, W_gat, att_src, att_dst, b_gat, ln_gamma, ln_beta, W1, b1, W2, b2, edge_index):
        import jax, jax.numpy as jnp
        import numpy as np
        B, N, D = (16, 128, 256)
        NUM_EXPERTS, TOP_K, HEADS = (4, 2, 4)
        N_EDGES = 32768
        LN_EPS = 1e-05

        def _layernorm(x, g, b):
            mu = x.mean(-1, keepdims=True)
            var = ((x - mu) ** 2).mean(-1, keepdims=True)
            return (x - mu) * jax.lax.rsqrt(var + LN_EPS) * g + b

        def _forward(x, edge_index, W_gat, att_src, att_dst, b_gat, ln_gamma, ln_beta, W1, b1, W2, b2):
            Bc, Nc, Dc = x.shape
            M = Bc * Nc
            x_flat = x.reshape(M, Dc)
            h = (x_flat @ W_gat).reshape(M, HEADS, NUM_EXPERTS)
            loops = jnp.arange(M, dtype=edge_index.dtype)
            src = jnp.concatenate([edge_index[0], loops])
            dst = jnp.concatenate([edge_index[1], loops])
            a_src = (h * att_src).sum(-1)
            a_dst = (h * att_dst).sum(-1)
            e = jax.nn.leaky_relu(a_src[src] + a_dst[dst], negative_slope=0.2)
            e_max = jax.ops.segment_max(e, dst, num_segments=M)
            ee = jnp.exp(e - e_max[dst])
            denom = jax.ops.segment_sum(ee, dst, num_segments=M)
            alpha = ee / (denom[dst] + 1e-16)
            msg = h[src] * alpha[:, :, None]
            agg = jax.ops.segment_sum(msg, dst, num_segments=M).reshape(M, HEADS * NUM_EXPERTS) + b_gat
            scores = _layernorm(agg, ln_gamma, ln_beta).reshape(M, HEADS, NUM_EXPERTS).mean(1)
            scores = scores.reshape(Bc, Nc, NUM_EXPERTS)
            topk_s, topk_i = jax.lax.top_k(scores, TOP_K)
            w = jax.nn.softmax(topk_s, axis=-1)
            out = jnp.zeros_like(x)
            for ei in range(NUM_EXPERTS):
                g = jnp.where(topk_i == ei, w, 0.0).sum(-1)
                hh = jax.nn.gelu(x @ W1[ei] + b1[ei], approximate=False)
                out = out + g[..., None] * (hh @ W2[ei] + b2[ei])
            return out
        return _forward(x, edge_index, W_gat, att_src, att_dst, b_gat, ln_gamma, ln_beta, W1, b1, W2, b2)

    def _L1_gnn_ref(x, edge_index, W, att_src, att_dst, bias, gamma, beta):
        import jax, jax.numpy as jnp
        import numpy as np
        N_NODES = 3125
        N_EDGES = 50000
        D_IN = 256
        HEADS = 8
        D_HEAD = 32
        NEG_SLOPE = 0.2
        BN_EPS = 1e-05
        N = x.shape[0]
        H, D = att_src.shape
        xh = (x @ W).reshape(N, H, D)
        a_src = jnp.einsum('nhd,hd->nh', xh, att_src)
        a_dst = jnp.einsum('nhd,hd->nh', xh, att_dst)
        loops = jnp.arange(N, dtype=edge_index.dtype)
        src = jnp.concatenate([edge_index[0], loops])
        dst = jnp.concatenate([edge_index[1], loops])
        e = jax.nn.leaky_relu(a_src[src] + a_dst[dst], NEG_SLOPE)
        m = jax.ops.segment_max(e, dst, num_segments=N)
        e = jnp.exp(e - m[dst])
        denom = jax.ops.segment_sum(e, dst, num_segments=N)
        alpha = e / denom[dst]
        msg = xh[src] * alpha[:, :, None]
        out = jax.ops.segment_sum(msg, dst, num_segments=N).reshape(N, H * D) + bias
        mean = jnp.mean(out, axis=0)
        var = jnp.var(out, axis=0)
        out = (out - mean) * jax.lax.rsqrt(var + BN_EPS) * gamma + beta
        return out + x

    def _L1_mix_ref(x, kln_weight, kln_bias, vln_weight, vln_bias):
        import jax, jax.numpy as jnp
        import numpy as np
        HEADS = 8
        EPS = 1e-05

        def _ln(t, w, b, headc):
            m = jnp.mean(t, axis=-1, keepdims=True)
            d = t - m
            std = jnp.sqrt(jnp.sum(d * d, axis=-1, keepdims=True) / (headc - 1))
            return w * (d / (std + EPS)) + b
        B, N, C = x.shape
        headc = C // HEADS
        qkv = x.reshape(B, N, HEADS, headc).transpose(0, 2, 1, 3)
        k = _ln(qkv, kln_weight, kln_bias, headc)
        v = _ln(qkv, vln_weight, vln_bias, headc)
        kv = jnp.einsum('bhnd,bhne->bhde', k, v) / N
        out = jnp.einsum('bhnd,bhde->bhne', qkv, kv)
        out = out.transpose(0, 2, 1, 3).reshape(B, N, C)
        return out + x

    def _L1_ffn_ref(x, router_w, router_b, W1, b1, W2, b2):
        import jax, jax.numpy as jnp
        import numpy as np
        B, K, D = (512, 16, 256)
        E = 32
        H = int(D * 0.25)
        xf = x.reshape(-1, D)
        logits = xf @ router_w.T + router_b
        idx = jnp.argmax(logits, axis=-1)
        w1t = jnp.take(W1, idx, axis=0)
        h = jnp.einsum('nd,ndh->nh', xf, w1t) + jnp.take(b1, idx, axis=0)
        h = jax.nn.relu(h)
        w2t = jnp.take(W2, idx, axis=0)
        out = jnp.einsum('nh,nhd->nd', h, w2t) + jnp.take(b2, idx, axis=0)
        out = jax.nn.relu(out)
        return out.reshape(x.shape)
    edge_index = jnp.stack([src, dst])
    xn = _layernorm(x, axis=-1)
    x = x + _L0_gnn_ref(xn, edge_index, L0_gnn_W1, L0_gnn_att_src1, L0_gnn_att_dst1, L0_gnn_b1, L0_gnn_W2, L0_gnn_att_src2, L0_gnn_att_dst2, L0_gnn_b2) + _L0_mix_ref(xn[None], L0_mix_Wq, L0_mix_Wkv, L0_mix_Wproj, L0_mix_bproj)[0]
    x = x + _L0_ffn_ref(_layernorm(x, axis=-1)[None], L0_ffn_W_gat, L0_ffn_att_src, L0_ffn_att_dst, L0_ffn_b_gat, L0_ffn_ln_gamma, L0_ffn_ln_beta, L0_ffn_W1, L0_ffn_b1, L0_ffn_W2, L0_ffn_b2, L0_ffn_edge_index)[0]
    xn = _layernorm(x, axis=-1)
    x = x + _L1_gnn_ref(xn, edge_index, L1_gnn_W, L1_gnn_att_src, L1_gnn_att_dst, L1_gnn_bias, L1_gnn_gamma, L1_gnn_beta) + _L1_mix_ref(xn[None], L1_mix_kln_weight, L1_mix_kln_bias, L1_mix_vln_weight, L1_mix_vln_bias)[0]
    x = x + _L1_ffn_ref(_layernorm(x, axis=-1)[None], L1_ffn_router_w, L1_ffn_router_b, L1_ffn_W1, L1_ffn_b1, L1_ffn_W2, L1_ffn_b2)[0]
    return x

_drawn_inputs = setup_inputs


def setup_inputs(seed=0):
    import zlib

    import numpy as np

    out = dict(_drawn_inputs(seed))
    spreads = {'L0_mix_bproj': (0.0, 0.1),
     'L0_ffn_b_gat': (0.0, 0.1),
     'L0_ffn_ln_gamma': (1.0, 0.2),
     'L0_ffn_ln_beta': (0.0, 0.1),
     'L0_ffn_b1': (0.0, 0.1),
     'L0_ffn_b2': (0.0, 0.1),
     'L1_gnn_gamma': (1.0, 0.2),
     'L1_gnn_beta': (0.0, 0.3),
     'L1_mix_kln_weight': (1.0, 0.2),
     'L1_mix_kln_bias': (0.0, 0.281),
     'L1_mix_vln_weight': (1.0, 0.2),
     'L1_mix_vln_bias': (0.0, 0.1)}
    factors = {'L0_gnn_att_dst1': 2.777,
     'L0_gnn_att_src2': 5.274,
     'L0_gnn_att_dst2': 7.643,
     'L0_mix_Wq': 8.0,
     'L0_mix_Wkv': 6.285,
     'L0_mix_Wproj': 4.809,
     'L1_gnn_bias': 64.0,
     'L1_ffn_router_b': 4.943,
     'L1_ffn_b1': 27.008,
     'L1_ffn_b2': 8.0}
    for name, (base, spread) in spreads.items():
        noise = np.random.default_rng([zlib.crc32(name.encode()), seed]).standard_normal(out[name].shape)
        drawn = base * np.exp(spread * noise) if base else spread * noise
        out[name] = jnp.asarray(drawn.astype(out[name].dtype))
    for name, factor in factors.items():
        out[name] = (out[name] * factor).astype(out[name].dtype)
    return out
```

```python
from contextlib import ExitStack

import concourse.bass as bass
import numpy as np
from concourse import mybir
from concourse.alu_op_type import AluOpType as ALU

F32 = mybir.dt.float32
BF16 = mybir.dt.bfloat16
I32 = mybir.dt.int32
ACT = mybir.ActivationFunctionType
AX = mybir.AxisListType.X

P = 128
N = 3125
T = -(-N // P)
TAIL = N - (T - 1) * P
C = 256
H8 = 8
NEG = -1.0e30
SLOPE = 0.2
IDX = 4096
PADV = (IDX - 1) * IDX
G = 8
S2 = G // 2
AHEAD = 3
NBUF = 4
EW = 19
FFN_NODES = 16 * 128
EXP0, F0 = 4, 512
EXP1, F1 = 32, 64
TB = 5
TOK = TB * P


class EdgeSet:

    def __init__(self, name, edges, tiles, j, c):
        self.name, self.edges, self.tiles, self.J = name, edges, tiles, j
        self.W = c + 16
        self.Q = 16 * j
        self.groups = -(-(-(-edges // (2 * P)) + tiles - 1) // (S2 * NBUF)) * NBUF
        self.steps = self.groups * S2
        assert self.Q * P >= edges + 2 * P
        self.L = j * P


MAIN = EdgeSet("m", 50000, T, 25, 256)
FFN = EdgeSet("f", 32768, FFN_NODES // P, 17, 16)
GATS = [(MAIN, 256), (MAIN, 256), (FFN, 16), (MAIN, 256)]

PASSES = [("prep_m", 12), ("prep_f", 9), ("wT", 8)]


def _passes():
    out = list(PASSES)
    for g, (es, c) in enumerate(GATS):
        out.append((f"xT{g}", T))
        if g == 3:
            out += [("mix1o", T)]
        if g == 0:
            out += [("q", 2 * TB * 2), ("kv", T), ]
        out.append((f"h{g}", T))
        if g == 0:
            out += [("mixo", T), ("aT", T), ("proj", T)]
        out += [(f"sA{g}", -(-es.J // 4)), (f"sB{g}", -(-es.J // 4))]
    out += [("bnm", 1), ("bnv", 1), ("xT4", T), ("rt", T), ("ohT", T)]
    base, at = {}, 5
    for n, k in out:
        base[n] = (at, k)
        at += k
    return base


BASE = _passes()


def groups_before(g):
    return sum(es.groups for es, _ in GATS[:g])


def build(nc, A, out):
    ctx = ExitStack()
    with ctx:
        def sb(name, shape, dt=F32):
            return ctx.enter_context(nc.sbuf_tensor(name, shape, dt))

        def dram(name, shape, dt=F32):
            return nc.dram_tensor(name, shape, dt, kind="Internal").ap()

        sems = {}

        def S(name):
            if name not in sems:
                sems[name] = ctx.enter_context(nc.semaphore(name))
            return sems[name]

        arena = sb("arena", [P, 29904])
        R1 = arena[:, 0:6800]
        R2 = arena[:, 6800:13600]
        R4 = arena[:, 13600:21200]
        R3 = arena[:, 21200:29904]
        X = sb("X", [P, T, C])
        oneh = sb("oneh", [P, 2, G, P])
        onehB = sb("onehB", [P, 2, G, P], BF16)
        onehT = sb("onehT", [P, G, P], BF16)
        identB = sb("identB", [P, P], BF16)
        iotaB = sb("iotaB", [P, P], BF16)
        dS = sb("dS", [P, T, 3, H8], BF16)
        ident = sb("ident", [P, P])
        ones = sb("ones", [P, P])
        iota = sb("iota", [P, MAIN.Q])
        stage = sb("stage", [P, NBUF, G, EW])
        idx = sb("idx", [P, NBUF, G], I32)
        idx_s = sb("idx_s", [P, 2, G], I32)
        dat_s = sb("dat_s", [P, 2, G], I32)
        padT = sb("padT", [P, 16], I32)
        sg = sb("sg", [P, 2, G, H8])
        zz = sb("zz", [P, G, 2, H8])
        zd = sb("zd", [P, G, H8])
        drel = sb("drel", [P, 2, G])
        Wn = sb("Wn", [P, 2, C])
        brow = sb("brow", [P, 4, C])
        dsb = {e.name: sb("dsb_" + e.name, [P, 3, e.Q]) for e in (MAIN, FFN)}
        srcI = {e.name: sb("srcI_" + e.name, [P, e.Q], I32) for e in (MAIN, FFN)}
        flagA = {e.name: sb("flagA_" + e.name, [P, e.L + 1], BF16) for e in (MAIN, FFN)}
        seam = {e.name: sb("seam_" + e.name, [1, 4, H8, 16]) for e in (MAIN, FFN)}
        t128 = {e.name: sb("t128_" + e.name, [P, e.steps]) for e in (MAIN, FFN)}
        steps = {e.name: sb("steps_" + e.name, [65, e.steps], I32) for e in (MAIN, FFN)}
        tI, tP, cI = ({k: v[32 * q:32 * q + 1, :] for k, v in steps.items()} for q in range(3))
        rowc = sb("rowc", [1, 3, H8, 16])
        chan = sb("chan", [P, 1])
        zrow = oneh[:, :, :, :].rearrange("p a b c -> p (a b c)")[0:1, 1024:1536]
        rowsum = sb("rowsum", [P, 200])
        small3 = oneh[:, :, :, :].rearrange("p a b c -> p (a b c)")[:, 0:4 * T * H8].rearrange(
            "p (q t h) -> p q t h", q=4, t=T)
        small4 = onehT[:, :, :].rearrange("p a b -> p (a b)").bitcast(F32)
        carry = sb("carry", [P, 1])
        mv = sb("mv", [P, T, 2])
        st6 = sb("st6", [P, TB, 6])
        rstd = sb("rstd", [P, T])
        epsc = sb("epsc", [P, 1])
        BD = sb("BD", [P, 2, 132])
        mask = sb("mask", [P, 132])
        b1T = sb("b1T", [P, 16])
        rwT = sb("rwT", [P, 2, EXP1])
        gates = sb("gates", [P, T, EXP0])
        dcol = sb("dcol", [P, 8])
        PS = ctx.enter_context(nc.psum_tensor("PS", [P, 8, 512], F32))

        def Hv(c):
            return R2[:, 0:T * (c + 16)].rearrange("p (t w) -> p t w", t=T)

        def Av(c):
            return R1[:, 0:T * (c + 16)].rearrange("p (t w) -> p t w", t=T)

        def nodes(region):
            return region[:, 0:T * C].rearrange("p (t c) -> p t c", t=T)

        XT = R3[:, 0:2 * T * P].rearrange("p (k n) -> p k n", k=2)

        def EV(es):
            return R4[:, 0:es.Q * EW].rearrange("p (q w) -> p q w", w=EW)

        def rows(g):
            w, at = GATS[g][1] + 16, (2 * T * P if g == 2 else 0)
            return R3[:, at:at + NBUF * G * w].rearrange("p (b u w) -> p b u w", b=NBUF, u=G)

        def scan_bufs(g):
            L = GATS[g][0].L
            return (R1[:, 1000:1000 + L], R1[:, 3200:3200 + L]) if g == 2 else (R3[:, 0:L], R3[:, 3200:3200 + L])

        def s_cols(g):
            L = GATS[g][0].L
            return R4[:, 5200:5200 + L] if g == 2 else R1[:, 0:L]

        pk = {e.name: dram("pk_" + e.name, (e.Q * P + P,), I32) for e in (MAIN, FFN)}
        srt1 = dram("srt1", (FFN.edges, 1), I32)
        srt2 = dram("srt2", (FFN.edges, 1), I32)
        tab = [dram(f"tab{g}", (T * P, c + 8)) for g, (_, c) in enumerate(GATS)]
        stab = [dram(f"stab{g}", (T * P, H8)) for g in range(4)]

        SC = FFN.edges // P
        DIGITS = ((12, 64), (18, 32))
        sortO = R3.bitcast(BF16)[:, 0:64 * SC]
        sortH = arena[:, 0:64 * SC]
        sx = arena[:, 16384:21200]
        srtV = sx[:, 0:SC].bitcast(I32)
        srtT = sx[:, SC:2 * SC].bitcast(I32)
        srtD = sx[:, 2 * SC:3 * SC]
        srtP = sx[:, 3 * SC:4 * SC]
        srtI = sx[:, 4 * SC:5 * SC].bitcast(I32)
        sGl = sx[:, 5 * SC:5 * SC + 64]
        sCnt = sx[:, 5 * SC + 64:5 * SC + 128]
        sGex = sx[:, 5 * SC + 128:5 * SC + 192]
        sXo = sx[:, 5 * SC + 192:5 * SC + 256]
        ltri = sx[:, 6 * SC:6 * SC + 128]
        offd = sx[:, 6 * SC + 128:6 * SC + 256]
        pkS = R3[0:125, 0:400].bitcast(I32)
        pkD = R3[0:125, 400:800].bitcast(I32)

        def prepv(es):
            nb = -(-es.Q // P)
            return [nb] + [R1[:, k * 512:k * 512 + nb * P].rearrange("p (b i) -> p b i", b=nb) for k in range(4)]

        sel0 = R1[:, 2048:2048 + 128]
        cmpT = R1[:, 2304:2304 + MAIN.Q]
        small = R1[:, 3000:3032]
        tS = R1[:, 3200:3200 + 2 * MAIN.steps]
        pkA = R2[:, 0:3200]
        dA = R2[:, 3200:6400]
        fA = R4[:, 0:3200]

        wraw = R1[:, 0:2048].rearrange("p (o c) -> p o c", o=8)
        wT = R3[:, 6400:8448].rearrange("p (k o m) -> p k o m", k=2, o=8)
        qT = R4[:, 0:2 * T * P].rearrange("p (k n) -> p k n", k=2)
        K0 = nodes(R1)
        V0 = R2[:, 0:T * 258].rearrange("p (t a w) -> p t a w", t=T, a=2)
        AO = nodes(R1)
        eluT = oneh[:, :, :, :].rearrange("p a b c -> p (a b c)")
        K1, V1 = nodes(R1), nodes(R4)
        W1e = R4[:, 0:4096].rearrange("p (e k f) -> p e k f", e=EXP0, k=2)
        W2e = R2[:, 0:4096].rearrange("p (e k f) -> p e k f", e=EXP0, k=4)
        hh = R1[:, 0:2 * 4 * TOK].rearrange("p (b f n) -> p b f n", b=2, f=4)
        b1e = R2[0:16, 4096:4224]
        b2e = R2[0:1, 4300:4300 + 1024]
        W1x = R4[:, 0:4096].rearrange("p (k m) -> p k m", k=2)
        W2r = R2[:, 0:4096].rearrange("p (j c) -> p j c", j=16)
        b1r = R2[0:16, 4096:4224]
        b2r = R2[0:32, 4300:4556]
        rwr = R2[0:32, 4600:4856]
        ohE = R4[0:32, 4100:4100 + T * P]
        selE = R3[0:32, 6400:6400 + 2048].rearrange("p (e m) -> p e m", e=32)
        selJ = R3[0:32, 6400:6400 + 2048].rearrange("p (j m) -> p j m", j=16)
        hm = R1[:, 0:2 * TOK].rearrange("p (b n) -> p b n", b=2)
        ohS = R1[0:32, 2000:2000 + TOK]
        ha = R1[:, 1300:1300 + TOK].rearrange("p (b n) -> p b n", b=2)

        block = ctx.enter_context(nc.Block())

        def offsets(engine, table, step, n, last):
            return nc.values_load_multi_w_load_instructions(
                table[:, at(step, n)], engines=(engine,), min_val=0, max_val=last, bass_reorder=False,
                skip_runtime_bounds_check_because="the tables are clamped when they are built")[1]

        def at(start, n):
            return slice(start, start + n) if isinstance(start, int) else bass.ds(start, n)

        def bank(b):
            return PS[:, b, :]

        class Chain:

            def __init__(self, eng, name):
                self.eng, self.sem, self.n, self.i, self.k0 = eng, S(name), 0, None, 0

            def value(self):
                return self.n if self.i is None else self.i * self.K + self.n

            def __call__(self, ins):
                ins.then_inc(self.sem, 1)
                self.n += 1
                self.eng.wait_ge(self.sem, self.value())

            def loop(self, count, per, body, first=0):
                self.n -= first * per
                n0 = self.n
                with self.eng.Fori(first, count) as i:
                    self.i, self.K = i, per
                    body(i)
                    assert self.n - n0 == per, (self.n - n0, per)
                    self.i = None
                self.n = n0 + per * count

        def consume(eng, name, fn):
            base, n = BASE[name]
            if n == T:
                with eng.Fori(0, T // TB) as i:
                    for k in range(TB):
                        t = i * TB + k
                        eng.wait_ge(S("bank_full"), t + (base - 4))
                        fn(t, k).then_inc(S("bank_free"), 1)
            else:
                for t in range(n):
                    eng.wait_ge(S("bank_full"), t + base - 4)
                    fn(t, t % TB).then_inc(S("bank_free"), 1)
            eng.wait_ge(S("bank_free"), base + n)

        def fill(eng, name, fn):
            base, n = BASE[name]
            eng.wait_ge(S("bank_free"), base)
            for t in range(n):
                if t >= TB:
                    eng.wait_ge(S("bank_free"), t + base - 4)
                fn(t, t % TB).then_inc(S("bank_full"), 1)

        @block.sync
        def _(sp):
            def load(dst, src, name):
                sp.dma_start(dst, src).then_inc(S(name), 16)

            load(pkS, A["src"].rearrange("(p c) -> p c", p=125), "ld_edges")
            load(pkD, A["dst"].rearrange("(p c) -> p c", p=125), "ld_edges")
            load(srtT, A["L0_ffn_edge_index"][0].rearrange("(p c) -> p c", p=P), "ld_fedges")
            load(srtV, A["L0_ffn_edge_index"][1].rearrange("(p c) -> p c", p=P), "ld_fedges")
            sp.wait_ge(S("x_cleared"), 1)
            load(X[:, 0:T - 1, :], A["x"][0:(T - 1) * P, :].rearrange("(t p) c -> p t c", p=P), "ld_x")
            load(X[0:TAIL, T - 1, :], A["x"][(T - 1) * P:N, :], "ld_x")
            sp.wait_ge(S("packed"), 1)
            sp.dma_start(pk["m"][0:50000].rearrange("(p c) -> p c", p=125), pkS).then_inc(S("pkm_st"), 16)
            for e in (MAIN, FFN):
                n = e.Q * P + P - e.edges
                w = n // 16
                assert n % 16 == 0 and w <= P or e is FFN
                for o in range(0, w, P):
                    k = min(P, w - o)
                    sp.dma_start(pk[e.name][e.edges + 16 * o:e.edges + 16 * (o + k)].rearrange("(p c) -> p c", c=16),
                                 padT[0:k, 0:16]).then_inc(S("pk_st"), 16)
            for b in range(2):
                sp.wait_ge(S(f"scat{b}"), 8 * SC)
            load(srtV, srt1.rearrange("(p c) w -> p (c w)", p=P), "ld_sort1")

            def load_prep(es, k):
                nb, a, b, _, _ = prepv(es)
                name = "ld_prep"
                for dst, off in ((a, 0), (b, 1)):
                    v = pk[es.name][off:off + es.Q * P].rearrange("(q i) -> q i", i=P)
                    load(dst[:, 0:nb - 1, :].bitcast(I32), v[0:(nb - 1) * P].rearrange("(b p) i -> p b i", p=P), name)
                    load(dst[0:16, nb - 1, :].bitcast(I32), v[(nb - 1) * P:es.Q], name)
                rws = pk[es.name][0:es.Q * P].rearrange("(r x) -> r x", r=16)
                load(pkA[:, 0:es.L].bitcast(I32), rws.unsqueeze(1).to_broadcast((16, H8, es.L)), name)

            for b in range(2):
                sp.wait_ge(S(f"scat{b}"), 16 * SC)
            sp.dma_start(pk["f"][0:FFN.edges].rearrange("(p c) -> p c", p=P),
                         srt2.rearrange("(p c) w -> p (c w)", p=P)).then_inc(S("pk_st"), 16)
            sp.wait_ge(S("pk_st"), 64)
            sp.wait_ge(S("pkm_st"), 16)
            load_prep(MAIN, 0)
            sp.wait_ge(S("prep_done"), 1)
            load_prep(FFN, 1)
            sp.wait_ge(S("prep_done"), 2)
            for i, (w, n) in enumerate((("L0_mix_Wq", 2), ("L0_mix_Wkv", 4), ("L0_mix_Wproj", 2))):
                o = (0, 2, 6)[i]
                load(wraw[:, o:o + n, :], A[w].rearrange("(o p) c -> p o c", p=P), "ld_wraw")

            def row(i, name, sem):
                v = A[name]
                if len(v.shape) == 2:
                    v = v.rearrange("a b -> (a b)")
                if len(v.shape) == 3:
                    v = v.rearrange("a b c -> (a b c)")
                n = v.shape[0]
                load(brow[:, i, 0:n], v.unsqueeze(0).to_broadcast((P, n)), sem)

            wnames = [("L0_gnn_W1", "L0_gnn_att_src1", "L0_gnn_att_dst1"),
                      ("L0_gnn_W2", "L0_gnn_att_src2", "L0_gnn_att_dst2"),
                      ("L0_ffn_W_gat", "L0_ffn_att_src", "L0_ffn_att_dst"),
                      ("L1_gnn_W", "L1_gnn_att_src", "L1_gnn_att_dst")]
            for g, (es, c) in enumerate(GATS):
                if g:
                    sp.wait_ge(S("fin_done"), g)
                if g == 3:
                    row(0, "L1_mix_kln_weight", "ld_mix1")
                    row(1, "L1_mix_kln_bias", "ld_mix1")
                    row(2, "L1_mix_vln_weight", "ld_mix1")
                    row(3, "L1_mix_vln_bias", "ld_mix1")
                load(Wn[:, :, 0:c], A[wnames[g][0]].rearrange("(k p) c -> p k c", p=P), "ld_gw")
                if g == 3:
                    sp.wait_ge(S("mix1_kv"), 1)
                row(0, wnames[g][1], "ld_gw")
                row(1, wnames[g][2], "ld_gw")
                if g == 0:
                    row(2, "L0_gnn_b1", "ld_b")
                    row(3, "L0_mix_bproj", "ld_b")
                if g == 1:
                    row(2, "L0_gnn_b2", "ld_b")
                if g == 2:
                    row(2, "L0_ffn_b_gat", "ld_b")
                    row(3, "L0_ffn_ln_gamma", "ld_b")
                if g == 3:
                    row(2, "L1_gnn_bias", "ld_b")
                sp.wait_ge(S("tab_ready"), g + 1)
                sp.dma_start(tab[g].rearrange("(t p) w -> p t w", p=P), Hv(c)[:, :, 0:c + 8]).then_inc(S("tab_st"), 16)
                sp.dma_start(stab[g].rearrange("(t p) w -> p t w", p=P), Hv(c)[:, :, c:c + 8]).then_inc(S("tab_st"), 16)
                if g == 2:
                    sp.wait_ge(S("att_used"), 3)
                    row(0, "L0_ffn_ln_beta", "ld_b2")
                    sp.wait_ge(S("fin_done"), 3)
                    load(W1e[:, :, :, :].rearrange("p e k f -> p (e k) f"), A["L0_ffn_W1"].rearrange("e (k p) f -> p (e k) f", p=P), "ld_moe")
                    load(W2e[:, :, :, :].rearrange("p e k f -> p (e k) f"), A["L0_ffn_W2"].rearrange("e (k p) f -> p (e k) f", p=P), "ld_moe")
                    load(b1e, A["L0_ffn_b1"].rearrange("e (k p) -> (e k) p", p=P), "ld_moe")
                    load(b2e, A["L0_ffn_b2"].rearrange("e c -> (e c)").unsqueeze(0), "ld_moe")
                    sp.wait_ge(S("moe0_done"), 1)
                if g == 3:
                    sp.wait_ge(S("att_used"), 4)
                    row(0, "L1_gnn_gamma", "ld_b2")
                    row(1, "L1_gnn_beta", "ld_b2")
            sp.wait_ge(S("fin_done"), 4)
            for k in range(2):
                load(W1x[:, k, :].rearrange("p (e f) -> p e f", e=EXP1),
                     A["L1_ffn_W1"][:, k * P:(k + 1) * P, :].rearrange("e p f -> p e f"), "ld_moe1")
            load(W2r, A["L1_ffn_W2"].rearrange("(j e) f c -> (e f) j c", e=2), "ld_moe1")
            load(b1r, A["L1_ffn_b1"].rearrange("(j e) f -> j (e f)", e=2), "ld_moe1")
            load(b2r, A["L1_ffn_b2"], "ld_moe1")
            load(rwr, A["L1_ffn_router_w"], "ld_moe1")
            sp.wait_ge(S("bn_done"), 1)
            row(0, "L1_ffn_router_b", "ld_rb")
            sp.wait_ge(S("moe1_done"), 1)
            sp.dma_start(out[0:(T - 1) * P, :].rearrange("(t p) c -> p t c", p=P), X[:, 0:T - 1, :]).then_inc(S("st_out"), 16)
            sp.dma_start(out[(T - 1) * P:N, :], X[0:TAIL, T - 1, :]).then_inc(S("st_out"), 16)
            sp.wait_ge(S("st_out"), 32)


        @block.gpsimd
        def _(pool):
            L = Chain(pool, "pool_chain")
            L(pool.memset(ident[:, :], 0.0))
            L(pool.affine_select(out=ident[:, :], in_=ident[:, :], compare_op=ALU.not_equal, fill=1.0,
                                 base=0, pattern=[[-1, P]], channel_multiplier=1))
            L(pool.tensor_copy(identB[:, :], ident[:, :]))
            L(pool.memset(ones[:, :], 1.0))
            L(pool.affine_select(out=ltri, in_=ones[:, :], compare_op=ALU.is_gt, fill=0.0,
                                 base=0, pattern=[[1, P]], channel_multiplier=-1))
            L(pool.affine_select(out=offd, in_=ones[:, :], compare_op=ALU.not_equal, fill=0.0,
                                 base=0, pattern=[[-1, P]], channel_multiplier=1))
            L(pool.iota(iota[:, :], [[1, MAIN.Q]], base=0, channel_multiplier=0,
                        allow_small_or_imprecise_dtypes=True))
            L(pool.tensor_copy(iotaB[:, :], iota[:, 0:P]))
            L(pool.iota(chan[:, :], [[0, 1]], base=0, channel_multiplier=1, allow_small_or_imprecise_dtypes=True))
            L(pool.memset(mask[:, :], 1.0))
            for v, pat, neg in ((mask[:, 0:P].rearrange("p (h e) -> p h e", h=4), [[-32, 4], [0, 32]], [[32, 4], [0, 32]]),
                                (mask[:, P:P + 4], [[-32, 4]], [[32, 4]])):
                L(pool.affine_select(out=v, in_=v, compare_op=ALU.is_ge, fill=0.0, base=0,
                                     pattern=pat, channel_multiplier=1))
                L(pool.affine_select(out=v, in_=v, compare_op=ALU.is_gt, fill=0.0, base=32,
                                     pattern=neg, channel_multiplier=-1))
            pool.sem_inc(S("consts"), 1)

            for p in range(2):
                pool.wait_ge(S("rank_ready"), p + 1)
                dst = (srt1, srt2)[p]

                def body(i, p=p, dst=dst):
                    for b in range(2):
                        if not isinstance(i, int) or p:
                            pool.wait_ge(S(f"scat{b}"), i * P + p * 8 * SC)
                        L(pool.tensor_copy(idx_s[:, b, :], srtI[:, at(i * 16 + 8 * b, 8)]))
                        L(pool.tensor_copy(dat_s[:, b, :], srtV[:, at(i * 16 + 8 * b, 8)]))
                        pool.sem_inc(S("pool_turn"), 1)
                        for u in range(G):
                            pool.indirect_dma_start(
                                out=dst, out_offset=bass.IndirectOffsetOnAxis(ap=idx_s[:, b, u:u + 1], axis=0),
                                in_=dat_s[:, b, u:u + 1], in_offset=None).then_inc(S(f"scat{b}"), 16)
                body(0)
                L.loop(SC // 16, 4, body, first=1)

            sgat0 = P
            for g, (es, c) in enumerate(GATS):
                sp_rows = rows(g)
                pool.wait_ge(S("tab_st"), 32 * (g + 1))
                pool.wait_ge(S("prep_done"), 2)
                n0 = sum(e.Q // 16 for e, _ in GATS[:g])

                def body(i, es=es, g=g, n0=n0):
                    for b in range(2):
                        pool.wait_ge(S(f"sg_free{b}"), i + (n0 + 1))
                        L(pool.tensor_copy(idx_s[:, b, :], srcI[es.name][:, bass.ds(i * 16 + 8 * b, 8)]))
                        pool.sem_inc(S("pool_turn"), 1)
                        for u in range(G):
                            pool.indirect_dma_start(
                                out=sg[:, b, u, :], out_offset=None, in_=stab[g],
                                in_offset=bass.IndirectOffsetOnAxis(ap=idx_s[:, b, u:u + 1], axis=0),
                            ).then_inc(S(f"sgat{b}"), 16)
                L.loop(es.Q // 16, 2, body)
                pool.wait_ge(S("rows_free"), g + 1)
                with pool.Fori(0, es.groups // NBUF) as i:
                    for b in range(NBUF):
                        pool.wait_ge(S("staged"), i * NBUF + (b + 1 + groups_before(g)))
                        pool.sem_inc(S("pool_turn"), 1)
                        for u in range(G):
                            pool.indirect_dma_start(
                                out=sp_rows[:, b, u, 0:c + 8], out_offset=None, in_=tab[g],
                                in_offset=bass.IndirectOffsetOnAxis(ap=idx[:, b, u:u + 1], axis=0),
                            ).then_inc(S(f"gat{b}"), 16)
            pool.wait_ge(S("xt_used"), 1)
            L(pool.memset(selE, 0.0))
            L(pool.affine_select(out=selE, in_=selE, compare_op=ALU.not_equal, fill=1.0, base=0,
                                 pattern=[[-1, 32], [0, 64]], channel_multiplier=1))
            pool.sem_inc(S("sel_ready"), 1)

        @block.vector
        def _(v):
            L = Chain(v, "dve_chain")
            tt, ts, stt = v.tensor_tensor, v.tensor_scalar, v.scalar_tensor_tensor

            def tell(name, k=1):
                v.sem_inc(S(name), k)

            def scan(out_, d0, d1, init, o0, o1):
                return v.tensor_tensor_scan(out_, d0, d1, init, o0, o1)

            tell("bank_free", TB)
            tell("step_done", 4)
            tell("group_done", NBUF)
            tell("moe_free", 4)
            tell("pair_done", 2)
            L(v.memset(X[:, T - 1, :], 0.0))
            tell("x_cleared")
            L(v.memset(padT[:, :], PADV))
            L(v.memset(epsc[:, :], 1e-5))
            v.wait_ge(S("ld_edges"), 32)
            L(ts(pkD, pkD, 12, None, ALU.logical_shift_left))
            L(tt(pkS, pkS, pkD, ALU.bitwise_or))
            tell("packed")
            v.wait_ge(S("ld_fedges"), 32)
            L(ts(srtV, srtV, 12, None, ALU.logical_shift_left))
            L(tt(srtV, srtV, srtT, ALU.bitwise_or))

            v.wait_ge(S("consts"), 1)
            v.wait_ge(S("pkm_st"), 16)
            for p, (sh, B) in enumerate(DIGITS):
                if p:
                    v.wait_ge(S("ld_sort1"), 16)
                O = sortO[:, 0:B * SC].rearrange("p (b c) -> p b c", b=B)
                Hc = sortH[:, 0:B * SC].rearrange("p (b c) -> p b c", b=B)
                L(ts(srtT, srtV, sh, B - 1, ALU.logical_shift_right, ALU.bitwise_and))
                L(v.tensor_copy(srtD, srtT))
                L(tt(O, srtD.unsqueeze(1).to_broadcast((P, B, SC)),
                     iota[:, 0:B].unsqueeze(2).to_broadcast((P, B, SC)), ALU.is_equal))
                L(scan(sortH[:, 0:B * SC], sortO[:, 0:B * SC], sortO[:, 0:B * SC], 0.0, ALU.add, ALU.max))
                L(v.tensor_copy(sGl[:, 0:B], Hc[:, :, SC - 1]))
                L(v.memset(sGex[:, 0:1], 0.0))
                L(v.tensor_copy(sGex[:, 1:B], sGl[:, 0:B - 1]))
                L(tt(sCnt[:, 0:B], sGl[:, 0:B], sGex[:, 0:B], ALU.subtract))
                tell("counts_ready")
                v.wait_ge(S("offsets"), p + 1)
                L(ts(sXo[:, 0:B], bank(7)[:, 0:B], -1.0, None, ALU.add))
                L(tt(Hc, Hc, sXo[:, 0:B].unsqueeze(2).to_broadcast((P, B, SC)), ALU.add))
                L(tt(Hc, Hc, O, ALU.mult))
                L(v.tensor_reduce(srtP, Hc.rearrange("p b c -> p c b"), AX, ALU.add))
                L(v.tensor_copy(srtI, srtP))
                tell("rank_ready")

            def consts_of(es, k):
                nb, a, b, c, d = prepv(es)
                nm = es.name
                v.wait_ge(S("ld_prep"), 80 * (k + 1))
                last = [(slice(0, P), slice(0, nb - 1)), (slice(0, 16), slice(nb - 1, nb))]
                for ps_, bs in last:
                    A_, B_, C_, D_ = (q[ps_, bs, :] for q in (a, b, c, d))
                    Ai, Bi = A_.bitcast(I32), B_.bitcast(I32)
                    L(ts(D_.bitcast(I32), Ai, IDX - 1, None, ALU.bitwise_and))
                    L(v.tensor_copy(C_, D_.bitcast(I32)))
                    L(ts(Ai, Ai, 12, None, ALU.logical_shift_right))
                    L(ts(Bi, Bi, 12, None, ALU.logical_shift_right))
                    L(v.tensor_copy(D_, Ai))
                    L(v.tensor_copy(A_, Bi))
                    L(tt(B_, A_, D_, ALU.not_equal))
                    L(v.tensor_copy(A_, D_))
                tell("prep_rows")
                Ll = es.L
                L(ts(fA[:, 0:Ll].bitcast(I32), pkA[:, 0:Ll].bitcast(I32), 12, None, ALU.logical_shift_right))
                L(v.tensor_copy(dA[:, 0:Ll], fA[:, 0:Ll].bitcast(I32)))
                L(tt(fA[:, 1:Ll], dA[:, 1:Ll], dA[:, 0:Ll - 1], ALU.not_equal))
                L(ts(flagA[nm][:, 1:Ll], fA[:, 1:Ll], NEG, None, ALU.mult))
                L(v.memset(flagA[nm][:, 0:1], 0.0))
                L(v.memset(flagA[nm][:, Ll:Ll + 1], 0.0))
                tell("prep_scan")
                consume(v, "prep_" + nm, lambda t, kk: v.tensor_copy(
                    dsb[nm][:, t // nb, (t % nb) * P:min((t % nb + 1) * P, es.Q)],
                    bank(kk)[:, 0:min(P, es.Q - (t % nb) * P)]))
                L(v.tensor_copy(srcI[nm][:, :].rearrange("p (j r) -> p r j", r=16),
                                dsb[nm][:, 1, :].rearrange("p (r j) -> p r j", r=16)))
                v.wait_ge(S("ends_ps"), k + 1)
                L(v.tensor_copy(rowc[0:1, 0:2, :, :], bank(7)[0:1, 0:256].rearrange("p (k r h) -> p k h r", k=2, h=H8)))
                f_, l_ = rowc[0:1, 0, :, :], rowc[0:1, 1, :, :]
                sm = seam[nm]
                L(v.memset(sm[:, :, :, :], 1.0))
                L(tt(sm[:, 0, :, 1:16], f_[:, :, 1:16], f_[:, :, 0:15], ALU.not_equal))
                L(tt(sm[:, 1, :, 1:16], f_[:, :, 1:16], l_[:, :, 0:15], ALU.not_equal))
                L(tt(sm[:, 2, :, 0:15], l_[:, :, 1:16], l_[:, :, 0:15], ALU.not_equal))
                L(tt(sm[:, 3, :, 0:15], f_[:, :, 1:16], l_[:, :, 0:15], ALU.not_equal))
                L(ts(sm[:, :, :, :], sm[:, :, :, :], NEG, None, ALU.mult))
                n = es.tiles - 1
                L(v.memset(sel0, 0.0))
                L(v.memset(sel0[0:1, :], 1.0))
                tell("sel0_ready")
                v.wait_ge(S("firsts_ps"), k + 1)
                thr, cnt = small[:, 0:1], small[:, 1:2]
                L(ts(thr, chan[:, :], 128.0, 128.0, ALU.mult, ALU.add))
                L(ts(cmpT[0:n, 0:es.Q // 2], bank(6)[0:n, 0:es.Q:2], thr[0:n, :], None, ALU.is_lt))
                L(v.tensor_reduce(cnt[0:n, :], cmpT[0:n, 0:es.Q // 2], AX, ALU.add))
                L(stt(out=cnt[0:n, :], in0=cnt[0:n, :], scalar=1.0, in1=chan[0:n, :], op0=ALU.max, op1=ALU.add))
                L(ts(cmpT[0:n, 0:es.steps], iota[0:n, 0:es.steps], cnt[0:n, :], None, ALU.is_ge))
                tell("leave_ready")
                v.wait_ge(S("tiles_ps"), k + 1)
                L(v.tensor_copy(tS[:, 0:es.steps], bank(5)[:, 0:es.steps]))
                L(ts(t128[nm][:, :], tS[:, 0:es.steps], 128.0, None, ALU.mult))
                for tb, w, q in ((tI, es.W, 0), (tP, 3 * H8, 32)):
                    L(ts(tS[:, MAIN.steps:MAIN.steps + es.steps], tS[:, 0:es.steps], float(w), None, ALU.mult))
                    L(v.tensor_copy(tb[nm], tS[q:q + 1, MAIN.steps:MAIN.steps + es.steps]))
                L(tt(cmpT[:, 0:es.steps], iota[:, 0:es.steps], tS[:, 0:es.steps], ALU.subtract))
                L(ts(cmpT[:, 0:es.steps], cmpT[:, 0:es.steps], float(es.Q // 2 - 1), 2.0 * EW, ALU.min, ALU.mult))
                L(v.tensor_copy(cI[nm], cmpT[64:65, 0:es.steps]))
                tell("prep_done")

            consts_of(MAIN, 0)
            consts_of(FFN, 1)

            def norm(k, dst):
                for t in range(T):
                    L(v.bn_stats(st6[:, t % TB, :], X[:, t, :]))
                    L(v.bn_aggr(mv[:, t, :], st6[:, t % TB, :]))
                tell("var_ready")
                v.wait_ge(S("std_ready"), k + 1)
                L(v.reciprocal(rstd[:, :], rstd[:, :]))
                L(tt(dst, X[:, :, :], mv[:, :, 0:1].to_broadcast((P, T, C)), ALU.subtract))
                L(tt(dst, dst, rstd[:, :].unsqueeze(2).to_broadcast((P, T, C)), ALU.mult))
                tell("xn_ready")

            def elu1(region, name):
                for q in range(4):
                    L(ts(eluT[:, 0:1600], region[:, q * 1600:(q + 1) * 1600], 0.0, None, ALU.min))
                    tell("elu_min")
                    v.wait_ge(S("elu_exp"), 4 * (name == "k") + q + 1)
                    L(stt(out=region[:, q * 1600:(q + 1) * 1600], in0=region[:, q * 1600:(q + 1) * 1600], scalar=0.0,
                          in1=eluT[:, 0:1600], op0=ALU.max, op1=ALU.add))

            def lrelu(x):
                L(stt(out=x, in0=x, scalar=SLOPE, in1=x, op0=ALU.mult, op1=ALU.max))

            def attention_scores(g, es, c):
                H = Hv(c)
                heads = (8, 1, 4, 8)[g]
                rep = 8 // heads
                tmp = R1[:, 0:T * c].rearrange("p (t c) -> p t c", t=T)
                v.wait_ge(S("ld_gw"), 16 * 3 * (g + 1))
                for q in range(2):
                    L(tt(tmp, H[:, :, 0:c], brow[:, q, 0:c].unsqueeze(1).to_broadcast((P, T, c)), ALU.mult))
                    sc = rowsum[:, 0:T * heads]
                    L(v.tensor_reduce(sc, tmp.rearrange("p t (h e) -> p (t h) e", h=heads), AX, ALU.add))
                    sc = sc.rearrange("p (t h) -> p t h", t=T)
                    for r in range(rep):
                        col = H[:, :, c + 8 * q:c + 8 * q + 8].rearrange("p t (h r) -> p t h r", r=rep)[:, :, :, r]
                        L(v.tensor_copy(col, sc))
                tell("tab_ready")
                tell("att_used")
                rest = small3[:, 0, :, :]
                L(v.tensor_copy(rest, H[:, :, c + 8:c + 16]))
                for q in range(3):
                    L(v.tensor_copy(dS[:, :, q, :], rest))
                    if q < 2:
                        L(tt(rest, rest, dS[:, :, q, :], ALU.subtract))

            def scan_max(g, es):
                SA, MA = scan_bufs(g)
                fl = flagA[es.name]
                sm = seam[es.name]
                v.wait_ge(S("s_ready"), g + 1)
                L(v.tensor_copy(EV(es).rearrange("p (r j) w -> p j r w", j=es.J)[:, :, :, 0:8],
                                s_cols(g).rearrange("p (j r h) -> p j r h", r=16, h=H8)))
                v.wait_ge(S("bank_free"), BASE[f"sA{g}"][0] + BASE[f"sA{g}"][1])
                Ll = es.L

                def seams(n, resets, seam_, end, shift, rev):
                    tell("end_ready")
                    v.wait_ge(S("end_row"), 2 * g + n + 1)
                    T_ = bank(7)[0:1, 0:P].rearrange("p (r h) -> p h r", h=H8)
                    e_, i_ = rowc[0:1, 0, :, :], rowc[0:1, 1, :, :]
                    L(v.memset(e_, NEG))
                    if rev:
                        L(tt(e_[:, :, 0:15], T_[:, :, 1:16], seam_[:, :, 0:15], ALU.add))
                    else:
                        L(tt(e_[:, :, 1:16], T_[:, :, 0:15], seam_[:, :, 1:16], ALU.add))
                    a_, b_, o_ = (q.rearrange("p h r -> p (h r)") for q in (resets, e_, i_))
                    if rev:
                        a_, b_, o_ = a_[:, ::-1], b_[:, ::-1], o_[:, ::-1]
                    L(scan(o_, a_, b_, NEG, ALU.add, ALU.max))
                    L(v.tensor_copy(rowc[0:1, 2, :, :].rearrange("p h r -> p (h r)").rearrange("p (r h) -> p h r", h=H8), i_))
                    tell("carry_row")
                    v.wait_ge(S("carry_ps"), 2 * g + n + 1)
                    L(v.tensor_copy(carry[:, :], bank(7)[:, 256:257]))

                L(scan(MA, fl[:, 0:Ll], SA, NEG, ALU.add, ALU.max))
                L(v.tensor_copy(dcol[:, 0:1], MA[:, Ll - 1:Ll]))
                seams(0, sm[:, 0, :, :], sm[:, 1, :, :], None, 1, False)
                L(scan(MA, fl[:, 0:Ll], SA, carry[:, 0:1], ALU.add, ALU.max))
                bk = fl[:, 1:Ll + 1][:, ::-1]
                L(scan(SA[:, ::-1], bk, MA[:, ::-1], NEG, ALU.add, ALU.max))
                L(v.tensor_copy(dcol[:, 0:1], SA[:, 0:1]))
                seams(1, sm[:, 2, :, :], sm[:, 3, :, :], None, -1, True)
                L(scan(SA[:, ::-1], bk, MA[:, ::-1], carry[:, 0:1], ALU.add, ALU.max))
                tell("max_ready")

            def edges(g, es, c):
                nm = es.name
                R, A_ = rows(g), Av(c)
                gb = groups_before(g)
                sb_ = gb * S2
                fills = sum(e.groups // NBUF for e, _ in GATS[:g])
                base, k = BASE[f"sB{g}"]
                v.wait_ge(S("bank_free"), base + k)
                L(v.memset(R1[:, 0:T * (c + 16)], 0.0))
                tell("rows_free")


                def onehots(n, b):
                    v.wait_ge(S("staged"), n + (gb + 1))
                    tt(drel[:, b % 2, :].rearrange("p (k a) -> p k a", a=2),
                       stage[:, b, :, 16].rearrange("p (k a) -> p k a", a=2),
                       t128[nm][:, at(n * S2, S2)].unsqueeze(2).to_broadcast((P, S2, 2)),
                       ALU.subtract).then_inc(S("rel_done"), 1)
                    v.wait_ge(S("rel_done"), n + (gb + 1))
                    for u in range(G):
                        ins = ts(onehB[:, b % 2, u, :], iotaB[:, :], drel[:, b % 2, u:u + 1], None, ALU.is_equal)
                    ins.then_inc(S("oneh_ready"), 1)

                def group(n, b, more):
                    if more:
                        onehots(n + 1, (b + 1) % NBUF)
                    v.wait_ge(S("d_ready"), n + (gb + 1))
                    v.tensor_reduce(zd[:, :, :], bank(6)[:, 0:3 * G * H8].rearrange("p (u k h) -> p u h k", u=G, k=3),
                                    AX, ALU.add).then_inc(S("z_done"), 1)
                    v.wait_ge(S("z_done"), n * 4 + (4 * gb + 1))
                    tt(zz[:, :, :, :], stage[:, b, :, 0:16].rearrange("p u (k h) -> p u k h", k=2),
                       zd[:, :, :].unsqueeze(2).to_broadcast((P, G, 2, H8)), ALU.add).then_inc(S("z_done"), 1)
                    v.wait_ge(S("z_done"), n * 4 + (4 * gb + 2))
                    stt(out=zz[:, :, :, :], in0=zz[:, :, :, :], scalar=SLOPE, in1=zz[:, :, :, :], op0=ALU.mult,
                        op1=ALU.max).then_inc(S("z_done"), 1)
                    v.wait_ge(S("z_done"), n * 4 + (4 * gb + 3))
                    tt(zd[:, :, :], zz[:, :, 0, :], zz[:, :, 1, :], ALU.subtract).then_inc(S("z_done"), 1)
                    v.wait_ge(S("z_done"), n * 4 + (4 * gb + 4))
                    ts(zd[:, :, :], zd[:, :, :], 0.0, None, ALU.min).then_inc(S("z_ready"), 1)
                    tt(R[:, b, :, c + 8:c + 16], stage[:, b, :, 8:16],
                       stage[:, b, :, 18:19].to_broadcast((P, G, H8)), ALU.mult)
                    if not isinstance(n, int) or n:
                        add_up(n - 1)
                    v.wait_ge(S("w_ready"), n + (gb + 1))
                    for u in range(0, G, 2):
                        r = R[:, b, u:u + 2, 0:c].rearrange("p u (h e) -> p u h e", h=H8)
                        tt(r, r, R[:, b, u:u + 2, c:c + 8].unsqueeze(3).to_broadcast((P, 2, H8, c // 8)),
                           ALU.mult).then_inc(S("scaled"), 1)

                def add_up(n):
                    offs = offsets(mybir.EngineType.DVE, tI[nm], n * S2, S2, (es.tiles - 1) * es.W)
                    for k in range(S2):
                        v.wait_ge(S("summed"), n * S2 + (sb_ + k + 1))
                        v.wait_ge(S("step_done"), n * S2 + (sb_ + k + 4))
                        a = R1[:, bass.ds(offs[k], c + 16)]
                        tt(a, a, bank(k)[:, 0:c + 16], ALU.add).then_inc(S("step_done"), 1)
                    v.wait_ge(S("step_done"), n * S2 + (sb_ + S2 + 4))
                    v.sem_inc(S("group_done"), 1)

                onehots(0, 0)
                group(0, 0, True)
                rounds = (es.groups - 1) // NBUF
                with v.Fori(0, rounds) as i:
                    for j in range(NBUF):
                        group(i * NBUF + (j + 1), (j + 1) % NBUF, True)
                for n in range(1 + rounds * NBUF, es.groups):
                    group(n, n % NBUF, n < es.groups - 1)
                add_up(es.groups - 1)

            def finish(g, es, c):
                H, A_ = Hv(c), Av(c)
                s_, d_ = H[:, :, c:c + 8], H[:, :, c + 8:c + 16]
                den, mx = A_[:, :, c:c + 8], A_[:, :, c + 8:c + 16]
                n3 = [small3[:, q, :, :] for q in range(4)]
                L(ts(n3[0], den, 0.5, NEG, ALU.is_lt, ALU.mult))
                L(tt(mx, mx, n3[0], ALU.add))
                L(tt(mx, mx, d_, ALU.add))
                L(tt(s_, s_, d_, ALU.add))
                lrelu(mx)
                lrelu(s_)
                L(tt(n3[0], mx, s_, ALU.max))
                L(tt(n3[1], mx, n3[0], ALU.subtract))
                L(tt(n3[2], s_, n3[0], ALU.subtract))
                tell("fin_z")
                v.wait_ge(S("fin_e"), g + 1)
                L(tt(den, den, n3[1], ALU.mult))
                L(tt(den, den, n3[2], ALU.add))
                if g != 3:
                    L(ts(den, den, 1e-16, None, ALU.add))
                L(v.reciprocal(n3[0], den))
                L(tt(n3[1], n3[1], n3[0], ALU.mult))
                L(tt(n3[2], n3[2], n3[0], ALU.mult))
                a_ = A_[:, :, 0:c].rearrange("p t (h e) -> p t h e", h=H8)
                h_ = H[:, :, 0:c].rearrange("p t (h e) -> p t h e", h=H8)
                L(tt(a_, a_, n3[1].unsqueeze(3).to_broadcast((P, T, H8, c // 8)), ALU.mult))
                L(tt(h_, h_, n3[2].unsqueeze(3).to_broadcast((P, T, H8, c // 8)), ALU.mult))
                L(tt(A_[:, :, 0:c], A_[:, :, 0:c], H[:, :, 0:c], ALU.add))
                v.wait_ge(S("ld_b"), (32, 48, 80, 96)[g])
                L(tt(A_[:, :, 0:c], A_[:, :, 0:c], brow[:, 2, 0:c].unsqueeze(1).to_broadcast((P, T, c)), ALU.add))

            def fill_records(es):
                L(v.tensor_copy(EV(es)[:, :, 16:19], dsb[es.name][:, :, :].rearrange("p k q -> p q k")))
                tell("records")

            v.wait_ge(S("ld_x"), 32)
            norm(0, nodes(R2))
            v.wait_ge(S("q_copied"), 1)
            elu1(R4[:, 0:2 * T * P], "q")
            tell("q_ready")
            v.wait_ge(S("kv_copied"), 1)
            elu1(R1[:, 0:T * C], "k")
            L(v.memset(V0[:, :, :, 128:129], 1.0))
            tell("k_ready")
            v.wait_ge(S("ctx_ps"), 1)
            for a in range(2):
                L(v.tensor_copy(dcol[:, a:a + 1], bank(6 + a)[:, 128:129]))
                L(tt(BD[:, a, 0:P], bank(6 + a)[:, 0:P], mask[:, 0:P], ALU.mult))
                L(ts(BD[:, a, P:P + 4], mask[:, P:P + 4], dcol[:, a:a + 1], None, ALU.mult))
            tell("ctx_ready")
            v.wait_ge(S("h_copied"), 1)
            attention_scores(0, *GATS[0])

            base, _ = BASE["mixo"]

            def mixo(i):
                for k in range(TB):
                    v.wait_ge(S("bank_full"), i * TB + (k + base - 4))
                    pv = bank(k)[:, 0:264].rearrange("p (a w) -> p a w", a=2)
                    dn = dcol[:, 0:8].rearrange("p (a w) -> p a w", a=2)
                    L(ts(dn, pv[:, :, P:P + 4], 1e-6, None, ALU.max))
                    L(v.reciprocal(dn, dn))
                    L(tt(AO[:, bass.ds(i * TB + k, 1), :].rearrange("p o (a h e) -> p (o a) h e", a=2, h=4),
                         pv[:, :, 0:P].rearrange("p a (h e) -> p a h e", h=4),
                         dn.unsqueeze(3).to_broadcast((P, 2, 4, 32)), ALU.mult))
                    v.sem_inc(S("bank_free"), 1)
            L.loop(T // TB, 3 * TB, mixo)
            v.wait_ge(S("bank_free"), base + T)
            tell("ao_ready")
            consume(v, "proj", lambda t, k: tt(X[:, bass.ds(t, 1), :].rearrange("p a c -> p (a c)"),
                                               X[:, bass.ds(t, 1), :].rearrange("p a c -> p (a c)"),
                                               bank(k)[:, 0:C], ALU.add))
            v.wait_ge(S("ld_b"), 32)
            L(tt(X[:, :, :], X[:, :, :], brow[:, 3, :].unsqueeze(1).to_broadcast((P, T, C)), ALU.add))
            fill_records(MAIN)
            scan_max(0, MAIN)
            edges(0, *GATS[0])
            finish(0, *GATS[0])
            L(ts(Av(C)[:, :, 0:C], Av(C)[:, :, 0:C], 0.0, None, ALU.max))
            tell("fin_done")
            tell("xn_ready")
            v.wait_ge(S("h_copied"), 2)
            attention_scores(1, *GATS[1])
            fill_records(MAIN)
            scan_max(1, MAIN)
            edges(1, *GATS[1])
            finish(1, *GATS[1])
            L(tt(X[:, :, :], X[:, :, :], Av(C)[:, :, 0:C], ALU.add))
            tell("fin_done")

            norm(1, nodes(R2))
            v.wait_ge(S("h_copied"), 3)
            attention_scores(2, *GATS[2])
            fill_records(FFN)
            scan_max(2, FFN)
            edges(2, *GATS[2])
            finish(2, *GATS[2])
            O16 = Av(16)[:, :, 0:16]
            m1, m2 = rowsum[:, 0:T], rowsum[:, T:2 * T]
            L(v.tensor_reduce(m1, O16, AX, ALU.add))
            L(ts(m1, m1, 1.0 / 16, None, ALU.mult))
            L(tt(O16, O16, m1.unsqueeze(2).to_broadcast((P, T, 16)), ALU.subtract))
            sq = small4[:, 0:T * 16].rearrange("p (t c) -> p t c", t=T)
            L(tt(sq, O16, O16, ALU.mult))
            L(v.tensor_reduce(m2, sq, AX, ALU.add))
            L(ts(rstd[:, :], m2, 1.0 / 16, None, ALU.mult))
            tell("rvar_ready")
            v.wait_ge(S("rstd_ready"), 1)
            L(v.reciprocal(rstd[:, :], rstd[:, :]))
            L(tt(O16, O16, rstd[:, :].unsqueeze(2).to_broadcast((P, T, 16)), ALU.mult))
            v.wait_ge(S("ld_b2"), 16)
            L(tt(O16, O16, brow[:, 3, 0:16].unsqueeze(1).to_broadcast((P, T, 16)), ALU.mult))
            L(tt(O16, O16, brow[:, 0, 0:16].unsqueeze(1).to_broadcast((P, T, 16)), ALU.add))
            sc = small4[:, 400:400 + 4 * T].rearrange("p (t e) -> p t e", t=T)
            L(v.tensor_reduce(sc, O16.rearrange("p t (h e) -> p t e h", h=4), AX, ALU.add))
            L(ts(sc, sc, 0.25, None, ALU.mult))
            cmp4 = small4[:, 0:T * 4].rearrange("p (t e) -> p t e", t=T)
            rk = small4[:, 100:100 + T * 4].rearrange("p (t e) -> p t e", t=T)
            L(v.memset(rk, 0.0))
            for j in range(EXP0):
                sj = sc[:, :, j:j + 1].to_broadcast((P, T, EXP0))
                L(tt(cmp4, sj, sc, ALU.is_gt))
                L(tt(rk, rk, cmp4, ALU.add))
                if j < EXP0 - 1:
                    w = EXP0 - 1 - j
                    L(tt(cmp4[:, :, 0:w], sc[:, :, j:j + 1].to_broadcast((P, T, w)), sc[:, :, j + 1:EXP0], ALU.is_equal))
                    L(tt(rk[:, :, j + 1:EXP0], rk[:, :, j + 1:EXP0], cmp4[:, :, 0:w], ALU.add))
            L(v.tensor_reduce(m1, sc, AX, ALU.max))
            L(tt(gates[:, :, :], sc, m1.unsqueeze(2).to_broadcast((P, T, EXP0)), ALU.subtract))
            tell("gate_z")
            v.wait_ge(S("gate_e"), 1)
            L(stt(out=gates[:, :, :], in0=rk, scalar=1.5, in1=gates[:, :, :], op0=ALU.is_lt, op1=ALU.mult))
            L(v.tensor_reduce(m1, gates[:, :, :], AX, ALU.add))
            L(v.reciprocal(m1, m1))
            L(tt(gates[:, :, :], gates[:, :, :], m1.unsqueeze(2).to_broadcast((P, T, EXP0)), ALU.mult))
            tell("fin_done")
            nE = EXP0 * TB
            with v.Fori(0, T // TB) as i:
                for e in range(EXP0):
                    for k in range(TB):
                        o = e * TB + k
                        v.wait_ge(S("moe_full"), i * nE + (o + 1 + 2 * TB))
                        if e:
                            v.wait_ge(S("moe_free"), i * nE + (o - TB + 1 + 4))
                        x = X[:, bass.ds(i * TB + k, 1), :].rearrange("p a c -> p (a c)")
                        stt(out=x, in0=bank(o % 4)[:, 0:C],
                            scalar=gates[:, bass.ds(i * TB + k, 1), e:e + 1].rearrange("p a c -> p (a c)"),
                            in1=x, op0=ALU.mult, op1=ALU.add).then_inc(S("moe_free"), 1)
            v.wait_ge(S("moe_free"), 4 + nE * (T // TB))
            tell("moe0_done")

            XN = nodes(R2)
            norm(2, XN)
            L(stt(out=X[:, :, :], in0=XN, scalar=2.0, in1=X[:, :, :], op0=ALU.mult, op1=ALU.add))
            g3 = lambda r: r[:, 0:T * C].rearrange("p (q e) -> p q e", e=32)
            mean, std = rowsum[:, 0:200], small4[:, 0:200]
            L(v.tensor_reduce(mean, g3(R2), AX, ALU.add))
            L(ts(mean, mean, 1.0 / 32, None, ALU.mult))
            L(tt(g3(R1), g3(R2), mean.unsqueeze(2).to_broadcast((P, 200, 32)), ALU.subtract))
            L(tt(g3(R4), g3(R1), g3(R1), ALU.mult))
            L(v.tensor_reduce(std, g3(R4), AX, ALU.add))
            tell("hvar_ready")
            v.wait_ge(S("hstd_ready"), 1)
            L(ts(std, std, 1e-5, None, ALU.add))
            L(v.reciprocal(std, std))
            L(tt(g3(R1), g3(R1), std.unsqueeze(2).to_broadcast((P, 200, 32)), ALU.mult))
            v.wait_ge(S("ld_mix1"), 64)
            bc = lambda q: brow[:, q, :].unsqueeze(1).to_broadcast((P, T, C))
            L(tt(V1, K1, bc(2), ALU.mult))
            L(tt(V1, V1, bc(3), ALU.add))
            L(tt(K1, K1, bc(0), ALU.mult))
            L(tt(K1, K1, bc(1), ALU.add))
            tell("mix1_kv")
            v.wait_ge(S("ctx_ps"), 2)
            for a in range(2):
                L(stt(out=BD[:, a, 0:P], in0=bank(6 + a)[:, 0:P], scalar=1.0 / N, in1=mask[:, 0:P], op0=ALU.mult,
                      op1=ALU.mult))
            tell("ctx_ready")
            consume(v, "mix1o", lambda t, k: tt(X[:, bass.ds(t, 1), :].rearrange("p a c -> p (a c)"),
                                                X[:, bass.ds(t, 1), :].rearrange("p a c -> p (a c)"),
                                                bank(k)[:, 0:C], ALU.add))
            v.wait_ge(S("h_copied"), 4)
            attention_scores(3, *GATS[3])
            fill_records(MAIN)
            scan_max(3, MAIN)
            edges(3, *GATS[3])
            finish(3, *GATS[3])
            out3 = Av(C)[:, :, 0:C]
            meanS, varS = R2[:, 0:C], R2[:, C:2 * C]
            tell("bn_in")
            base, _ = BASE["bnm"]
            v.wait_ge(S("bank_full"), base - 4)
            ts(meanS, bank(0)[:, 0:C], 1.0 / N, None, ALU.mult).then_inc(S("bank_free"), 1)
            v.wait_ge(S("bank_free"), base + 1)
            L(tt(out3, out3, meanS.unsqueeze(1).to_broadcast((P, T, C)), ALU.subtract))
            L(tt(nodes(R4), out3, out3, ALU.mult))
            tell("bn_in")
            v.wait_ge(S("bank_full"), base - 3)
            ts(varS, bank(0)[:, 0:C], 1.0 / N, None, ALU.mult).then_inc(S("bank_free"), 1)
            v.wait_ge(S("bank_free"), base + 2)
            tell("bn_var")
            v.wait_ge(S("bn_std"), 1)
            L(v.reciprocal(varS, varS))
            v.wait_ge(S("ld_b2"), 48)
            L(tt(varS, varS, brow[:, 0, :], ALU.mult))
            L(tt(out3, out3, varS.unsqueeze(1).to_broadcast((P, T, C)), ALU.mult))
            L(tt(out3, out3, bc(1), ALU.add))
            L(tt(X[:, :, :], X[:, :, :], out3, ALU.add))
            tell("fin_done")
            tell("bn_done")

            norm(3, nodes(R1))
            v.wait_ge(S("ld_rb"), 16)
            base, _ = BASE["rt"]
            lg = R1[:, 0:T * 32].rearrange("p (t e) -> p t e", t=T)
            eq = R1[:, 1000:1000 + T * 32].rearrange("p (t e) -> p t e", t=T)
            v.wait_ge(S("xt_used"), 1)
            consume(v, "rt", lambda t, k: tt(lg[:, bass.ds(t, 1), :].rearrange("p a e -> p (a e)"), bank(k)[:, 0:32],
                                             brow[:, 0, 0:32], ALU.add))
            mx = rowsum[:, 0:T]
            L(v.tensor_reduce(mx, lg, AX, ALU.max))
            L(tt(eq, lg, mx.unsqueeze(2).to_broadcast((P, T, 32)), ALU.is_equal))
            rev = small4[:, 0:32]
            L(ts(rev, iota[:, 0:32], -1.0, 32.0, ALU.mult, ALU.add))
            L(tt(eq, eq, rev.unsqueeze(1).to_broadcast((P, T, 32)), ALU.mult))
            L(v.tensor_reduce(mx, eq, AX, ALU.max))
            L(tt(lg, eq, mx.unsqueeze(2).to_broadcast((P, T, 32)), ALU.is_equal))
            L(v.memset(zrow, 0.0))
            tell("choice")
            consume(v, "ohT", lambda t, k: v.tensor_copy(ohE[:, bass.ds(t * P, P)], bank(k)[0:32, 0:P]))
            tell("ohT_ready")
            def out_block(i):
                L(v.tensor_copy(ohS, ohE[:, bass.ds(i * TOK, TOK)]))
                v.sem_inc(S("block_choice"), 1)
                for j in range(16):
                    for hf in range(2):
                        n = 2 * j + hf
                        v.wait_ge(S("relu_done"), i * 32 + (n + 1))
                        if hf == 0:
                            v.wait_ge(S("w2_done"), i * 16 + (j + 1))
                        tt(hm[:, j % 2, hf * 320:(hf + 1) * 320], ha[:, hf, :], bank(5 + hf)[:, 0:320],
                           ALU.mult).then_inc(S("pair_done"), 1)
                v.wait_ge(S("out_full"), i + 1)
                for b in range(3):
                    w = 2 if b < 2 else 1
                    x = X[:, bass.ds(i * TB + 2 * b, w), :].rearrange("p a c -> p (a c)")
                    L(stt(out=x, in0=bank(b)[:, 0:w * C], scalar=0.0, in1=x, op0=ALU.max, op1=ALU.add))
                v.sem_inc(S("out_free"), 1)
            L.loop(T // TB, 4, out_block)
            tell("moe1_done")

        @block.scalar
        def _(s):
            L = Chain(s, "act_chain")
            act = s.activation

            def copy(out_, in_):
                return act(out_, in_, ACT.Copy)

            def tell(name, k=1):
                s.sem_inc(S(name), k)

            def to_xt(g):
                consume(s, f"xT{g}", lambda t, k: copy(XT[:, :, bass.ds(t * P, P)],
                                                       bank(k)[:, 0:2 * P].rearrange("p (a n) -> p a n", a=2)))
                tell("xt_ready")

            def std(src, dst, bias):
                L(act(dst, src, ACT.Sqrt, bias=bias))

            for b in range(2):
                tell(f"sg_free{b}")

            def gat(g, es, c):
                E = EV(es)
                nm = es.name
                n0 = sum(e.Q // 16 for e, _ in GATS[:g])
                s.wait_ge(S("records"), g + 1)

                with s.Fori(0, es.Q // 16) as i:
                    for b in range(2):
                        s.wait_ge(S(f"sgat{b}"), i * P + (P * n0 + P))
                        copy(s_cols(g)[:, bass.ds(i * P + 64 * b, 64)],
                             sg[:, b, :, :].rearrange("p u h -> p (u h)")).then_inc(S(f"sg_free{b}"), 1)
                for b in range(2):
                    s.wait_ge(S(f"sg_free{b}"), n0 + es.Q // 16 + 1)
                tell("s_ready")
                SA, _ = scan_bufs(g)

                def down(t, k):
                    w = min(4, es.J - 4 * t) * P
                    return copy(SA[:, 4 * t * P:4 * t * P + w], bank(k)[:, 0:w])
                consume(s, f"sA{g}", down)
                Er = E.rearrange("p (r j) w -> p j r w", j=es.J)

                def up(t, k):
                    w = min(4, es.J - 4 * t)
                    for q in range(w):
                        ins = copy(Er[:, 4 * t + q, :, 8:16], bank(k)[:, q * P:(q + 1) * P].rearrange("p (r h) -> p r h", h=H8))
                    return ins
                consume(s, f"sB{g}", up)

                gb = groups_before(g)
                R = rows(g)

                def stage_in(n, b):
                    s.wait_ge(S("group_done"), n + (gb + 1))
                    offs = offsets(mybir.EngineType.Activation, cI[nm], n * S2, S2, (es.Q - 2) * EW)
                    for k in range(S2):
                        ins = copy(stage[:, b, 2 * k:2 * k + 2, :].rearrange("p u w -> p (u w)"),
                                   R4[:, bass.ds(offs[k], 2 * EW)])
                    ins.then_inc(S("rec_done"), 1)
                    s.wait_ge(S("rec_done"), n + (gb + 1))
                    copy(idx[:, b, :], stage[:, b, :, 17]).then_inc(S("staged"), 1)

                def turned(n, b):
                    s.wait_ge(S("turned_ps"), n + (gb + 1))
                    copy(onehT[:, :, :], bank(4).bitcast(BF16).rearrange("p (u e) -> p u e", u=G)).then_inc(S("turned"), 1)
                    if gb or not isinstance(n, int) or n > 1:
                        s.wait_ge(S("group_done"), n + (gb + NBUF - 1))
                    copy(oneh[:, b % 2, :, :], onehB[:, b % 2, :, :]).then_inc(S("oneh_copied"), 1)

                def group(n, b, more, more3):
                    s.wait_ge(S("z_ready"), n + (gb + 1))
                    k = n // NBUF if isinstance(n, int) else None
                    gathered(n, b, k)
                    act(R[:, b, :, c:c + 8], zd[:, :, :], ACT.Exp).then_inc(S("w_ready"), 1)
                    if more:
                        turned(n + 1, b + 1)
                    if more3:
                        stage_in(n + AHEAD, (b + AHEAD) % NBUF)

                fills = sum(e.groups // NBUF for e, _ in GATS[:g])

                def gathered(n, b, k):
                    q = k if k is not None else cur[0]
                    s.wait_ge(S(f"gat{b}"), q * P + (P * fills + P))

                cur = [None]
                last = es.groups // NBUF - 1
                for b in range(AHEAD):
                    stage_in(b, b)
                turned(0, 0)
                with s.Fori(0, last) as i:
                    cur[0] = i
                    for b in range(NBUF):
                        group(i * NBUF + b, b, True, True)
                for b in range(NBUF):
                    group(last * NBUF + b, b, b < NBUF - 1, b + AHEAD < NBUF)
                s.wait_ge(S("fin_z"), g + 1)
                L(act(small3[:, 1:3, :, :], small3[:, 1:3, :, :], ACT.Exp))
                tell("fin_e")

            def to_h(g, c):
                consume(s, f"h{g}", lambda t, k: copy(Hv(c)[:, bass.ds(t, 1), 0:c].rearrange("p a c -> p (a c)"),
                                                      bank(k)[:, 0:c]))
                tell("h_copied")

            def node_std(k):
                s.wait_ge(S("var_ready"), k + 1)
                std(mv[:, :, 1], rstd[:, :], epsc[:, 0:1])
                tell("std_ready")

            consume(s, "wT", lambda t, k: copy(wT[:, :, t, :], bank(k)[:, 0:2 * P].rearrange("p (a n) -> p a n", a=2)))
            tell("wT_ready")
            node_std(0)
            to_xt(0)
            consume(s, "q", lambda t, k: copy(qT[:, t // 10, (t % 10) * 320:(t % 10 + 1) * 320], bank(k)[:, 0:320]))
            tell("q_copied")

            def kv(t, k):
                copy(K0[:, bass.ds(t, 1), :].rearrange("p a c -> p (a c)"), bank(k)[:, 0:C])
                return copy(V0[:, bass.ds(t, 1), :, 0:P].rearrange("p o a w -> p (o a) w"),
                            bank(k)[:, C:2 * C].rearrange("p (a w) -> p a w", a=2))
            for q in range(4):
                s.wait_ge(S("elu_min"), q + 1)
                L(act(eluT[:, 0:1600], eluT[:, 0:1600], ACT.Exp))
                tell("elu_exp")
            consume(s, "kv", kv)
            tell("kv_copied")
            for q in range(4, 8):
                s.wait_ge(S("elu_min"), q + 1)
                L(act(eluT[:, 0:1600], eluT[:, 0:1600], ACT.Exp))
                tell("elu_exp")
            to_h(0, C)
            s.wait_ge(S("ao_ready"), 1)
            consume(s, "aT", lambda t, k: copy(XT[:, :, bass.ds(t * P, P)],
                                               bank(k)[:, 0:2 * P].rearrange("p (a n) -> p a n", a=2)))
            tell("aT_ready")
            gat(0, *GATS[0])
            to_xt(1)
            to_h(1, C)
            gat(1, *GATS[1])
            node_std(1)
            to_xt(2)
            to_h(2, 16)
            gat(2, *GATS[2])
            s.wait_ge(S("rvar_ready"), 1)
            std(rstd[:, :], rstd[:, :], epsc[:, 0:1])
            tell("rstd_ready")
            s.wait_ge(S("gate_z"), 1)
            L(act(gates[:, :, :], gates[:, :, :], ACT.Exp))
            tell("gate_e")
            s.wait_ge(S("b1_ps"), 1)
            L(copy(b1T[:, :], bank(7)[:, 0:16]))
            tell("b1_ready")
            with s.Fori(0, T // TB) as i:
                for e in range(EXP0):
                    s.wait_ge(S("moe_full"), i * (EXP0 * TB) + (e + 1) * TB)
                    for f in range(4):
                        for hf in range(2):
                            m = (e * 4 + f) * 2 + hf
                            s.wait_ge(S("hid_full"), i * 32 + (m + 1))
                            col = e * 4 + f
                            act(hh[:, e % 2, f, hf * 320:(hf + 1) * 320], bank(4 + m % 4)[:, 0:320], ACT.Gelu,
                                bias=b1T[:, col:col + 1]).then_inc(S("hid_free"), 1)
            node_std(2)
            s.wait_ge(S("hvar_ready"), 1)
            L(act(small4[:, 0:200], small4[:, 0:200], ACT.Sqrt, scale=1.0 / 31))
            tell("hstd_ready")
            to_xt(3)
            to_h(3, C)
            gat(3, *GATS[3])
            s.wait_ge(S("bn_var"), 1)
            std(R2[:, C:2 * C], R2[:, C:2 * C], epsc[:, 0:1])
            tell("bn_std")
            node_std(3)
            s.wait_ge(S("b1_ps"), 2)
            L(copy(b1T[:, :], bank(7)[:, 0:16]))
            L(copy(rwT[:, :, :], bank(7)[:, 64:128].rearrange("p (k e) -> p k e", k=2)))
            tell("b1_ready")
            to_xt(4)
            tell("xt_used")
            with s.Fori(0, T // TB) as i:
                for j in range(16):
                    for hf in range(2):
                        n = 2 * j + hf
                        s.wait_ge(S("pair_full"), i * 32 + (n + 1))
                        s.wait_ge(S("pair_done"), i * 32 + (n + 1))
                        act(ha[:, hf, :], bank(3 + hf)[:, 0:320], ACT.Relu,
                            bias=b1T[:, j:j + 1]).then_inc(S("relu_done"), 1)

        @block.tensor
        def _(pe):
            mm = pe.matmul

            def turn(out_, in_, k=P):
                return pe.transpose(out_, in_, ident[0:k, 0:k])

            pe.wait_ge(S("consts"), 1)
            for p, (sh, B) in enumerate(DIGITS):
                pe.wait_ge(S("counts_ready"), p + 1)
                mm(bank(7)[:, 0:B], ltri, sCnt[:, 0:B], start=True, stop=False)
                mm(bank(7)[:, 0:B], offd, sGex[:, 0:B], start=False, stop=True).then_inc(S("offsets"), 1)

            def prepare(es, k):
                nb, a, b, c, d = prepv(es)
                pe.wait_ge(S("prep_rows"), k + 1)

                def chunk_cols(t, kk):
                    w = min(P, es.Q - (t % nb) * P)
                    src = (a, c, b)[t // nb]
                    return turn(bank(kk)[:, 0:w], src[0:w, t % nb, :], w)
                fill(pe, "prep_" + es.name, chunk_cols)
                pe.wait_ge(S("prep_scan"), k + 1)
                for q, col in enumerate((0, es.L - 1)):
                    ins = mm(bank(7)[0:1, q * P:(q + 1) * P], dA[:, col:col + 1], ident[:, :], start=True, stop=True)
                ins.then_inc(S("ends_ps"), 1)
                pe.wait_ge(S("sel0_ready"), k + 1)
                n = es.tiles - 1
                mm(bank(6)[0:n, 0:es.Q], sel0[:, 0:n], dsb[es.name][:, 0, :], start=True, stop=True).then_inc(S("firsts_ps"), 1)
                pe.wait_ge(S("leave_ready"), k + 1)
                mm(bank(5)[:, 0:es.steps], ones[0:n, :], cmpT[0:n, 0:es.steps], start=True, stop=True).then_inc(S("tiles_ps"), 1)

            prepare(MAIN, 0)
            prepare(FFN, 1)

            pe.wait_ge(S("ld_wraw"), 48)

            def w_turn(t, kk):
                for k in range(2):
                    ins = turn(bank(kk)[:, k * P:(k + 1) * P], wraw[:, t, k * P:(k + 1) * P])
                return ins
            fill(pe, "wT", w_turn)

            def x_turn(name, src):
                def one(t, kk):
                    for k in range(2):
                        ins = turn(bank(kk)[:, k * P:(k + 1) * P],
                                   src[:, t, k * P:(k + 1) * P])
                    return ins
                fill(pe, name, one)

            def product(name, rhs, n):
                def one(t, kk):
                    for k in range(2):
                        ins = mm(bank(kk)[:, 0:n], XT[:, k, t * P:(t + 1) * P], rhs(k), start=(k == 0), stop=(k == 1))
                    return ins
                fill(pe, name, one)

            def gat(g, es, c):
                pe.wait_ge(S("s_ready"), g + 1)
                SA, MA = scan_bufs(g)

                def down(t, kk):
                    for q in range(min(4, es.J - 4 * t)):
                        ins = turn(bank(kk)[:, q * P:(q + 1) * P], s_cols(g)[:, (4 * t + q) * P:(4 * t + q + 1) * P])
                    return ins
                fill(pe, f"sA{g}", down)
                for n in range(2):
                    pe.wait_ge(S("end_ready"), 2 * g + n + 1)
                    mm(bank(7)[0:1, 0:P], dcol[:, 0:1], ident[:, :], start=True, stop=True).then_inc(S("end_row"), 1)
                    pe.wait_ge(S("carry_row"), 2 * g + n + 1)
                    mm(bank(7)[:, 256:257], rowc[0:1, 2, :, :].rearrange("p h r -> p (h r)"), ones[0:1, 0:1],
                       start=True, stop=True).then_inc(S("carry_ps"), 1)
                pe.wait_ge(S("max_ready"), g + 1)

                def up(t, kk):
                    for q in range(min(4, es.J - 4 * t)):
                        j = 4 * t + q
                        ins = turn(bank(kk)[:, q * P:(q + 1) * P], SA[:, j * P:(j + 1) * P])
                    return ins
                fill(pe, f"sB{g}", up)
                base, k = BASE[f"sB{g}"]
                pe.wait_ge(S("bank_free"), base + k)

                nm, H, R = es.name, Hv(c), rows(g)
                gb = groups_before(g)
                sb_ = gb * S2

                def turns(n, b):
                    pe.wait_ge(S("oneh_ready"), n + (gb + 1))
                    pe.wait_ge(S("turned"), n + gb) if gb or not isinstance(n, int) or n else None
                    for u in range(G):
                        ins = pe.transpose(bank(4).bitcast(BF16)[:, u * P:(u + 1) * P], onehB[:, b % 2, u, :], identB[:, :])
                    ins.then_inc(S("turned_ps"), 1)

                def fetch(n):
                    pe.wait_ge(S("turned"), n + (gb + 1))
                    if gb or not isinstance(n, int) or n:
                        pe.wait_ge(S("z_ready"), n + gb)
                    offs = offsets(mybir.EngineType.PE, tP[nm], n * S2, S2, (es.tiles - 1) * 3 * H8)
                    dcols = dS[:, :, :, :].rearrange("p t k h -> p (t k h)")
                    for u in range(G):
                        ins = mm(bank(6)[:, u * 24:(u + 1) * 24], onehT[:, u, :], dcols[:, bass.ds(offs[u // 2], 24)],
                                 start=True, stop=True)
                    ins.then_inc(S("d_ready"), 1)

                def group(n, b, more):
                    if more:
                        turns(n + 1, b + 1)
                    pe.wait_ge(S("oneh_copied"), n + (gb + 1))
                    for k in range(S2):
                        if k == S2 // 2 and more:
                            fetch(n + 1)
                        pe.wait_ge(S("scaled"), n * S2 + (sb_ + k + 1))
                        pe.wait_ge(S("step_done"), n * S2 + (sb_ + k + 1))
                        for u in (2 * k, 2 * k + 1):
                            ins = mm(bank(k)[:, 0:c + 16], oneh[:, b % 2, u, :], R[:, b, u, 0:c + 16],
                                     start=(u % 2 == 0), stop=(u % 2 == 1))
                        ins.then_inc(S("summed"), 1)

                last = es.groups // NBUF - 1
                turns(0, 0)
                fetch(0)
                with pe.Fori(0, last) as i:
                    for b in range(NBUF):
                        group(i * NBUF + b, b, True)
                for b in range(NBUF):
                    group(last * NBUF + b, b, b < NBUF - 1)

            pe.wait_ge(S("xn_ready"), 1)
            x_turn("xT0", nodes(R2))
            pe.wait_ge(S("wT_ready"), 1)
            pe.wait_ge(S("xt_ready"), 1)

            def q_rows(t, kk):
                for k in range(2):
                    ins = mm(bank(kk)[:, 0:320], wT[:, k, t // 10, :], XT[:, k, (t % 10) * 320:(t % 10 + 1) * 320],
                             start=(k == 0), stop=(k == 1))
                return ins
            fill(pe, "q", q_rows)
            product("kv", lambda k: wT[:, k, 2:6, :].rearrange("p o m -> p (o m)"), 512)

            def context(Kv, rhs):
                for a in range(2):
                    for t in range(T):
                        kk = P if t < T - 1 else TAIL
                        r = rhs(a, t, kk)
                        ins = mm(bank(6 + a)[:, 0:r.shape[-1]], Kv[0:kk, t, a * P:(a + 1) * P], r,
                                 start=(t == 0), stop=(t == T - 1))
                ins.then_inc(S("ctx_ps"), 1)

            pe.wait_ge(S("k_ready"), 1)
            context(K0, lambda a, t, kk: V0[0:kk, t, a, :])
            pe.wait_ge(S("ctx_ready"), 1)
            pe.wait_ge(S("ld_gw"), 48)
            product("h0", lambda k: Wn[:, k, :], C)

            def mixo(t, kk):
                for a in range(2):
                    ins = mm(bank(kk)[:, a * 132:(a + 1) * 132], qT[:, a, t * P:(t + 1) * P], BD[:, a, :],
                             start=True, stop=True)
                return ins
            fill(pe, "mixo", mixo)
            pe.wait_ge(S("ao_ready"), 1)
            x_turn("aT", AO)
            pe.wait_ge(S("aT_ready"), 1)
            product("proj", lambda k: wT[:, k, 6:8, :].rearrange("p o m -> p (o m)"), C)
            gat(0, *GATS[0])
            pe.wait_ge(S("xn_ready"), 2)
            x_turn("xT1", Av(C)[:, :, 0:C])
            pe.wait_ge(S("ld_gw"), 96)
            pe.wait_ge(S("xt_ready"), 2)
            product("h1", lambda k: Wn[:, k, :], C)
            gat(1, *GATS[1])
            pe.wait_ge(S("xn_ready"), 3)
            x_turn("xT2", nodes(R2))
            pe.wait_ge(S("ld_gw"), 144)
            pe.wait_ge(S("xt_ready"), 3)
            product("h2", lambda k: Wn[:, k, 0:16], 16)
            gat(2, *GATS[2])

            pe.wait_ge(S("ld_moe"), 64)
            turn(bank(7)[:, 0:16], b1e, 16).then_inc(S("b1_ps"), 1)
            pe.wait_ge(S("b1_ready"), 1)
            pe.wait_ge(S("fin_done"), 3)
            pe.sem_inc(S("hid_free"), 4)
            pe.sem_inc(S("moe_full"), 2 * TB)

            with pe.Fori(0, T // TB) as i:
                def up_proj(e):
                    for f in range(4):
                        for hf in range(2):
                            m = (e * 4 + f) * 2 + hf
                            pe.wait_ge(S("hid_free"), i * 32 + (m + 1))
                            for k in range(2):
                                ins = mm(bank(4 + m % 4)[:, 0:320], W1e[:, e, k, f * P:(f + 1) * P],
                                         XT[:, k, bass.ds(i * TOK + hf * 320, 320)], start=(k == 0), stop=(k == 1))
                            ins.then_inc(S("hid_full"), 1)

                def down_proj(e):
                    pe.wait_ge(S("hid_free"), i * 32 + (4 + 8 * (e + 1)))
                    for k in range(TB):
                        o = e * TB + k
                        pe.wait_ge(S("moe_free"), i * (EXP0 * TB) + (o + 1))
                        mm(bank(o % 4)[:, 0:C], ones[0:1, :], b2e[:, e * C:(e + 1) * C], start=True, stop=False)
                        for f in range(4):
                            ins = mm(bank(o % 4)[:, 0:C], hh[:, e % 2, f, k * P:(k + 1) * P], W2e[:, e, f, :],
                                     start=False, stop=(f == 3))
                        ins.then_inc(S("moe_full"), 1)

                up_proj(0)
                for e in range(EXP0):
                    if e < EXP0 - 1:
                        up_proj(e + 1)
                    down_proj(e)

            pe.wait_ge(S("xn_ready"), 4)
            pe.wait_ge(S("moe0_done"), 1)
            x_turn("xT3", nodes(R2))
            pe.wait_ge(S("mix1_kv"), 1)
            context(K1, lambda a, t, kk: V1[0:kk, t, a * P:(a + 1) * P])
            pe.wait_ge(S("ctx_ready"), 2)
            pe.wait_ge(S("xt_ready"), 4)

            def mix1o(t, kk):
                for a in range(2):
                    ins = mm(bank(kk)[:, a * P:(a + 1) * P], XT[:, a, t * P:(t + 1) * P], BD[:, a, 0:P],
                             start=True, stop=True)
                return ins
            fill(pe, "mix1o", mix1o)
            pe.wait_ge(S("ld_gw"), 192)
            product("h3", lambda k: Wn[:, k, :], C)
            gat(3, *GATS[3])

            for n, src in enumerate((Av(C), nodes(R4))):
                pe.wait_ge(S("bn_in"), n + 1)
                for t in range(T):
                    kk = P if t < T - 1 else TAIL
                    ins = mm(bank(0)[:, 0:C], ones[0:kk, :], src[0:kk, t, 0:C], start=(t == 0), stop=(t == T - 1))
                ins.then_inc(S("bank_full"), 1)

            pe.wait_ge(S("ld_moe1"), 16 * 6)
            turn(bank(7)[:, 0:16], b1r, 16)
            for k in range(2):
                ins = turn(bank(7)[:, 64 + 32 * k:96 + 32 * k], rwr[:, k * P:(k + 1) * P], 32)
            ins.then_inc(S("b1_ps"), 1)
            pe.wait_ge(S("xn_ready"), 5)
            x_turn("xT4", nodes(R1))
            pe.wait_ge(S("xt_ready"), 5)
            pe.wait_ge(S("b1_ready"), 2)
            product("rt", lambda k: rwT[:, k, :], 32)
            pe.wait_ge(S("choice"), 1)
            chosen = R1[:, 0:T * 32].rearrange("p (t e) -> p t e", t=T)
            fill(pe, "ohT", lambda t, kk: turn(bank(kk)[0:32, 0:P], chosen[:, t, :]))
            pe.wait_ge(S("ohT_ready"), 1)
            pe.wait_ge(S("sel_ready"), 1)
            pe.sem_inc(S("w2_done"), 1)
            pe.sem_inc(S("out_free"), 1)
            with pe.Fori(0, T // TB) as i:
                pe.wait_ge(S("out_free"), i + 1)
                for b in range(3):
                    mm(bank(b)[:, 0:512], zrow[0:1, 0:P], zrow[0:1, :], start=True, stop=False, skip_group_check=True)

                def up_pair(j):
                    for hf in range(2):
                        n = 2 * j + hf
                        pe.wait_ge(S("pair_done"), i * 32 + (n + 1))
                        cols = bass.ds(i * TOK + hf * 320, 320)
                        for k in range(2):
                            mm(bank(3 + hf)[:, 0:320], W1x[:, k, j * P:(j + 1) * P], XT[:, k, cols],
                               start=(k == 0), stop=(k == 1))
                        mm(bank(5 + hf)[:, 0:320], selJ[:, j, :], ohE[:, cols],
                           start=True, stop=True).then_inc(S("pair_full"), 1)

                def out_of(k):
                    return bank(k // 2)[:, (k % 2) * C:(k % 2 + 1) * C]

                def down_pair(j):
                    pe.wait_ge(S("pair_done"), i * 32 + (2 + 2 * (j + 1)))
                    for k in range(TB):
                        ins = mm(out_of(k), hm[:, j % 2, k * P:(k + 1) * P], W2r[:, j, :], start=False, stop=False,
                                 skip_group_check=True)
                    ins.then_inc(S("w2_done"), 1)

                up_pair(0)
                pe.wait_ge(S("block_choice"), i + 1)
                for k in range(TB):
                    mm(out_of(k), ohS[:, k * P:(k + 1) * P], b2r, start=False, stop=False, skip_group_check=True)
                for j in range(16):
                    if j < 15:
                        up_pair(j + 1)
                    down_pair(j)
                for b in range(3):
                    ins = mm(bank(b)[:, 0:512], zrow[0:1, 0:P], zrow[0:1, :], start=False, stop=True, skip_group_check=True)
                ins.then_inc(S("out_full"), 1)


_OUTS = [((N, C), "float32")]
_INS = ['x', 'src', 'dst', 'L0_gnn_W1', 'L0_gnn_att_src1', 'L0_gnn_att_dst1', 'L0_gnn_b1', 'L0_gnn_W2',
        'L0_gnn_att_src2', 'L0_gnn_att_dst2', 'L0_gnn_b2', 'L0_mix_Wq', 'L0_mix_Wkv', 'L0_mix_Wproj',
        'L0_mix_bproj', 'L0_ffn_W_gat', 'L0_ffn_att_src', 'L0_ffn_att_dst', 'L0_ffn_b_gat', 'L0_ffn_ln_gamma',
        'L0_ffn_ln_beta', 'L0_ffn_W1', 'L0_ffn_b1', 'L0_ffn_W2', 'L0_ffn_b2', 'L0_ffn_edge_index', 'L1_gnn_W',
        'L1_gnn_att_src', 'L1_gnn_att_dst', 'L1_gnn_bias', 'L1_gnn_gamma', 'L1_gnn_beta', 'L1_mix_kln_weight',
        'L1_mix_kln_bias', 'L1_mix_vln_weight', 'L1_mix_vln_bias', 'L1_ffn_router_w', 'L1_ffn_router_b',
        'L1_ffn_W1', 'L1_ffn_b1', 'L1_ffn_W2', 'L1_ffn_b2']


def kernel(**inputs):
    import concourse.bacc as _bacc
    from concourse.bass_utils import run_bass_kernel_spmd as _run

    nc = _bacc.Bacc("TRN2", target_bir_lowering=False, num_devices=1)
    arrays, aps = {}, {}
    for name in _INS:
        a = np.ascontiguousarray(inputs[name])
        arrays[f"in_{name}"] = a
        aps[name] = nc.dram_tensor(f"in_{name}", a.shape, mybir.dt.from_np(a.dtype), kind="ExternalInput").ap()
    res = nc.dram_tensor("out_0", (N, C), F32, kind="ExternalOutput").ap()
    build(nc, aps, res)
    r = _run(nc, [arrays], core_ids=[0])
    return r.results[0]["out_0"]
```

```python
from contextlib import ExitStack

import concourse.bass as bass
import numpy as np
from concourse import mybir
from concourse.alu_op_type import AluOpType as ALU

F32 = mybir.dt.float32
BF16 = mybir.dt.bfloat16
I32 = mybir.dt.int32
ACT = mybir.ActivationFunctionType
AX = mybir.AxisListType.X

P = 128
N = 3125
T = -(-N // P)
TAIL = N - (T - 1) * P
C = 256
H8 = 8
NEG = -1.0e30
SLOPE = 0.2
IDX = 4096
PADV = (IDX - 1) * IDX
G = 8
S2 = G // 2
EARLY = 2
AHEAD = 3
NBUF = 4
EW = 19
FFN_NODES = 16 * 128
EXP0, F0 = 4, 512
EXP1, F1 = 32, 64
TB = 5
TOK = TB * P


class EdgeSet:

    def __init__(self, name, edges, tiles, j, c):
        self.name, self.edges, self.tiles, self.J = name, edges, tiles, j
        self.W = c + 16
        self.Q = 16 * j
        self.groups = -(-(-(-edges // (2 * P)) + tiles - 1) // (S2 * NBUF)) * NBUF
        self.steps = self.groups * S2
        assert self.Q * P >= edges + 2 * P
        self.L = j * P


MAIN = EdgeSet("m", 50000, T, 25, 256)
FFN = EdgeSet("f", 32768, FFN_NODES // P, 17, 16)
GATS = [(MAIN, 256), (MAIN, 256), (FFN, 16), (MAIN, 256)]
HEADS = (8, 1, 4, 8)

PASSES = [("prep_m", 12), ("wT", 8)]


def _passes():
    out = list(PASSES)
    for g, (es, c) in enumerate(GATS):
        out.append((f"xT{g}", T))
        if g == 3:
            out += [("mix1o", T)]
        if g == 0:
            out += [("q", 2 * TB * 2), ("kv", T), ]
        out.append((f"h{g}", T))
        if g == 0:
            out += [("mixo", T), ("aT", T), ("proj", T)]
        if g == 1:
            out += [("prep_f", 9)]
        out += [(f"sA{g}", -(-es.J // 4)), (f"sB{g}", -(-es.J // 4))]
    out += [("bnm", 1), ("bnv", 1), ("xT4", T), ("rt", T), ("ohT", T), ("chosen", 10)]
    base, at = {}, 5
    for n, k in out:
        base[n] = (at, k)
        at += k
    return base


BASE = _passes()


def rounds_before(g):
    return sum(es.J for es, _ in GATS[:g])


def loads_before(g, b):
    return sum((es.J + 1 - b) // 2 for es, _ in GATS[:g])


def groups_before(g):
    return sum(es.groups for es, _ in GATS[:g])


def build(nc, A, out):
    ctx = ExitStack()
    with ctx:
        def sb(name, shape, dt=F32):
            return ctx.enter_context(nc.sbuf_tensor(name, shape, dt))

        def dram(name, shape, dt=F32):
            return nc.dram_tensor(name, shape, dt, kind="Internal").ap()

        sems = {}

        def S(name):
            if name not in sems:
                sems[name] = ctx.enter_context(nc.semaphore(name))
            return sems[name]

        arena = sb("arena", [P, 29904])
        R1 = arena[:, 0:6800]
        R2 = arena[:, 6800:13600]
        R4 = arena[:, 13600:21200]
        R3 = arena[:, 21200:29904]
        X = sb("X", [P, T, C])
        oneh = sb("oneh", [P, 2, G, P])
        onehB = sb("onehB", [P, 2, G, P], BF16)
        onehT = sb("onehT", [P, G, P], BF16)
        identB = sb("identB", [P, P], BF16)
        iotaB = sb("iotaB", [P, P], BF16)
        dS = sb("dS", [P, T, 3, H8], BF16)
        ident = sb("ident", [P, P])
        ones = sb("ones", [P, P])
        iota = sb("iota", [P, MAIN.Q])
        stage = sb("stage", [P, NBUF, G, EW])
        idx = sb("idx", [P, NBUF, G], I32)
        sProd = R1[:, 3200:4800]
        sMask = R1[:, 4800:5200].bitcast(BF16)
        idx_s = sb("idx_s", [P, 2, G], I32)
        dat_s = sb("dat_s", [P, 2, G], I32)
        padT = sb("padT", [P, 16], I32)
        zz = sb("zz", [P, G, 2, H8])
        zd = sb("zd", [P, G, H8])
        drel = sb("drel", [P, 2, G])
        Wn = sb("Wn", [P, 2, C + 16])
        brow = sb("brow", [P, 4, C])
        dsb = {e.name: sb("dsb_" + e.name, [P, 3, e.Q]) for e in (MAIN, FFN)}
        srcT = {e.name: sb("srcT_" + e.name, [P, e.Q], BF16) for e in (MAIN, FFN)}
        flagA = {e.name: sb("flagA_" + e.name, [P, e.L + 1], BF16) for e in (MAIN, FFN)}
        seam = {e.name: sb("seam_" + e.name, [1, 4, H8, 16]) for e in (MAIN, FFN)}
        t128 = {e.name: sb("t128_" + e.name, [P, e.steps]) for e in (MAIN, FFN)}
        steps = {e.name: sb("steps_" + e.name, [65, e.steps], I32) for e in (MAIN, FFN)}
        tI, tP, cI = ({k: v[32 * q:32 * q + 1, :] for k, v in steps.items()} for q in range(3))
        rowc = sb("rowc", [1, 3, H8, 16])
        chan = sb("chan", [P, 1])
        zrow = oneh[:, :, :, :].rearrange("p a b c -> p (a b c)")[0:1, 1024:1536]
        rowsum = sb("rowsum", [P, 200])
        small3 = oneh[:, :, :, :].rearrange("p a b c -> p (a b c)")[:, 0:4 * T * H8].rearrange(
            "p (q t h) -> p q t h", q=4, t=T)
        small4 = onehT[:, :, :].rearrange("p a b -> p (a b)").bitcast(F32)
        carry = sb("carry", [P, 1])
        mv = sb("mv", [P, T, 2])
        st6 = sb("st6", [P, TB, 6])
        rstd = sb("rstd", [P, T])
        epsc = sb("epsc", [P, 1])
        BD = sb("BD", [P, 2, 132])
        mask = sb("mask", [P, 132])
        b1T = sb("b1T", [P, 16])
        rwT = sb("rwT", [P, 2, EXP1])
        gates = sb("gates", [P, T, EXP0])
        dcol = sb("dcol", [P, 8])
        PS = ctx.enter_context(nc.psum_tensor("PS", [P, 8, 512], F32))

        def Hv(c):
            return R2[:, 0:T * (c + 16)].rearrange("p (t w) -> p t w", t=T)

        def Av(c):
            return R1[:, 0:T * (c + 16)].rearrange("p (t w) -> p t w", t=T)

        def nodes(region):
            return region[:, 0:T * C].rearrange("p (t c) -> p t c", t=T)

        XT = R3[:, 0:2 * T * P].rearrange("p (k n) -> p k n", k=2)

        def EV(es):
            return R4[:, 0:es.Q * EW].rearrange("p (q w) -> p q w", w=EW)

        def rows(g):
            w = GATS[g][1] + 16
            return (R2[:, 1000:1000 + NBUF * G * w] if g == 2 else R3[:, 0:NBUF * G * w]).rearrange("p (b u w) -> p b u w", b=NBUF, u=G)

        def scan_bufs(g):
            L = GATS[g][0].L
            return (R1[:, 1000:1000 + L], R1[:, 3200:3200 + L]) if g == 2 else (R3[:, 5504:5504 + L], R1[:, 3200:3200 + L])

        lows = R3[:, 6400:8448].bitcast(BF16).rearrange("p (b e) -> p b e", b=2)
        place = oneh[:, :, :, :].rearrange("p a b c -> p (a b c)").bitcast(BF16).rearrange("p (b e) -> p b e", b=2)

        def s_parts(g):
            w = GATS[g][0].tiles * HEADS[g]
            return onehT[:, :, :].rearrange("p a b -> p (a b)")[:, 0:3 * w], w

        def s_cols(g):
            L = GATS[g][0].L
            return R4[:, 5200:5200 + L] if g == 2 else R1[:, 0:L]

        pk = {e.name: dram("pk_" + e.name, (e.Q * P + P,), I32) for e in (MAIN, FFN)}
        srt1 = dram("srt1", (FFN.edges, 1), I32)
        srt2 = dram("srt2", (FFN.edges, 1), I32)
        tab = [dram(f"tab{g}", (T * P, c + 8)) for g, (_, c) in enumerate(GATS)]
        lowQ = {e.name: dram("lowQ_" + e.name, (e.Q * P,), BF16) for e in (MAIN, FFN)}
        low = {e.name: dram("low_" + e.name, (e.Q * P,), BF16) for e in (MAIN, FFN)}

        SC = FFN.edges // P
        DIGITS = ((12, 64), (18, 32))
        sortO = (R3.bitcast(BF16), R4.bitcast(BF16))
        sortH = (arena[:, 0:64 * SC], R3)
        keep = (R4[:, 6400:7600], Wn[:, :, :].rearrange("p k c -> p (k c)"))
        srtV, srtI = ([k[:, q * SC:(q + 1) * SC].bitcast(I32) for k in keep] for q in range(2))
        ltri, offd = R4[:, 6912:7040], R4[:, 7040:7168]
        rest = R4[:, 4096:6400]
        srtT = rest[:, 0:SC].bitcast(I32)
        srtD = rest[:, SC:2 * SC]
        srtP = rest[:, 2 * SC:3 * SC]
        sGl, sCnt, sGex, sXo = (rest[:, 3 * SC + 64 * q:3 * SC + 64 * (q + 1)] for q in range(4))
        pkS = R3[0:125, 0:400].bitcast(I32)
        pkD = R3[0:125, 400:800].bitcast(I32)

        def prepv(es):
            nb = -(-es.Q // P)
            return [nb] + [R1[:, k * 512:k * 512 + nb * P].rearrange("p (b i) -> p b i", b=nb) for k in range(4)]

        sel0 = R1[:, 2048:2048 + 128]
        cmpT = R1[:, 2304:2304 + MAIN.Q]
        small = R1[:, 3000:3032]
        lowI = R1[:, 4300:4812].bitcast(I32)
        lowB = R1[:, 4812:5068].bitcast(BF16)
        tileI = R1[:, 5100:5500].bitcast(I32)
        tS = R1[:, 3200:3200 + 2 * MAIN.steps]
        pkA = R3[:, 0:3200]
        dA = R3[:, 3200:6400]
        fA = R4[:, 0:3200]

        wraw = R1[:, 0:2048].rearrange("p (o c) -> p o c", o=8)
        wT = R3[:, 6400:8448].rearrange("p (k o m) -> p k o m", k=2, o=8)
        qT = R4[:, 0:2 * T * P].rearrange("p (k n) -> p k n", k=2)
        K0 = nodes(R1)
        V0 = R2[:, 0:T * 258].rearrange("p (t a w) -> p t a w", t=T, a=2)
        AO = nodes(R1)
        eluT = oneh[:, :, :, :].rearrange("p a b c -> p (a b c)")
        K1, V1 = nodes(R1), nodes(R4)
        W1e = R4[:, 0:4096].rearrange("p (e k f) -> p e k f", e=EXP0, k=2)
        W2e = R2[:, 0:4096].rearrange("p (e k f) -> p e k f", e=EXP0, k=4)
        hh = R1[:, 0:2 * 4 * TOK].rearrange("p (b f n) -> p b f n", b=2, f=4)
        b1e = R2[0:16, 4096:4224]
        b2e = R2[:, 4300:4300 + EXP0 * C]
        W1x = R4[:, 0:4096].rearrange("p (k m) -> p k m", k=2)
        W2r = R2[:, 0:4096].rearrange("p (j c) -> p j c", j=16)
        b1r = R2[0:16, 4096:4224]
        b2r = R2[0:32, 4300:4556]
        rwr = R2[0:32, 4600:4856]
        ohE = R4[0:32, 4100:4100 + T * P]
        experts = R3[0:32, 6400:6528]
        chosenB = R3[:, 6600:6600 + T * P // 2].bitcast(BF16)
        expertOf = R3[:, 8300:8316]
        hm = R1[:, 0:2 * TOK].rearrange("p (b n) -> p b n", b=2)
        ohS = R1[0:32, 2000:2000 + TOK]
        ha = R1[:, 1300:1300 + TOK].rearrange("p (b n) -> p b n", b=2)

        block = ctx.enter_context(nc.Block())

        def offsets(engine, table, step, n, last):
            return nc.values_load_multi_w_load_instructions(
                table[:, at(step, n)], engines=(engine,), min_val=0, max_val=last, bass_reorder=False,
                skip_runtime_bounds_check_because="the tables are clamped when they are built")[1]

        def at(start, n):
            return slice(start, start + n) if isinstance(start, int) else bass.ds(start, n)

        def bank(b):
            return PS[:, b, :]

        class Chain:

            def __init__(self, eng, name):
                self.eng, self.sem, self.n, self.i, self.k0 = eng, S(name), 0, None, 0

            def value(self):
                return self.n if self.i is None else self.i * self.K + self.n

            def __call__(self, ins):
                ins.then_inc(self.sem, 1)
                self.n += 1
                self.eng.wait_ge(self.sem, self.value())

            def loop(self, count, per, body, first=0):
                self.n -= first * per
                n0 = self.n
                with self.eng.Fori(first, count) as i:
                    self.i, self.K = i, per
                    body(i)
                    assert self.n - n0 == per, (self.n - n0, per)
                    self.i = None
                self.n = n0 + per * count

        def consume(eng, name, fn):
            base, n = BASE[name]
            if n == T:
                with eng.Fori(0, T // TB) as i:
                    for k in range(TB):
                        t = i * TB + k
                        eng.wait_ge(S("bank_full"), t + (base - 4))
                        fn(t, k).then_inc(S("bank_free"), 1)
            else:
                for t in range(n):
                    eng.wait_ge(S("bank_full"), t + base - 4)
                    fn(t, t % TB).then_inc(S("bank_free"), 1)
            eng.wait_ge(S("bank_free"), base + n)

        def fill(eng, name, fn):
            base, n = BASE[name]
            eng.wait_ge(S("bank_free"), base)
            for t in range(n):
                if t >= TB:
                    eng.wait_ge(S("bank_free"), t + base - 4)
                fn(t, t % TB).then_inc(S("bank_full"), 1)

        @block.sync
        def _(sp):
            def load(dst, src, name):
                sp.dma_start(dst, src).then_inc(S(name), 16)

            load(pkS, A["src"].rearrange("(p c) -> p c", p=125), "ld_edges")
            load(pkD, A["dst"].rearrange("(p c) -> p c", p=125), "ld_edges")
            load(srtT, A["L0_ffn_edge_index"][0].rearrange("(p c) -> p c", p=P), "ld_fedges")
            load(srtV[0], A["L0_ffn_edge_index"][1].rearrange("(p c) -> p c", p=P), "ld_fedges")
            sp.wait_ge(S("x_cleared"), 1)
            load(X[:, 0:T - 1, :], A["x"][0:(T - 1) * P, :].rearrange("(t p) c -> p t c", p=P), "ld_x")
            load(X[0:TAIL, T - 1, :], A["x"][(T - 1) * P:N, :], "ld_x")
            sp.wait_ge(S("packed"), 1)
            sp.dma_start(pk["m"][0:50000].rearrange("(p c) -> p c", p=125), pkS).then_inc(S("pkm_st"), 16)
            for e in (MAIN, FFN):
                n = e.Q * P + P - e.edges
                w = n // 16
                assert n % 16 == 0 and w <= P or e is FFN
                for o in range(0, w, P):
                    k = min(P, w - o)
                    sp.dma_start(pk[e.name][e.edges + 16 * o:e.edges + 16 * (o + k)].rearrange("(p c) -> p c", c=16),
                                 padT[0:k, 0:16]).then_inc(S("pk_st"), 16)
            def load_prep(es, k):
                nb, a, b, _, _ = prepv(es)
                name = "ld_prep"
                for dst, off in ((a, 0), (b, 1)):
                    v = pk[es.name][off:off + es.Q * P].rearrange("(q i) -> q i", i=P)
                    load(dst[:, 0:nb - 1, :].bitcast(I32), v[0:(nb - 1) * P].rearrange("(b p) i -> p b i", p=P), name)
                    load(dst[0:16, nb - 1, :].bitcast(I32), v[(nb - 1) * P:es.Q], name)
                rws = pk[es.name][0:es.Q * P].rearrange("(r x) -> r x", r=16)
                load(pkA[:, 0:es.L].bitcast(I32), rws.unsqueeze(1).to_broadcast((16, H8, es.L)), name)

            def store_low(es, k):
                nb = prepv(es)[0]
                v = lowQ[es.name].rearrange("(q i) -> q i", i=P)
                low3 = lowB[:, 0:nb * P].rearrange("p (b i) -> p b i", b=nb)
                sp.wait_ge(S("low_ready"), k + 1)
                sp.dma_start(v[0:(nb - 1) * P].rearrange("(b p) i -> p b i", p=P), low3[:, 0:nb - 1, :]).then_inc(S("low_st"), 16)
                sp.dma_start(v[(nb - 1) * P:es.Q], low3[0:16, nb - 1, :]).then_inc(S("low_st"), 16)
                sp.wait_ge(S("low_st"), 32 * (k + 1))
                sp.dma_start(low[es.name].rearrange("(j r i) -> j r i", r=16, i=P),
                             lowQ[es.name].rearrange("(r j i) -> j r i", r=16, i=P)).then_inc(S("low_order"), 16)

            def load_lows(g, es):
                n0 = rounds_before(g)

                def one(r, b, first):
                    if not first:
                        sp.wait_ge(S("low_used"), r + (n0 - 1))
                    sp.dma_start(lows[:, b, :], low[es.name][at(r * 2048, 2048)].unsqueeze(0).to_broadcast((P, 2048))
                                 ).then_inc(S(f"ld_low{b}"), 16)
                sp.wait_ge(S("records"), g + 1)
                sp.wait_ge(S("low_order"), 32 if g else 16)
                one(0, 0, True)
                one(1, 1, True)
                with sp.Fori(1, es.J // 2) as i:
                    for b in range(2):
                        one(i * 2 + b, b, False)
                one(es.J - 1, 0, False)

            sp.wait_ge(S("pk_st"), 48)
            sp.wait_ge(S("pkm_st"), 16)
            sp.wait_ge(S("rank_ready"), 1)
            load_prep(MAIN, 0)
            store_low(MAIN, 0)
            sp.wait_ge(S("prep_done"), 1)
            for i, (w, n) in enumerate((("L0_mix_Wq", 2), ("L0_mix_Wkv", 4), ("L0_mix_Wproj", 2))):
                o = (0, 2, 6)[i]
                load(wraw[:, o:o + n, :], A[w].rearrange("(o p) c -> p o c", p=P), "ld_wraw")

            def row(i, name, sem):
                v = A[name]
                if len(v.shape) == 2:
                    v = v.rearrange("a b -> (a b)")
                if len(v.shape) == 3:
                    v = v.rearrange("a b c -> (a b c)")
                n = v.shape[0]
                load(brow[:, i, 0:n], v.unsqueeze(0).to_broadcast((P, n)), sem)

            wnames = [("L0_gnn_W1", "L0_gnn_att_src1", "L0_gnn_att_dst1"),
                      ("L0_gnn_W2", "L0_gnn_att_src2", "L0_gnn_att_dst2"),
                      ("L0_ffn_W_gat", "L0_ffn_att_src", "L0_ffn_att_dst"),
                      ("L1_gnn_W", "L1_gnn_att_src", "L1_gnn_att_dst")]
            for g, (es, c) in enumerate(GATS):
                if g:
                    sp.wait_ge(S("fin_done"), g)
                if g == 3:
                    row(0, "L1_mix_kln_weight", "ld_mix1")
                    row(1, "L1_mix_kln_bias", "ld_mix1")
                    row(2, "L1_mix_vln_weight", "ld_mix1")
                    row(3, "L1_mix_vln_bias", "ld_mix1")
                load(Wn[:, :, 0:c], A[wnames[g][0]].rearrange("(k p) c -> p k c", p=P), "ld_gw")
                if g == 3:
                    sp.wait_ge(S("mix1_kv"), 1)
                row(0, wnames[g][1], "ld_gw")
                row(1, wnames[g][2], "ld_gw")
                if g == 0:
                    row(2, "L0_gnn_b1", "ld_b")
                    row(3, "L0_mix_bproj", "ld_b")
                if g == 1:
                    row(2, "L0_gnn_b2", "ld_b")
                if g == 2:
                    row(2, "L0_ffn_b_gat", "ld_b")
                    row(3, "L0_ffn_ln_gamma", "ld_b")
                if g == 3:
                    row(2, "L1_gnn_bias", "ld_b")
                sp.wait_ge(S("h_copied"), g + 1)
                sp.dma_start(tab[g].rearrange("(t p) w -> p t w", p=P), Hv(c)[:, :, 0:c + 8]).then_inc(S("tab_st"), 16)
                if g == 0:
                    for b in range(2):
                        sp.wait_ge(S(f"scat{b}"), 8 * SC)
                    sp.wait_ge(S("sort_room"), 1)
                    load(srtV[1], srt1.rearrange("(p c) w -> p (c w)", p=P), "ld_sort1")
                if g == 1:
                    load_prep(FFN, 1)
                    store_low(FFN, 1)
                load_lows(g, es)
                if g == 0:
                    for b in range(2):
                        sp.wait_ge(S(f"scat{b}"), 16 * SC)
                    sp.dma_start(pk["f"][0:FFN.edges].rearrange("(p c) -> p c", p=P),
                                 srt2.rearrange("(p c) w -> p (c w)", p=P)).then_inc(S("pk_st"), 16)
                    sp.wait_ge(S("pk_st"), 64)
                if g == 2:
                    sp.wait_ge(S("att_used"), 3)
                    row(0, "L0_ffn_ln_beta", "ld_b2")
                    sp.wait_ge(S("fin_done"), 3)
                    load(W1e[:, :, :, :].rearrange("p e k f -> p (e k) f"), A["L0_ffn_W1"].rearrange("e (k p) f -> p (e k) f", p=P), "ld_moe")
                    load(W2e[:, :, :, :].rearrange("p e k f -> p (e k) f"), A["L0_ffn_W2"].rearrange("e (k p) f -> p (e k) f", p=P), "ld_moe")
                    load(b1e, A["L0_ffn_b1"].rearrange("e (k p) -> (e k) p", p=P), "ld_moe")
                    load(b2e, A["L0_ffn_b2"].rearrange("e c -> (e c)").unsqueeze(0).to_broadcast((P, EXP0 * C)), "ld_moe")
                    sp.wait_ge(S("moe0_done"), 1)
                if g == 3:
                    sp.wait_ge(S("att_used"), 4)
                    row(0, "L1_gnn_gamma", "ld_b2")
                    row(1, "L1_gnn_beta", "ld_b2")
            sp.wait_ge(S("fin_done"), 4)
            for k in range(2):
                load(W1x[:, k, :].rearrange("p (e f) -> p e f", e=EXP1),
                     A["L1_ffn_W1"][:, k * P:(k + 1) * P, :].rearrange("e p f -> p e f"), "ld_moe1")
            load(W2r, A["L1_ffn_W2"].rearrange("(j e) f c -> (e f) j c", e=2), "ld_moe1")
            load(b1r, A["L1_ffn_b1"].rearrange("(j e) f -> j (e f)", e=2), "ld_moe1")
            load(b2r, A["L1_ffn_b2"], "ld_moe1")
            load(rwr, A["L1_ffn_router_w"], "ld_moe1")
            sp.wait_ge(S("bn_done"), 1)
            row(0, "L1_ffn_router_b", "ld_rb")
            sp.wait_ge(S("moe1_done"), 1)
            sp.dma_start(out[0:(T - 1) * P, :].rearrange("(t p) c -> p t c", p=P), X[:, 0:T - 1, :]).then_inc(S("st_out"), 16)
            sp.dma_start(out[(T - 1) * P:N, :], X[0:TAIL, T - 1, :]).then_inc(S("st_out"), 16)
            sp.wait_ge(S("st_out"), 32)


        @block.gpsimd
        def _(pool):
            L = Chain(pool, "pool_chain")
            L(pool.memset(ident[:, :], 0.0))
            L(pool.affine_select(out=ident[:, :], in_=ident[:, :], compare_op=ALU.not_equal, fill=1.0,
                                 base=0, pattern=[[-1, P]], channel_multiplier=1))
            L(pool.tensor_copy(identB[:, :], ident[:, :]))
            L(pool.memset(ones[:, :], 1.0))
            L(pool.affine_select(out=ltri, in_=ones[:, :], compare_op=ALU.is_gt, fill=0.0,
                                 base=0, pattern=[[1, P]], channel_multiplier=-1))
            L(pool.affine_select(out=offd, in_=ones[:, :], compare_op=ALU.not_equal, fill=0.0,
                                 base=0, pattern=[[-1, P]], channel_multiplier=1))
            L(pool.iota(iota[:, :], [[1, MAIN.Q]], base=0, channel_multiplier=0,
                        allow_small_or_imprecise_dtypes=True))
            L(pool.tensor_copy(iotaB[:, :], iota[:, 0:P]))
            L(pool.iota(chan[:, :], [[0, 1]], base=0, channel_multiplier=1, allow_small_or_imprecise_dtypes=True))
            L(pool.memset(mask[:, :], 1.0))
            for v, pat, neg in ((mask[:, 0:P].rearrange("p (h e) -> p h e", h=4), [[-32, 4], [0, 32]], [[32, 4], [0, 32]]),
                                (mask[:, P:P + 4], [[-32, 4]], [[32, 4]])):
                L(pool.affine_select(out=v, in_=v, compare_op=ALU.is_ge, fill=0.0, base=0,
                                     pattern=pat, channel_multiplier=1))
                L(pool.affine_select(out=v, in_=v, compare_op=ALU.is_gt, fill=0.0, base=32,
                                     pattern=neg, channel_multiplier=-1))
            pool.sem_inc(S("consts"), 1)

            for p in range(2):
                pool.wait_ge(S("rank_ready"), p + 1)
                dst = (srt1, srt2)[p]

                def body(i, p=p, dst=dst):
                    for b in range(2):
                        if not isinstance(i, int) or p:
                            pool.wait_ge(S(f"scat{b}"), i * P + p * 8 * SC)
                        L(pool.tensor_copy(idx_s[:, b, :], srtI[p][:, at(i * 16 + 8 * b, 8)]))
                        L(pool.tensor_copy(dat_s[:, b, :], srtV[p][:, at(i * 16 + 8 * b, 8)]))
                        pool.sem_inc(S("pool_turn"), 1)
                        for u in range(G):
                            pool.indirect_dma_start(
                                out=dst, out_offset=bass.IndirectOffsetOnAxis(ap=idx_s[:, b, u:u + 1], axis=0),
                                in_=dat_s[:, b, u:u + 1], in_offset=None).then_inc(S(f"scat{b}"), 16)
                body(0)
                L.loop(SC // 16, 4, body, first=1)

            for g, (es, c) in enumerate(GATS):
                sp_rows = rows(g)
                pool.wait_ge(S("tab_st"), 16 * (g + 1))
                def gather(b, g=g, c=c, sp_rows=sp_rows):
                    pool.sem_inc(S("pool_turn"), 1)
                    for u in range(G):
                        pool.indirect_dma_start(
                            out=sp_rows[:, b, u, 0:c + 8], out_offset=None, in_=tab[g],
                            in_offset=bass.IndirectOffsetOnAxis(ap=idx[:, b, u:u + 1], axis=0),
                        ).then_inc(S(f"gat{b}"), 16)
                for b in range(NBUF):
                    if b == 0:
                        pool.wait_ge(S("first_idx"), g + 1)
                    if b == EARLY:
                        pool.wait_ge(S("rows_free"), g + 1)
                    if b >= EARLY:
                        pool.wait_ge(S("staged"), b + 1 + groups_before(g))
                    gather(b)
                with pool.Fori(1, es.groups // NBUF) as i:
                    for b in range(NBUF):
                        pool.wait_ge(S("staged"), i * NBUF + (b + 1 + groups_before(g)))
                        gather(b)

        @block.vector
        def _(v):
            L = Chain(v, "dve_chain")
            tt, ts, stt = v.tensor_tensor, v.tensor_scalar, v.scalar_tensor_tensor

            def tell(name, k=1):
                v.sem_inc(S(name), k)

            def scan(out_, d0, d1, init, o0, o1):
                return v.tensor_tensor_scan(out_, d0, d1, init, o0, o1)

            tell("bank_free", TB)
            tell("step_done", 4)
            tell("group_done", NBUF)
            tell("moe_free", 4)
            tell("pair_done", 2)
            tell("s_free", 2)
            L(v.memset(X[:, T - 1, :], 0.0))
            tell("x_cleared")
            L(v.memset(padT[:, :], PADV))
            L(v.memset(epsc[:, :], 1e-5))
            v.wait_ge(S("ld_edges"), 32)
            L(ts(pkD, pkD, 12, None, ALU.logical_shift_left))
            L(tt(pkS, pkS, pkD, ALU.bitwise_or))
            tell("packed")
            v.wait_ge(S("ld_fedges"), 32)
            L(ts(srtV[0], srtV[0], 12, None, ALU.logical_shift_left))
            L(tt(srtV[0], srtV[0], srtT, ALU.bitwise_or))

            def sort_pass(p):
                sh, B = DIGITS[p]
                if p:
                    tell("sort_room")
                    v.wait_ge(S("ld_sort1"), 16)
                V, I, O_, H_ = srtV[p], srtI[p], sortO[p][:, 0:B * SC], sortH[p][:, 0:B * SC]
                O = O_.rearrange("p (b c) -> p b c", b=B)
                Hc = H_.rearrange("p (b c) -> p b c", b=B)
                L(ts(srtT, V, sh, B - 1, ALU.logical_shift_right, ALU.bitwise_and))
                L(v.tensor_copy(srtD, srtT))
                L(tt(O, srtD.unsqueeze(1).to_broadcast((P, B, SC)),
                     iota[:, 0:B].unsqueeze(2).to_broadcast((P, B, SC)), ALU.is_equal))
                L(scan(H_, O_, O_, 0.0, ALU.add, ALU.max))
                L(v.tensor_copy(sGl[:, 0:B], Hc[:, :, SC - 1]))
                L(v.memset(sGex[:, 0:1], 0.0))
                L(v.tensor_copy(sGex[:, 1:B], sGl[:, 0:B - 1]))
                L(tt(sCnt[:, 0:B], sGl[:, 0:B], sGex[:, 0:B], ALU.subtract))
                tell("counts_ready")
                v.wait_ge(S("offsets"), p + 1)
                L(ts(sXo[:, 0:B], bank(7)[:, 0:B], -1.0, None, ALU.add))
                L(tt(Hc, Hc, sXo[:, 0:B].unsqueeze(2).to_broadcast((P, B, SC)), ALU.add))
                L(tt(Hc, Hc, O, ALU.mult))
                L(v.tensor_reduce(srtP, Hc.rearrange("p b c -> p c b"), AX, ALU.add))
                L(v.tensor_copy(I, srtP))
                tell("rank_ready")

            v.wait_ge(S("consts"), 1)
            v.wait_ge(S("pkm_st"), 16)
            sort_pass(0)

            def consts_of(es, k):
                nb, a, b, c, d = prepv(es)
                nm = es.name
                v.wait_ge(S("ld_prep"), 80 * (k + 1))
                v.wait_ge(S("low_st"), 32 * k) if k else None
                last = [(slice(0, P), slice(0, nb - 1)), (slice(0, 16), slice(nb - 1, nb))]
                for ps_, bs in last:
                    A_, B_, C_, D_ = (q[ps_, bs, :] for q in (a, b, c, d))
                    Ai, Bi = A_.bitcast(I32), B_.bitcast(I32)
                    L(ts(D_.bitcast(I32), Ai, IDX - 1, None, ALU.bitwise_and))
                    L(v.tensor_copy(C_, D_.bitcast(I32)))
                    l3 = (q[:, 0:nb * P].rearrange("p (b i) -> p b i", b=nb)[ps_, bs, :] for q in (lowI, lowB))
                    li, lb = l3
                    L(ts(li, D_.bitcast(I32), P - 1, None, ALU.bitwise_and))
                    L(v.tensor_copy(lb, li))
                    L(ts(Ai, Ai, 12, None, ALU.logical_shift_right))
                    L(ts(Bi, Bi, 12, None, ALU.logical_shift_right))
                    L(v.tensor_copy(D_, Ai))
                    L(v.tensor_copy(A_, Bi))
                    L(tt(B_, A_, D_, ALU.not_equal))
                    L(v.tensor_copy(A_, D_))
                tell("low_ready")
                tell("prep_rows")
                Ll = es.L
                L(ts(fA[:, 0:Ll].bitcast(I32), pkA[:, 0:Ll].bitcast(I32), 12, None, ALU.logical_shift_right))
                L(v.tensor_copy(dA[:, 0:Ll], fA[:, 0:Ll].bitcast(I32)))
                L(tt(fA[:, 1:Ll], dA[:, 1:Ll], dA[:, 0:Ll - 1], ALU.not_equal))
                L(ts(flagA[nm][:, 1:Ll], fA[:, 1:Ll], NEG, None, ALU.mult))
                L(v.memset(flagA[nm][:, 0:1], 0.0))
                L(v.memset(flagA[nm][:, Ll:Ll + 1], 0.0))
                tell("prep_scan")
                consume(v, "prep_" + nm, lambda t, kk: v.tensor_copy(
                    dsb[nm][:, t // nb, (t % nb) * P:min((t % nb + 1) * P, es.Q)],
                    bank(kk)[:, 0:min(P, es.Q - (t % nb) * P)]))
                L(v.tensor_copy(tileI[:, 0:es.Q], dsb[nm][:, 1, :]))
                L(ts(tileI[:, 0:es.Q], tileI[:, 0:es.Q], 7, None, ALU.logical_shift_right))
                L(v.tensor_copy(srcT[nm][:, :].rearrange("p (j r) -> p r j", r=16),
                                tileI[:, 0:es.Q].rearrange("p (r j) -> p r j", r=16)))
                v.wait_ge(S("ends_ps"), k + 1)
                L(v.tensor_copy(rowc[0:1, 0:2, :, :], bank(7)[0:1, 0:256].rearrange("p (k r h) -> p k h r", k=2, h=H8)))
                f_, l_ = rowc[0:1, 0, :, :], rowc[0:1, 1, :, :]
                sm = seam[nm]
                L(v.memset(sm[:, :, :, :], 1.0))
                L(tt(sm[:, 0, :, 1:16], f_[:, :, 1:16], f_[:, :, 0:15], ALU.not_equal))
                L(tt(sm[:, 1, :, 1:16], f_[:, :, 1:16], l_[:, :, 0:15], ALU.not_equal))
                L(tt(sm[:, 2, :, 0:15], l_[:, :, 1:16], l_[:, :, 0:15], ALU.not_equal))
                L(tt(sm[:, 3, :, 0:15], f_[:, :, 1:16], l_[:, :, 0:15], ALU.not_equal))
                L(ts(sm[:, :, :, :], sm[:, :, :, :], NEG, None, ALU.mult))
                n = es.tiles - 1
                L(v.memset(sel0, 0.0))
                L(v.memset(sel0[0:1, :], 1.0))
                tell("sel0_ready")
                v.wait_ge(S("firsts_ps"), k + 1)
                thr, cnt = small[:, 0:1], small[:, 1:2]
                L(ts(thr, chan[:, :], 128.0, 128.0, ALU.mult, ALU.add))
                L(ts(cmpT[0:n, 0:es.Q // 2], bank(6)[0:n, 0:es.Q:2], thr[0:n, :], None, ALU.is_lt))
                L(v.tensor_reduce(cnt[0:n, :], cmpT[0:n, 0:es.Q // 2], AX, ALU.add))
                L(stt(out=cnt[0:n, :], in0=cnt[0:n, :], scalar=1.0, in1=chan[0:n, :], op0=ALU.max, op1=ALU.add))
                L(ts(cmpT[0:n, 0:es.steps], iota[0:n, 0:es.steps], cnt[0:n, :], None, ALU.is_ge))
                tell("leave_ready")
                v.wait_ge(S("tiles_ps"), k + 1)
                L(v.tensor_copy(tS[:, 0:es.steps], bank(5)[:, 0:es.steps]))
                L(ts(t128[nm][:, :], tS[:, 0:es.steps], 128.0, None, ALU.mult))
                for tb, w, q in ((tI, es.W, 0), (tP, 3 * H8, 32)):
                    L(ts(tS[:, MAIN.steps:MAIN.steps + es.steps], tS[:, 0:es.steps], float(w), None, ALU.mult))
                    L(v.tensor_copy(tb[nm], tS[q:q + 1, MAIN.steps:MAIN.steps + es.steps]))
                L(tt(cmpT[:, 0:es.steps], iota[:, 0:es.steps], tS[:, 0:es.steps], ALU.subtract))
                L(ts(cmpT[:, 0:es.steps], cmpT[:, 0:es.steps], float(es.Q // 2 - 1), 2.0 * EW, ALU.min, ALU.mult))
                L(v.tensor_copy(cI[nm], cmpT[64:65, 0:es.steps]))
                tell("prep_done")

            consts_of(MAIN, 0)

            def norm(k, dst):
                for t in range(T):
                    L(v.bn_stats(st6[:, t % TB, :], X[:, t, :]))
                    L(v.bn_aggr(mv[:, t, :], st6[:, t % TB, :]))
                tell("var_ready")
                v.wait_ge(S("std_ready"), k + 1)
                L(v.reciprocal(rstd[:, :], rstd[:, :]))
                L(tt(dst, X[:, :, :], mv[:, :, 0:1].to_broadcast((P, T, C)), ALU.subtract))
                L(tt(dst, dst, rstd[:, :].unsqueeze(2).to_broadcast((P, T, C)), ALU.mult))
                tell("xn_ready")

            def elu1(region, name):
                for q in range(4):
                    L(ts(eluT[:, 0:1600], region[:, q * 1600:(q + 1) * 1600], 0.0, None, ALU.min))
                    tell("elu_min")
                    v.wait_ge(S("elu_exp"), 4 * (name == "k") + q + 1)
                    L(stt(out=region[:, q * 1600:(q + 1) * 1600], in0=region[:, q * 1600:(q + 1) * 1600], scalar=0.0,
                          in1=eluT[:, 0:1600], op0=ALU.max, op1=ALU.add))

            def lrelu(x):
                L(stt(out=x, in0=x, scalar=SLOPE, in1=x, op0=ALU.mult, op1=ALU.max))

            def score_weights(g, es, c):
                heads = HEADS[g]
                rep = 8 // heads
                tmp = small3[:, :, :, :].rearrange("p q t h -> p (q t h)")[:, 0:2 * c].rearrange("p (k c) -> p k c", k=2)
                v.wait_ge(S("ld_gw"), 16 * 3 * (g + 1))
                for q in range(2):
                    L(tt(tmp, Wn[:, :, 0:c], brow[:, q, 0:c].unsqueeze(1).to_broadcast((P, 2, c)), ALU.mult))
                    sc = rowsum[:, 0:2 * heads]
                    L(v.tensor_reduce(sc, tmp.rearrange("p k (h e) -> p (k h) e", h=heads), AX, ALU.add))
                    sc = sc.rearrange("p (k h) -> p k h", k=2)
                    for r in range(rep):
                        L(v.tensor_copy(Wn[:, :, c + 8 * q:c + 8 * q + 8].rearrange("p k (h r) -> p k h r", r=rep)[:, :, :, r], sc))
                tell("att_used")

            def split_scores(g, es, c):
                H = Hv(c)
                heads = HEADS[g]
                rep = 8 // heads
                rest = small3[:, 0, :, :]
                L(v.tensor_copy(rest, H[:, :, c + 8:c + 16]))
                for q in range(3):
                    L(v.tensor_copy(dS[:, :, q, :], rest))
                    if q < 2:
                        L(tt(rest, rest, dS[:, :, q, :], ALU.subtract))
                parts, w = s_parts(g)
                parts = parts.rearrange("p (k t h) -> p k t h", k=3, h=heads)
                rest = small3[:, 0, 0:es.tiles, 0:heads]
                L(v.tensor_copy(rest, H[:, 0:es.tiles, c:c + 8].rearrange("p t (h r) -> p t h r", r=rep)[:, :, :, 0]))
                for q in range(3):
                    L(v.tensor_copy(parts[:, q, :, :], rest))
                    if q < 2:
                        L(tt(rest, rest, parts[:, q, :, :], ALU.subtract))
                tell("parts_ready")

            def fetch_s(g, es):
                heads, nt = HEADS[g], es.tiles
                rep = 8 // heads
                n0 = rounds_before(g)
                found = s_cols(g) if rep == 1 else R1[:, 5200:5200 + es.Q * heads]
                tiles_of = lambda x: x.unsqueeze(2).to_broadcast((P, 16, nt))
                mask3 = sMask[:, 0:32 * nt].rearrange("p (b u t) -> p b u t", b=2, u=16)
                prod = sProd[:, 0:8 * nt * heads].rearrange("p (u t h) -> p u t h", u=8, t=nt)

                def onehots(r, b):
                    v.wait_ge(S(f"ld_low{b}"), (r - b) * 8 + 16 * (loads_before(g, b) + 1) if isinstance(r, int)
                              else half_of(r, b) * 16 + 16 * (loads_before(g, b) + 1))
                    ts(place[:, b, :], lows[:, b, :], chan[:, :], None, ALU.is_equal).then_inc(S("low_used"), 1)
                    L(tt(mask3[:, b, :, :], iotaB[:, 0:nt].unsqueeze(1).to_broadcast((P, 16, nt)),
                         tiles_of(srcT[es.name][:, at(r * 16, 16)]), ALU.is_equal))

                cur = [None]

                def half_of(r, b):
                    return cur[0] + (1 if b == 0 else 0)

                def take(r, b):
                    for hf in range(2):
                        v.wait_ge(S("s_ps"), r * 2 + (2 * n0 + hf + 1))
                        ps = PS[:, 4 * hf:4 * hf + 4, :].rearrange("p b (a w) -> p (b a) w", a=2)[:, :, 0:nt * heads]
                        tt(prod, ps.rearrange("p u (t h) -> p u t h", h=heads),
                           mask3[:, b, 8 * hf:8 * hf + 8, :].unsqueeze(3).to_broadcast((P, 8, nt, heads)),
                           ALU.mult).then_inc(S("s_free"), 1)
                        v.wait_ge(S("s_free"), r * 2 + (2 * n0 + hf + 3))
                        w = 8 * heads
                        L(v.tensor_reduce(found[:, at(r * 2 * w + hf * w, w)].rearrange("p (u h) -> p u h", u=8),
                                          prod.rearrange("p u t h -> p u h t"), AX, ALU.add))

                onehots(0, 0)

                def body(i):
                    cur[0] = i
                    for b in range(2):
                        onehots(i * 2 + (b + 1), 1 - b)
                        take(i * 2 + b, b)
                L.loop(es.J // 2, 6, body)
                take(es.J - 1, 0)
                v.wait_ge(S("low_used"), n0 + es.J)
                if rep > 1:
                    L(v.tensor_copy(s_cols(g).rearrange("p (q r) -> p q r", r=rep),
                                    found.unsqueeze(2).to_broadcast((P, es.Q * heads, rep))))
                tell("s_ready")

            def scan_max(g, es):
                SA, MA = scan_bufs(g)
                fl = flagA[es.name]
                sm = seam[es.name]
                L(v.tensor_copy(EV(es).rearrange("p (r j) w -> p j r w", j=es.J)[:, :, :, 0:8],
                                s_cols(g).rearrange("p (j r h) -> p j r h", r=16, h=H8)))
                v.wait_ge(S("bank_free"), BASE[f"sA{g}"][0] + BASE[f"sA{g}"][1])
                Ll = es.L

                def seams(n, resets, seam_, end, shift, rev):
                    tell("end_ready")
                    v.wait_ge(S("end_row"), 2 * g + n + 1)
                    T_ = bank(7)[0:1, 0:P].rearrange("p (r h) -> p h r", h=H8)
                    e_, i_ = rowc[0:1, 0, :, :], rowc[0:1, 1, :, :]
                    L(v.memset(e_, NEG))
                    if rev:
                        L(tt(e_[:, :, 0:15], T_[:, :, 1:16], seam_[:, :, 0:15], ALU.add))
                    else:
                        L(tt(e_[:, :, 1:16], T_[:, :, 0:15], seam_[:, :, 1:16], ALU.add))
                    a_, b_, o_ = (q.rearrange("p h r -> p (h r)") for q in (resets, e_, i_))
                    if rev:
                        a_, b_, o_ = a_[:, ::-1], b_[:, ::-1], o_[:, ::-1]
                    L(scan(o_, a_, b_, NEG, ALU.add, ALU.max))
                    L(v.tensor_copy(rowc[0:1, 2, :, :].rearrange("p h r -> p (h r)").rearrange("p (r h) -> p h r", h=H8), i_))
                    tell("carry_row")
                    v.wait_ge(S("carry_ps"), 2 * g + n + 1)
                    L(v.tensor_copy(carry[:, :], bank(7)[:, 256:257]))

                L(scan(MA, fl[:, 0:Ll], SA, NEG, ALU.add, ALU.max))
                L(v.tensor_copy(dcol[:, 0:1], MA[:, Ll - 1:Ll]))
                seams(0, sm[:, 0, :, :], sm[:, 1, :, :], None, 1, False)
                L(scan(MA, fl[:, 0:Ll], SA, carry[:, 0:1], ALU.add, ALU.max))
                bk = fl[:, 1:Ll + 1][:, ::-1]
                L(scan(SA[:, ::-1], bk, MA[:, ::-1], NEG, ALU.add, ALU.max))
                L(v.tensor_copy(dcol[:, 0:1], SA[:, 0:1]))
                seams(1, sm[:, 2, :, :], sm[:, 3, :, :], None, -1, True)
                L(scan(SA[:, ::-1], bk, MA[:, ::-1], carry[:, 0:1], ALU.add, ALU.max))
                tell("max_ready")

            def edges(g, es, c):
                nm = es.name
                R, A_ = rows(g), Av(c)
                gb = groups_before(g)
                sb_ = gb * S2
                fills = sum(e.groups // NBUF for e, _ in GATS[:g])
                base, k = BASE[f"sB{g}"]
                L(v.memset(R1[:, 0:T * (c + 16)], 0.0))
                v.wait_ge(S("bank_free"), base + k)
                tell("rows_free")


                def onehots(n, b):
                    v.wait_ge(S("staged"), n + (gb + 1))
                    tt(drel[:, b % 2, :].rearrange("p (k a) -> p k a", a=2),
                       stage[:, b, :, 16].rearrange("p (k a) -> p k a", a=2),
                       t128[nm][:, at(n * S2, S2)].unsqueeze(2).to_broadcast((P, S2, 2)),
                       ALU.subtract).then_inc(S("rel_done"), 1)
                    v.wait_ge(S("rel_done"), n + (gb + 1))
                    for u in range(G):
                        ins = ts(onehB[:, b % 2, u, :], iotaB[:, :], drel[:, b % 2, u:u + 1], None, ALU.is_equal)
                    ins.then_inc(S("oneh_ready"), 1)

                def group(n, b, more):
                    if more:
                        onehots(n + 1, (b + 1) % NBUF)
                    v.wait_ge(S("d_ready"), n + (gb + 1))
                    v.tensor_reduce(zd[:, :, :], bank(6)[:, 0:3 * G * H8].rearrange("p (u k h) -> p u h k", u=G, k=3),
                                    AX, ALU.add).then_inc(S("z_done"), 1)
                    v.wait_ge(S("z_done"), n * 4 + (4 * gb + 1))
                    tt(zz[:, :, :, :], stage[:, b, :, 0:16].rearrange("p u (k h) -> p u k h", k=2),
                       zd[:, :, :].unsqueeze(2).to_broadcast((P, G, 2, H8)), ALU.add).then_inc(S("z_done"), 1)
                    v.wait_ge(S("z_done"), n * 4 + (4 * gb + 2))
                    stt(out=zz[:, :, :, :], in0=zz[:, :, :, :], scalar=SLOPE, in1=zz[:, :, :, :], op0=ALU.mult,
                        op1=ALU.max).then_inc(S("z_done"), 1)
                    v.wait_ge(S("z_done"), n * 4 + (4 * gb + 3))
                    tt(zd[:, :, :], zz[:, :, 0, :], zz[:, :, 1, :], ALU.subtract).then_inc(S("z_done"), 1)
                    v.wait_ge(S("z_done"), n * 4 + (4 * gb + 4))
                    ts(zd[:, :, :], zd[:, :, :], 0.0, None, ALU.min).then_inc(S("z_ready"), 1)
                    tt(R[:, b, :, c + 8:c + 16], stage[:, b, :, 8:16],
                       stage[:, b, :, 18:19].to_broadcast((P, G, H8)), ALU.mult)
                    if not isinstance(n, int) or n:
                        add_up(n - 1)
                    v.wait_ge(S("w_ready"), n + (gb + 1))
                    for u in range(0, G, 2):
                        r = R[:, b, u:u + 2, 0:c].rearrange("p u (h e) -> p u h e", h=H8)
                        tt(r, r, R[:, b, u:u + 2, c:c + 8].unsqueeze(3).to_broadcast((P, 2, H8, c // 8)),
                           ALU.mult).then_inc(S("scaled"), 1)

                def add_up(n):
                    offs = offsets(mybir.EngineType.DVE, tI[nm], n * S2, S2, (es.tiles - 1) * es.W)
                    for k in range(S2):
                        v.wait_ge(S("summed"), n * S2 + (sb_ + k + 1))
                        v.wait_ge(S("step_done"), n * S2 + (sb_ + k + 4))
                        a = R1[:, bass.ds(offs[k], c + 16)]
                        tt(a, a, bank(k)[:, 0:c + 16], ALU.add).then_inc(S("step_done"), 1)
                    v.wait_ge(S("step_done"), n * S2 + (sb_ + S2 + 4))
                    v.sem_inc(S("group_done"), 1)

                onehots(0, 0)
                group(0, 0, True)
                rounds = (es.groups - 1) // NBUF
                with v.Fori(0, rounds) as i:
                    for j in range(NBUF):
                        group(i * NBUF + (j + 1), (j + 1) % NBUF, True)
                for n in range(1 + rounds * NBUF, es.groups):
                    group(n, n % NBUF, n < es.groups - 1)
                add_up(es.groups - 1)

            def finish(g, es, c):
                H, A_ = Hv(c), Av(c)
                s_, d_ = H[:, :, c:c + 8], H[:, :, c + 8:c + 16]
                den, mx = A_[:, :, c:c + 8], A_[:, :, c + 8:c + 16]
                n3 = [small3[:, q, :, :] for q in range(4)]
                L(ts(n3[0], den, 0.5, NEG, ALU.is_lt, ALU.mult))
                L(tt(mx, mx, n3[0], ALU.add))
                L(tt(mx, mx, d_, ALU.add))
                L(tt(s_, s_, d_, ALU.add))
                lrelu(mx)
                lrelu(s_)
                L(tt(n3[0], mx, s_, ALU.max))
                L(tt(n3[1], mx, n3[0], ALU.subtract))
                L(tt(n3[2], s_, n3[0], ALU.subtract))
                tell("fin_z")
                v.wait_ge(S("fin_e"), g + 1)
                L(tt(den, den, n3[1], ALU.mult))
                L(tt(den, den, n3[2], ALU.add))
                if g != 3:
                    L(ts(den, den, 1e-16, None, ALU.add))
                L(v.reciprocal(n3[0], den))
                L(tt(n3[1], n3[1], n3[0], ALU.mult))
                L(tt(n3[2], n3[2], n3[0], ALU.mult))
                a_ = A_[:, :, 0:c].rearrange("p t (h e) -> p t h e", h=H8)
                h_ = H[:, :, 0:c].rearrange("p t (h e) -> p t h e", h=H8)
                L(tt(a_, a_, n3[1].unsqueeze(3).to_broadcast((P, T, H8, c // 8)), ALU.mult))
                L(tt(h_, h_, n3[2].unsqueeze(3).to_broadcast((P, T, H8, c // 8)), ALU.mult))
                L(tt(A_[:, :, 0:c], A_[:, :, 0:c], H[:, :, 0:c], ALU.add))
                v.wait_ge(S("ld_b"), (32, 48, 80, 96)[g])
                L(tt(A_[:, :, 0:c], A_[:, :, 0:c], brow[:, 2, 0:c].unsqueeze(1).to_broadcast((P, T, c)), ALU.add))

            def fill_records(es):
                L(v.tensor_copy(EV(es)[:, :, 16:19], dsb[es.name][:, :, :].rearrange("p k q -> p q k")))
                tell("records")

            v.wait_ge(S("ld_x"), 32)
            score_weights(0, *GATS[0])
            norm(0, nodes(R2))
            v.wait_ge(S("q_copied"), 1)
            elu1(R4[:, 0:2 * T * P], "q")
            tell("q_ready")
            v.wait_ge(S("kv_copied"), 1)
            elu1(R1[:, 0:T * C], "k")
            L(v.memset(V0[:, :, :, 128:129], 1.0))
            tell("k_ready")
            v.wait_ge(S("ctx_ps"), 1)
            for a in range(2):
                L(v.tensor_copy(dcol[:, a:a + 1], bank(6 + a)[:, 128:129]))
                L(tt(BD[:, a, 0:P], bank(6 + a)[:, 0:P], mask[:, 0:P], ALU.mult))
                L(ts(BD[:, a, P:P + 4], mask[:, P:P + 4], dcol[:, a:a + 1], None, ALU.mult))
            tell("ctx_ready")
            v.wait_ge(S("h_copied"), 1)
            split_scores(0, *GATS[0])

            base, _ = BASE["mixo"]

            def mixo(i):
                for k in range(TB):
                    v.wait_ge(S("bank_full"), i * TB + (k + base - 4))
                    pv = bank(k)[:, 0:264].rearrange("p (a w) -> p a w", a=2)
                    dn = dcol[:, 0:8].rearrange("p (a w) -> p a w", a=2)
                    L(ts(dn, pv[:, :, P:P + 4], 1e-6, None, ALU.max))
                    L(v.reciprocal(dn, dn))
                    L(tt(AO[:, bass.ds(i * TB + k, 1), :].rearrange("p o (a h e) -> p (o a) h e", a=2, h=4),
                         pv[:, :, 0:P].rearrange("p a (h e) -> p a h e", h=4),
                         dn.unsqueeze(3).to_broadcast((P, 2, 4, 32)), ALU.mult))
                    v.sem_inc(S("bank_free"), 1)
            L.loop(T // TB, 3 * TB, mixo)
            v.wait_ge(S("bank_free"), base + T)
            tell("ao_ready")
            consume(v, "proj", lambda t, k: tt(X[:, bass.ds(t, 1), :].rearrange("p a c -> p (a c)"),
                                               X[:, bass.ds(t, 1), :].rearrange("p a c -> p (a c)"),
                                               bank(k)[:, 0:C], ALU.add))
            v.wait_ge(S("ld_b"), 32)
            L(tt(X[:, :, :], X[:, :, :], brow[:, 3, :].unsqueeze(1).to_broadcast((P, T, C)), ALU.add))
            sort_pass(1)
            fill_records(MAIN)
            fetch_s(0, MAIN)
            scan_max(0, MAIN)
            edges(0, *GATS[0])
            finish(0, *GATS[0])
            L(ts(Av(C)[:, :, 0:C], Av(C)[:, :, 0:C], 0.0, None, ALU.max))
            tell("fin_done")
            tell("xn_ready")
            score_weights(1, *GATS[1])
            v.wait_ge(S("h_copied"), 2)
            split_scores(1, *GATS[1])
            consts_of(FFN, 1)
            fill_records(MAIN)
            fetch_s(1, MAIN)
            scan_max(1, MAIN)
            edges(1, *GATS[1])
            finish(1, *GATS[1])
            L(tt(X[:, :, :], X[:, :, :], Av(C)[:, :, 0:C], ALU.add))
            tell("fin_done")

            norm(1, nodes(R2))
            score_weights(2, *GATS[2])
            v.wait_ge(S("h_copied"), 3)
            split_scores(2, *GATS[2])
            fill_records(FFN)
            fetch_s(2, FFN)
            scan_max(2, FFN)
            edges(2, *GATS[2])
            finish(2, *GATS[2])
            O16 = Av(16)[:, :, 0:16]
            m1, m2 = rowsum[:, 0:T], rowsum[:, T:2 * T]
            L(v.tensor_reduce(m1, O16, AX, ALU.add))
            L(ts(m1, m1, 1.0 / 16, None, ALU.mult))
            L(tt(O16, O16, m1.unsqueeze(2).to_broadcast((P, T, 16)), ALU.subtract))
            sq = small4[:, 0:T * 16].rearrange("p (t c) -> p t c", t=T)
            L(tt(sq, O16, O16, ALU.mult))
            L(v.tensor_reduce(m2, sq, AX, ALU.add))
            L(ts(rstd[:, :], m2, 1.0 / 16, None, ALU.mult))
            tell("rvar_ready")
            v.wait_ge(S("rstd_ready"), 1)
            L(v.reciprocal(rstd[:, :], rstd[:, :]))
            L(tt(O16, O16, rstd[:, :].unsqueeze(2).to_broadcast((P, T, 16)), ALU.mult))
            v.wait_ge(S("ld_b2"), 16)
            L(tt(O16, O16, brow[:, 3, 0:16].unsqueeze(1).to_broadcast((P, T, 16)), ALU.mult))
            L(tt(O16, O16, brow[:, 0, 0:16].unsqueeze(1).to_broadcast((P, T, 16)), ALU.add))
            sc = small4[:, 400:400 + 4 * T].rearrange("p (t e) -> p t e", t=T)
            L(v.tensor_reduce(sc, O16.rearrange("p t (h e) -> p t e h", h=4), AX, ALU.add))
            L(ts(sc, sc, 0.25, None, ALU.mult))
            cmp4 = small4[:, 0:T * 4].rearrange("p (t e) -> p t e", t=T)
            rk = small4[:, 100:100 + T * 4].rearrange("p (t e) -> p t e", t=T)
            L(v.memset(rk, 0.0))
            for j in range(EXP0):
                sj = sc[:, :, j:j + 1].to_broadcast((P, T, EXP0))
                L(tt(cmp4, sj, sc, ALU.is_gt))
                L(tt(rk, rk, cmp4, ALU.add))
                if j < EXP0 - 1:
                    w = EXP0 - 1 - j
                    L(tt(cmp4[:, :, 0:w], sc[:, :, j:j + 1].to_broadcast((P, T, w)), sc[:, :, j + 1:EXP0], ALU.is_equal))
                    L(tt(rk[:, :, j + 1:EXP0], rk[:, :, j + 1:EXP0], cmp4[:, :, 0:w], ALU.add))
            L(v.tensor_reduce(m1, sc, AX, ALU.max))
            L(tt(gates[:, :, :], sc, m1.unsqueeze(2).to_broadcast((P, T, EXP0)), ALU.subtract))
            tell("gate_z")
            v.wait_ge(S("gate_e"), 1)
            L(stt(out=gates[:, :, :], in0=rk, scalar=1.5, in1=gates[:, :, :], op0=ALU.is_lt, op1=ALU.mult))
            L(v.tensor_reduce(m1, gates[:, :, :], AX, ALU.add))
            L(v.reciprocal(m1, m1))
            L(tt(gates[:, :, :], gates[:, :, :], m1.unsqueeze(2).to_broadcast((P, T, EXP0)), ALU.mult))
            tell("fin_done")
            v.wait_ge(S("ld_moe"), 64)
            nE = EXP0 * TB
            with v.Fori(0, T // TB) as i:
                for e in range(EXP0):
                    for k in range(TB):
                        o = e * TB + k
                        if e:
                            v.wait_ge(S("moe_free"), i * nE + (o - TB + 1 + 4))
                        x = X[:, bass.ds(i * TB + k, 1), :].rearrange("p a c -> p (a c)")
                        stt(out=x, in0=b2e[:, e * C:(e + 1) * C],
                            scalar=gates[:, bass.ds(i * TB + k, 1), e:e + 1].rearrange("p a c -> p (a c)"),
                            in1=x, op0=ALU.mult, op1=ALU.add).then_inc(S("bias_done"), 1)
                        v.wait_ge(S("bias_done"), i * nE + (o + 1))
                        v.wait_ge(S("moe_full"), i * nE + (o + 1 + 2 * TB))
                        stt(out=x, in0=bank(o % 4)[:, 0:C],
                            scalar=gates[:, bass.ds(i * TB + k, 1), e:e + 1].rearrange("p a c -> p (a c)"),
                            in1=x, op0=ALU.mult, op1=ALU.add).then_inc(S("moe_free"), 1)
            v.wait_ge(S("moe_free"), 4 + nE * (T // TB))
            tell("moe0_done")

            XN = nodes(R2)
            norm(2, XN)
            L(stt(out=X[:, :, :], in0=XN, scalar=2.0, in1=X[:, :, :], op0=ALU.mult, op1=ALU.add))
            g3 = lambda r: r[:, 0:T * C].rearrange("p (q e) -> p q e", e=32)
            mean, std = rowsum[:, 0:200], small4[:, 0:200]
            L(v.tensor_reduce(mean, g3(R2), AX, ALU.add))
            L(ts(mean, mean, 1.0 / 32, None, ALU.mult))
            L(tt(g3(R1), g3(R2), mean.unsqueeze(2).to_broadcast((P, 200, 32)), ALU.subtract))
            L(tt(g3(R4), g3(R1), g3(R1), ALU.mult))
            L(v.tensor_reduce(std, g3(R4), AX, ALU.add))
            tell("hvar_ready")
            v.wait_ge(S("hstd_ready"), 1)
            L(ts(std, std, 1e-5, None, ALU.add))
            L(v.reciprocal(std, std))
            L(tt(g3(R1), g3(R1), std.unsqueeze(2).to_broadcast((P, 200, 32)), ALU.mult))
            v.wait_ge(S("ld_mix1"), 64)
            bc = lambda q: brow[:, q, :].unsqueeze(1).to_broadcast((P, T, C))
            L(tt(V1, K1, bc(2), ALU.mult))
            L(tt(V1, V1, bc(3), ALU.add))
            L(tt(K1, K1, bc(0), ALU.mult))
            L(tt(K1, K1, bc(1), ALU.add))
            tell("mix1_kv")
            v.wait_ge(S("ctx_ps"), 2)
            for a in range(2):
                L(stt(out=BD[:, a, 0:P], in0=bank(6 + a)[:, 0:P], scalar=1.0 / N, in1=mask[:, 0:P], op0=ALU.mult,
                      op1=ALU.mult))
            tell("ctx_ready")
            score_weights(3, *GATS[3])
            consume(v, "mix1o", lambda t, k: tt(X[:, bass.ds(t, 1), :].rearrange("p a c -> p (a c)"),
                                                X[:, bass.ds(t, 1), :].rearrange("p a c -> p (a c)"),
                                                bank(k)[:, 0:C], ALU.add))
            v.wait_ge(S("h_copied"), 4)
            split_scores(3, *GATS[3])
            fill_records(MAIN)
            fetch_s(3, MAIN)
            scan_max(3, MAIN)
            edges(3, *GATS[3])
            finish(3, *GATS[3])
            out3 = Av(C)[:, :, 0:C]
            meanS, varS = R2[:, 0:C], R2[:, C:2 * C]
            tell("bn_in")
            base, _ = BASE["bnm"]
            v.wait_ge(S("bank_full"), base - 4)
            ts(meanS, bank(0)[:, 0:C], 1.0 / N, None, ALU.mult).then_inc(S("bank_free"), 1)
            v.wait_ge(S("bank_free"), base + 1)
            L(tt(out3, out3, meanS.unsqueeze(1).to_broadcast((P, T, C)), ALU.subtract))
            L(tt(nodes(R4), out3, out3, ALU.mult))
            tell("bn_in")
            v.wait_ge(S("bank_full"), base - 3)
            ts(varS, bank(0)[:, 0:C], 1.0 / N, None, ALU.mult).then_inc(S("bank_free"), 1)
            v.wait_ge(S("bank_free"), base + 2)
            tell("bn_var")
            v.wait_ge(S("bn_std"), 1)
            L(v.reciprocal(varS, varS))
            v.wait_ge(S("ld_b2"), 48)
            L(tt(varS, varS, brow[:, 0, :], ALU.mult))
            L(tt(out3, out3, varS.unsqueeze(1).to_broadcast((P, T, C)), ALU.mult))
            L(tt(out3, out3, bc(1), ALU.add))
            L(tt(X[:, :, :], X[:, :, :], out3, ALU.add))
            tell("fin_done")
            tell("bn_done")

            norm(3, nodes(R1))
            v.wait_ge(S("ld_rb"), 16)
            base, _ = BASE["rt"]
            lg = R1[:, 0:T * 32].rearrange("p (t e) -> p t e", t=T)
            eq = R1[:, 1000:1000 + T * 32].rearrange("p (t e) -> p t e", t=T)
            v.wait_ge(S("xt_used"), 1)
            consume(v, "rt", lambda t, k: tt(lg[:, bass.ds(t, 1), :].rearrange("p a e -> p (a e)"), bank(k)[:, 0:32],
                                             brow[:, 0, 0:32], ALU.add))
            mx = rowsum[:, 0:T]
            L(v.tensor_reduce(mx, lg, AX, ALU.max))
            L(tt(eq, lg, mx.unsqueeze(2).to_broadcast((P, T, 32)), ALU.is_equal))
            rev = small4[:, 0:32]
            L(ts(rev, iota[:, 0:32], -1.0, 32.0, ALU.mult, ALU.add))
            L(tt(eq, eq, rev.unsqueeze(1).to_broadcast((P, T, 32)), ALU.mult))
            L(v.tensor_reduce(mx, eq, AX, ALU.max))
            L(tt(lg, eq, mx.unsqueeze(2).to_broadcast((P, T, 32)), ALU.is_equal))
            L(v.memset(zrow, 0.0))
            L(ts(experts, ones[0:32, :], chan[0:32, :], None, ALU.mult))
            half = dcol[:, 0:1]
            L(ts(half, chan[:, :], 64.0, None, ALU.is_ge))
            L(ts(expertOf, iota[:, 0:16], 2.0, half, ALU.mult, ALU.add))
            tell("choice")
            consume(v, "ohT", lambda t, k: v.tensor_copy(ohE[:, bass.ds(t * P, P)], bank(k)[0:32, 0:P]))
            tell("ohT_ready")
            v.wait_ge(S("chosen"), 1)

            def out_block(i):
                L(v.tensor_copy(ohS, ohE[:, bass.ds(i * TOK, TOK)]))
                v.sem_inc(S("block_choice"), 1)
                for j in range(16):
                    for hf in range(2):
                        n = 2 * j + hf
                        v.wait_ge(S("relu_done"), i * 32 + (n + 5))
                        if hf == 0:
                            v.wait_ge(S("w2_done"), i * 16 + (j + 1))
                        stt(out=hm[:, j % 2, hf * 320:(hf + 1) * 320],
                            in0=chosenB[:, bass.ds(i * TOK + hf * 320, 320)],
                            scalar=expertOf[:, j:j + 1], in1=ha[:, hf, :], op0=ALU.is_equal,
                            op1=ALU.mult).then_inc(S("pair_done"), 1)
                v.wait_ge(S("out_full"), i + 1)
                for b in range(3):
                    w = 2 if b < 2 else 1
                    x = X[:, bass.ds(i * TB + 2 * b, w), :].rearrange("p a c -> p (a c)")
                    L(stt(out=x, in0=bank(b)[:, 0:w * C], scalar=0.0, in1=x, op0=ALU.max, op1=ALU.add))
                v.sem_inc(S("out_free"), 1)
            L.loop(T // TB, 4, out_block)
            tell("moe1_done")

        @block.scalar
        def _(s):
            L = Chain(s, "act_chain")
            act = s.activation

            def copy(out_, in_):
                return act(out_, in_, ACT.Copy)

            def tell(name, k=1):
                s.sem_inc(S(name), k)

            def to_xt(g):
                consume(s, f"xT{g}", lambda t, k: copy(XT[:, :, bass.ds(t * P, P)],
                                                       bank(k)[:, 0:2 * P].rearrange("p (a n) -> p a n", a=2)))
                tell("xt_ready")

            def std(src, dst, bias):
                L(act(dst, src, ACT.Sqrt, bias=bias))

            def gat(g, es, c):
                E = EV(es)
                nm = es.name
                s.wait_ge(S("records"), g + 1)
                for b in range(EARLY):
                    offs = offsets(mybir.EngineType.Activation, cI[nm], b * S2, S2, (es.Q - 2) * EW)
                    for k in range(S2):
                        L(copy(idx[:, b, 2 * k:2 * k + 2],
                               R4[:, bass.ds(offs[k], 2 * EW)].rearrange("p (u w) -> p u w", u=2)[:, :, 17]))
                tell("first_idx")
                SA, _ = scan_bufs(g)

                def down(t, k):
                    w = min(4, es.J - 4 * t) * P
                    return copy(SA[:, 4 * t * P:4 * t * P + w], bank(k)[:, 0:w])
                consume(s, f"sA{g}", down)
                Er = E.rearrange("p (r j) w -> p j r w", j=es.J)

                def up(t, k):
                    w = min(4, es.J - 4 * t)
                    for q in range(w):
                        ins = copy(Er[:, 4 * t + q, :, 8:16], bank(k)[:, q * P:(q + 1) * P].rearrange("p (r h) -> p r h", h=H8))
                    return ins
                consume(s, f"sB{g}", up)

                gb = groups_before(g)
                R = rows(g)

                def stage_in(n, b):
                    s.wait_ge(S("group_done"), n + (gb + 1))
                    offs = offsets(mybir.EngineType.Activation, cI[nm], n * S2, S2, (es.Q - 2) * EW)
                    for k in range(S2):
                        ins = copy(stage[:, b, 2 * k:2 * k + 2, :].rearrange("p u w -> p (u w)"),
                                   R4[:, bass.ds(offs[k], 2 * EW)])
                    ins.then_inc(S("rec_done"), 1)
                    s.wait_ge(S("rec_done"), n + (gb + 1))
                    if isinstance(n, int) and n < EARLY:
                        tell("staged")
                    else:
                        copy(idx[:, b, :], stage[:, b, :, 17]).then_inc(S("staged"), 1)

                def turned(n, b):
                    s.wait_ge(S("turned_ps"), n + (gb + 1))
                    copy(onehT[:, :, :], bank(4).bitcast(BF16).rearrange("p (u e) -> p u e", u=G)).then_inc(S("turned"), 1)
                    if gb or not isinstance(n, int) or n > 1:
                        s.wait_ge(S("group_done"), n + (gb + NBUF - 1))
                    copy(oneh[:, b % 2, :, :], onehB[:, b % 2, :, :]).then_inc(S("oneh_copied"), 1)

                def group(n, b, more, more3):
                    s.wait_ge(S("z_ready"), n + (gb + 1))
                    k = n // NBUF if isinstance(n, int) else None
                    gathered(n, b, k)
                    act(R[:, b, :, c:c + 8], zd[:, :, :], ACT.Exp).then_inc(S("w_ready"), 1)
                    if more:
                        turned(n + 1, b + 1)
                    if more3:
                        stage_in(n + AHEAD, (b + AHEAD) % NBUF)

                fills = sum(e.groups // NBUF for e, _ in GATS[:g])

                def gathered(n, b, k):
                    q = k if k is not None else cur[0]
                    s.wait_ge(S(f"gat{b}"), q * P + (P * fills + P))

                cur = [None]
                last = es.groups // NBUF - 1
                for b in range(AHEAD):
                    stage_in(b, b)
                turned(0, 0)
                with s.Fori(0, last) as i:
                    cur[0] = i
                    for b in range(NBUF):
                        group(i * NBUF + b, b, True, True)
                for b in range(NBUF):
                    group(last * NBUF + b, b, b < NBUF - 1, b + AHEAD < NBUF)
                s.wait_ge(S("fin_z"), g + 1)
                L(act(small3[:, 1:3, :, :], small3[:, 1:3, :, :], ACT.Exp))
                tell("fin_e")

            def to_h(g, c):
                consume(s, f"h{g}", lambda t, k: copy(Hv(c)[:, bass.ds(t, 1), :].rearrange("p a c -> p (a c)"),
                                                      bank(k)[:, 0:c + 16]))
                tell("h_copied")

            def node_std(k):
                s.wait_ge(S("var_ready"), k + 1)
                std(mv[:, :, 1], rstd[:, :], epsc[:, 0:1])
                tell("std_ready")

            consume(s, "wT", lambda t, k: copy(wT[:, :, t, :], bank(k)[:, 0:2 * P].rearrange("p (a n) -> p a n", a=2)))
            tell("wT_ready")
            node_std(0)
            to_xt(0)
            consume(s, "q", lambda t, k: copy(qT[:, t // 10, (t % 10) * 320:(t % 10 + 1) * 320], bank(k)[:, 0:320]))
            tell("q_copied")

            def kv(t, k):
                copy(K0[:, bass.ds(t, 1), :].rearrange("p a c -> p (a c)"), bank(k)[:, 0:C])
                return copy(V0[:, bass.ds(t, 1), :, 0:P].rearrange("p o a w -> p (o a) w"),
                            bank(k)[:, C:2 * C].rearrange("p (a w) -> p a w", a=2))
            for q in range(4):
                s.wait_ge(S("elu_min"), q + 1)
                L(act(eluT[:, 0:1600], eluT[:, 0:1600], ACT.Exp))
                tell("elu_exp")
            consume(s, "kv", kv)
            tell("kv_copied")
            for q in range(4, 8):
                s.wait_ge(S("elu_min"), q + 1)
                L(act(eluT[:, 0:1600], eluT[:, 0:1600], ACT.Exp))
                tell("elu_exp")
            to_h(0, C)
            s.wait_ge(S("ao_ready"), 1)
            consume(s, "aT", lambda t, k: copy(XT[:, :, bass.ds(t * P, P)],
                                               bank(k)[:, 0:2 * P].rearrange("p (a n) -> p a n", a=2)))
            tell("aT_ready")
            gat(0, *GATS[0])
            to_xt(1)
            to_h(1, C)
            gat(1, *GATS[1])
            node_std(1)
            to_xt(2)
            to_h(2, 16)
            gat(2, *GATS[2])
            s.wait_ge(S("rvar_ready"), 1)
            std(rstd[:, :], rstd[:, :], epsc[:, 0:1])
            tell("rstd_ready")
            s.wait_ge(S("gate_z"), 1)
            L(act(gates[:, :, :], gates[:, :, :], ACT.Exp))
            tell("gate_e")
            s.wait_ge(S("b1_ps"), 1)
            L(copy(b1T[:, :], bank(7)[:, 0:16]))
            tell("b1_ready")
            with s.Fori(0, T // TB) as i:
                for e in range(EXP0):
                    s.wait_ge(S("moe_full"), i * (EXP0 * TB) + (e + 1) * TB)
                    for f in range(4):
                        for hf in range(2):
                            m = (e * 4 + f) * 2 + hf
                            s.wait_ge(S("hid_full"), i * 32 + (m + 1))
                            col = e * 4 + f
                            act(hh[:, e % 2, f, hf * 320:(hf + 1) * 320], bank(4 + m % 4)[:, 0:320], ACT.Gelu,
                                bias=b1T[:, col:col + 1]).then_inc(S("hid_free"), 1)
            node_std(2)
            s.wait_ge(S("hvar_ready"), 1)
            L(act(small4[:, 0:200], small4[:, 0:200], ACT.Sqrt, scale=1.0 / 31))
            tell("hstd_ready")
            to_xt(3)
            to_h(3, C)
            gat(3, *GATS[3])
            s.wait_ge(S("bn_var"), 1)
            std(R2[:, C:2 * C], R2[:, C:2 * C], epsc[:, 0:1])
            tell("bn_std")
            node_std(3)
            s.wait_ge(S("b1_ps"), 2)
            L(copy(b1T[:, :], bank(7)[:, 0:16]))
            L(copy(rwT[:, :, :], bank(7)[:, 64:128].rearrange("p (k e) -> p k e", k=2)))
            tell("b1_ready")
            to_xt(4)
            tell("xt_used")
            consume(s, "chosen", lambda t, k: copy(chosenB[:, t * 320:(t + 1) * 320], bank(k)[:, 0:320]))
            tell("chosen")
            tell("relu_done", 4)
            with s.Fori(0, T // TB) as i:
                for j in range(16):
                    for hf in range(2):
                        n = 2 * j + hf
                        s.wait_ge(S("pair_full"), i * 32 + (n + 1))
                        s.wait_ge(S("pair_done"), i * 32 + (n + 1))
                        act(ha[:, hf, :], bank(3 + n % 4)[:, 0:320], ACT.Relu,
                            bias=b1T[:, j:j + 1]).then_inc(S("relu_done"), 1)

        @block.tensor
        def _(pe):
            mm = pe.matmul

            def turn(out_, in_, k=P):
                return pe.transpose(out_, in_, ident[0:k, 0:k])

            pe.wait_ge(S("consts"), 1)
            def sort_offsets(p):
                B = DIGITS[p][1]
                pe.wait_ge(S("counts_ready"), p + 1)
                mm(bank(7)[:, 0:B], ltri, sCnt[:, 0:B], start=True, stop=False)
                mm(bank(7)[:, 0:B], offd, sGex[:, 0:B], start=False, stop=True).then_inc(S("offsets"), 1)
            sort_offsets(0)

            def prepare(es, k):
                nb, a, b, c, d = prepv(es)
                pe.wait_ge(S("prep_rows"), k + 1)

                def chunk_cols(t, kk):
                    w = min(P, es.Q - (t % nb) * P)
                    src = (a, c, b)[t // nb]
                    return turn(bank(kk)[:, 0:w], src[0:w, t % nb, :], w)
                fill(pe, "prep_" + es.name, chunk_cols)
                pe.wait_ge(S("prep_scan"), k + 1)
                for q, col in enumerate((0, es.L - 1)):
                    ins = mm(bank(7)[0:1, q * P:(q + 1) * P], dA[:, col:col + 1], ident[:, :], start=True, stop=True)
                ins.then_inc(S("ends_ps"), 1)
                pe.wait_ge(S("sel0_ready"), k + 1)
                n = es.tiles - 1
                mm(bank(6)[0:n, 0:es.Q], sel0[:, 0:n], dsb[es.name][:, 0, :], start=True, stop=True).then_inc(S("firsts_ps"), 1)
                pe.wait_ge(S("leave_ready"), k + 1)
                mm(bank(5)[:, 0:es.steps], ones[0:n, :], cmpT[0:n, 0:es.steps], start=True, stop=True).then_inc(S("tiles_ps"), 1)

            prepare(MAIN, 0)

            pe.wait_ge(S("ld_wraw"), 48)

            def w_turn(t, kk):
                for k in range(2):
                    ins = turn(bank(kk)[:, k * P:(k + 1) * P], wraw[:, t, k * P:(k + 1) * P])
                return ins
            fill(pe, "wT", w_turn)

            def x_turn(name, src):
                def one(t, kk):
                    for k in range(2):
                        ins = turn(bank(kk)[:, k * P:(k + 1) * P],
                                   src[:, t, k * P:(k + 1) * P])
                    return ins
                fill(pe, name, one)

            def product(name, rhs, n):
                def one(t, kk):
                    for k in range(2):
                        ins = mm(bank(kk)[:, 0:n], XT[:, k, t * P:(t + 1) * P], rhs(k), start=(k == 0), stop=(k == 1))
                    return ins
                fill(pe, name, one)

            def gat(g, es, c):
                pe.wait_ge(S("parts_ready"), g + 1)
                parts, w = s_parts(g)
                n0 = rounds_before(g)

                def find(r, b):
                    pe.wait_ge(S("low_used"), r + (n0 + 1))
                    for hf in range(2):
                        pe.wait_ge(S("s_free"), r * 2 + (2 * n0 + hf + 1))
                        for u in range(8):
                            for k in range(3):
                                ins = mm(bank(4 * hf + u // 2)[:, (u % 2) * 256:(u % 2) * 256 + w],
                                         place[:, b, (8 * hf + u) * P:(8 * hf + u + 1) * P], parts[:, k * w:(k + 1) * w],
                                         start=(k == 0), stop=(k == 2))
                        ins.then_inc(S("s_ps"), 1)
                with pe.Fori(0, es.J // 2) as i:
                    for b in range(2):
                        find(i * 2 + b, b)
                find(es.J - 1, 0)
                pe.wait_ge(S("s_ready"), g + 1)
                SA, MA = scan_bufs(g)

                def down(t, kk):
                    for q in range(min(4, es.J - 4 * t)):
                        ins = turn(bank(kk)[:, q * P:(q + 1) * P], s_cols(g)[:, (4 * t + q) * P:(4 * t + q + 1) * P])
                    return ins
                fill(pe, f"sA{g}", down)
                for n in range(2):
                    pe.wait_ge(S("end_ready"), 2 * g + n + 1)
                    mm(bank(7)[0:1, 0:P], dcol[:, 0:1], ident[:, :], start=True, stop=True).then_inc(S("end_row"), 1)
                    pe.wait_ge(S("carry_row"), 2 * g + n + 1)
                    mm(bank(7)[:, 256:257], rowc[0:1, 2, :, :].rearrange("p h r -> p (h r)"), ones[0:1, 0:1],
                       start=True, stop=True).then_inc(S("carry_ps"), 1)
                pe.wait_ge(S("max_ready"), g + 1)

                def up(t, kk):
                    for q in range(min(4, es.J - 4 * t)):
                        j = 4 * t + q
                        ins = turn(bank(kk)[:, q * P:(q + 1) * P], SA[:, j * P:(j + 1) * P])
                    return ins
                fill(pe, f"sB{g}", up)
                base, k = BASE[f"sB{g}"]
                pe.wait_ge(S("bank_free"), base + k)

                nm, H, R = es.name, Hv(c), rows(g)
                gb = groups_before(g)
                sb_ = gb * S2

                def turns(n, b):
                    pe.wait_ge(S("oneh_ready"), n + (gb + 1))
                    pe.wait_ge(S("turned"), n + gb) if gb or not isinstance(n, int) or n else None
                    for u in range(G):
                        ins = pe.transpose(bank(4).bitcast(BF16)[:, u * P:(u + 1) * P], onehB[:, b % 2, u, :], identB[:, :])
                    ins.then_inc(S("turned_ps"), 1)

                def fetch(n):
                    pe.wait_ge(S("turned"), n + (gb + 1))
                    if gb or not isinstance(n, int) or n:
                        pe.wait_ge(S("z_ready"), n + gb)
                    offs = offsets(mybir.EngineType.PE, tP[nm], n * S2, S2, (es.tiles - 1) * 3 * H8)
                    dcols = dS[:, :, :, :].rearrange("p t k h -> p (t k h)")
                    for u in range(G):
                        ins = mm(bank(6)[:, u * 24:(u + 1) * 24], onehT[:, u, :], dcols[:, bass.ds(offs[u // 2], 24)],
                                 start=True, stop=True)
                    ins.then_inc(S("d_ready"), 1)

                def group(n, b, more):
                    if more:
                        turns(n + 1, b + 1)
                    pe.wait_ge(S("oneh_copied"), n + (gb + 1))
                    for k in range(S2):
                        if k == S2 // 2 and more:
                            fetch(n + 1)
                        pe.wait_ge(S("scaled"), n * S2 + (sb_ + k + 1))
                        pe.wait_ge(S("step_done"), n * S2 + (sb_ + k + 1))
                        for u in (2 * k, 2 * k + 1):
                            ins = mm(bank(k)[:, 0:c + 16], oneh[:, b % 2, u, :], R[:, b, u, 0:c + 16],
                                     start=(u % 2 == 0), stop=(u % 2 == 1))
                        ins.then_inc(S("summed"), 1)

                last = es.groups // NBUF - 1
                turns(0, 0)
                fetch(0)
                with pe.Fori(0, last) as i:
                    for b in range(NBUF):
                        group(i * NBUF + b, b, True)
                for b in range(NBUF):
                    group(last * NBUF + b, b, b < NBUF - 1)

            pe.wait_ge(S("xn_ready"), 1)
            x_turn("xT0", nodes(R2))
            pe.wait_ge(S("wT_ready"), 1)
            pe.wait_ge(S("xt_ready"), 1)

            def q_rows(t, kk):
                for k in range(2):
                    ins = mm(bank(kk)[:, 0:320], wT[:, k, t // 10, :], XT[:, k, (t % 10) * 320:(t % 10 + 1) * 320],
                             start=(k == 0), stop=(k == 1))
                return ins
            fill(pe, "q", q_rows)
            product("kv", lambda k: wT[:, k, 2:6, :].rearrange("p o m -> p (o m)"), 512)

            def context(Kv, rhs):
                for a in range(2):
                    for t in range(T):
                        kk = P if t < T - 1 else TAIL
                        r = rhs(a, t, kk)
                        ins = mm(bank(6 + a)[:, 0:r.shape[-1]], Kv[0:kk, t, a * P:(a + 1) * P], r,
                                 start=(t == 0), stop=(t == T - 1))
                ins.then_inc(S("ctx_ps"), 1)

            pe.wait_ge(S("k_ready"), 1)
            context(K0, lambda a, t, kk: V0[0:kk, t, a, :])
            pe.wait_ge(S("ctx_ready"), 1)
            pe.wait_ge(S("att_used"), 1)
            product("h0", lambda k: Wn[:, k, :], C + 16)

            def mixo(t, kk):
                for a in range(2):
                    ins = mm(bank(kk)[:, a * 132:(a + 1) * 132], qT[:, a, t * P:(t + 1) * P], BD[:, a, :],
                             start=True, stop=True)
                return ins
            fill(pe, "mixo", mixo)
            pe.wait_ge(S("ao_ready"), 1)
            x_turn("aT", AO)
            pe.wait_ge(S("aT_ready"), 1)
            product("proj", lambda k: wT[:, k, 6:8, :].rearrange("p o m -> p (o m)"), C)
            sort_offsets(1)
            gat(0, *GATS[0])
            pe.wait_ge(S("xn_ready"), 2)
            x_turn("xT1", Av(C)[:, :, 0:C])
            pe.wait_ge(S("att_used"), 2)
            pe.wait_ge(S("xt_ready"), 2)
            product("h1", lambda k: Wn[:, k, :], C + 16)
            prepare(FFN, 1)
            gat(1, *GATS[1])
            pe.wait_ge(S("xn_ready"), 3)
            x_turn("xT2", nodes(R2))
            pe.wait_ge(S("att_used"), 3)
            pe.wait_ge(S("xt_ready"), 3)
            product("h2", lambda k: Wn[:, k, 0:32], 32)
            gat(2, *GATS[2])

            pe.wait_ge(S("ld_moe"), 64)
            turn(bank(7)[:, 0:16], b1e, 16).then_inc(S("b1_ps"), 1)
            pe.wait_ge(S("b1_ready"), 1)
            pe.wait_ge(S("fin_done"), 3)
            pe.sem_inc(S("hid_free"), 4)
            pe.sem_inc(S("moe_full"), 2 * TB)

            with pe.Fori(0, T // TB) as i:
                def up_proj(e):
                    for f in range(4):
                        for hf in range(2):
                            m = (e * 4 + f) * 2 + hf
                            pe.wait_ge(S("hid_free"), i * 32 + (m + 1))
                            for k in range(2):
                                ins = mm(bank(4 + m % 4)[:, 0:320], W1e[:, e, k, f * P:(f + 1) * P],
                                         XT[:, k, bass.ds(i * TOK + hf * 320, 320)], start=(k == 0), stop=(k == 1))
                            ins.then_inc(S("hid_full"), 1)

                def down_proj(e):
                    pe.wait_ge(S("hid_free"), i * 32 + (4 + 8 * (e + 1)))
                    for k in range(TB):
                        o = e * TB + k
                        pe.wait_ge(S("moe_free"), i * (EXP0 * TB) + (o + 1))
                        for f in range(4):
                            ins = mm(bank(o % 4)[:, 0:C], hh[:, e % 2, f, k * P:(k + 1) * P], W2e[:, e, f, :],
                                     start=(f == 0), stop=(f == 3))
                        ins.then_inc(S("moe_full"), 1)

                up_proj(0)
                for e in range(EXP0):
                    if e < EXP0 - 1:
                        up_proj(e + 1)
                    down_proj(e)

            pe.wait_ge(S("xn_ready"), 4)
            pe.wait_ge(S("moe0_done"), 1)
            x_turn("xT3", nodes(R2))
            pe.wait_ge(S("mix1_kv"), 1)
            context(K1, lambda a, t, kk: V1[0:kk, t, a * P:(a + 1) * P])
            pe.wait_ge(S("ctx_ready"), 2)
            pe.wait_ge(S("xt_ready"), 4)

            def mix1o(t, kk):
                for a in range(2):
                    ins = mm(bank(kk)[:, a * P:(a + 1) * P], XT[:, a, t * P:(t + 1) * P], BD[:, a, 0:P],
                             start=True, stop=True)
                return ins
            fill(pe, "mix1o", mix1o)
            pe.wait_ge(S("att_used"), 4)
            product("h3", lambda k: Wn[:, k, :], C + 16)
            gat(3, *GATS[3])

            for n, src in enumerate((Av(C), nodes(R4))):
                pe.wait_ge(S("bn_in"), n + 1)
                for t in range(T):
                    kk = P if t < T - 1 else TAIL
                    ins = mm(bank(0)[:, 0:C], ones[0:kk, :], src[0:kk, t, 0:C], start=(t == 0), stop=(t == T - 1))
                ins.then_inc(S("bank_full"), 1)

            pe.wait_ge(S("ld_moe1"), 16 * 6)
            turn(bank(7)[:, 0:16], b1r, 16)
            for k in range(2):
                ins = turn(bank(7)[:, 64 + 32 * k:96 + 32 * k], rwr[:, k * P:(k + 1) * P], 32)
            ins.then_inc(S("b1_ps"), 1)
            pe.wait_ge(S("xn_ready"), 5)
            x_turn("xT4", nodes(R1))
            pe.wait_ge(S("xt_ready"), 5)
            pe.wait_ge(S("b1_ready"), 2)
            product("rt", lambda k: rwT[:, k, :], 32)
            pe.wait_ge(S("choice"), 1)
            chosen = R1[:, 0:T * 32].rearrange("p (t e) -> p t e", t=T)
            fill(pe, "ohT", lambda t, kk: turn(bank(kk)[0:32, 0:P], chosen[:, t, :]))
            pe.wait_ge(S("ohT_ready"), 1)
            fill(pe, "chosen", lambda t, kk: mm(bank(kk)[:, 0:320], experts, ohE[:, t * 320:(t + 1) * 320],
                                                start=True, stop=True))
            pe.wait_ge(S("chosen"), 1)
            pe.sem_inc(S("w2_done"), 2)
            pe.sem_inc(S("out_free"), 1)
            with pe.Fori(0, T // TB) as i:
                def up_pair(j):
                    for hf in range(2):
                        n = 2 * j + hf
                        pe.wait_ge(S("relu_done"), i * 32 + (n + 1))
                        cols = bass.ds(i * TOK + hf * 320, 320)
                        for k in range(2):
                            ins = mm(bank(3 + n % 4)[:, 0:320], W1x[:, k, j * P:(j + 1) * P], XT[:, k, cols],
                                     start=(k == 0), stop=(k == 1))
                        ins.then_inc(S("pair_full"), 1)

                def out_of(k):
                    return bank(k // 2)[:, (k % 2) * C:(k % 2 + 1) * C]

                def down_pair(j):
                    pe.wait_ge(S("pair_done"), i * 32 + (2 + 2 * (j + 1)))
                    for k in range(TB):
                        ins = mm(out_of(k), hm[:, j % 2, k * P:(k + 1) * P], W2r[:, j, :], start=False, stop=False,
                                 skip_group_check=True)
                    ins.then_inc(S("w2_done"), 1)

                up_pair(0)
                pe.wait_ge(S("out_free"), i + 1)
                for b in range(3):
                    mm(bank(b)[:, 0:512], zrow[0:1, 0:P], zrow[0:1, :], start=True, stop=False, skip_group_check=True)
                pe.wait_ge(S("block_choice"), i + 1)
                for k in range(TB):
                    mm(out_of(k), ohS[:, k * P:(k + 1) * P], b2r, start=False, stop=False, skip_group_check=True)
                for j in range(16):
                    if j < 15:
                        up_pair(j + 1)
                    down_pair(j)
                for b in range(3):
                    ins = mm(bank(b)[:, 0:512], zrow[0:1, 0:P], zrow[0:1, :], start=False, stop=True, skip_group_check=True)
                ins.then_inc(S("out_full"), 1)


_OUTS = [((N, C), "float32")]
_INS = ['x', 'src', 'dst', 'L0_gnn_W1', 'L0_gnn_att_src1', 'L0_gnn_att_dst1', 'L0_gnn_b1', 'L0_gnn_W2',
        'L0_gnn_att_src2', 'L0_gnn_att_dst2', 'L0_gnn_b2', 'L0_mix_Wq', 'L0_mix_Wkv', 'L0_mix_Wproj',
        'L0_mix_bproj', 'L0_ffn_W_gat', 'L0_ffn_att_src', 'L0_ffn_att_dst', 'L0_ffn_b_gat', 'L0_ffn_ln_gamma',
        'L0_ffn_ln_beta', 'L0_ffn_W1', 'L0_ffn_b1', 'L0_ffn_W2', 'L0_ffn_b2', 'L0_ffn_edge_index', 'L1_gnn_W',
        'L1_gnn_att_src', 'L1_gnn_att_dst', 'L1_gnn_bias', 'L1_gnn_gamma', 'L1_gnn_beta', 'L1_mix_kln_weight',
        'L1_mix_kln_bias', 'L1_mix_vln_weight', 'L1_mix_vln_bias', 'L1_ffn_router_w', 'L1_ffn_router_b',
        'L1_ffn_W1', 'L1_ffn_b1', 'L1_ffn_W2', 'L1_ffn_b2']


def kernel(**inputs):
    import concourse.bacc as _bacc
    from concourse.bass_utils import run_bass_kernel_spmd as _run

    nc = _bacc.Bacc("TRN2", target_bir_lowering=False, num_devices=1)
    arrays, aps = {}, {}
    for name in _INS:
        a = np.ascontiguousarray(inputs[name])
        arrays[f"in_{name}"] = a
        aps[name] = nc.dram_tensor(f"in_{name}", a.shape, mybir.dt.from_np(a.dtype), kind="ExternalInput").ap()
    res = nc.dram_tensor("out_0", (N, C), F32, kind="ExternalOutput").ap()
    build(nc, aps, res)
    r = _run(nc, [arrays], core_ids=[0])
    return r.results[0]["out_0"]
```

```python
from contextlib import ExitStack

import concourse.bass as bass
import numpy as np
from concourse import mybir
from concourse.alu_op_type import AluOpType as ALU

F32 = mybir.dt.float32
BF16 = mybir.dt.bfloat16
I32 = mybir.dt.int32
ACT = mybir.ActivationFunctionType
AX = mybir.AxisListType.X

P = 128
N = 3125
T = -(-N // P)
TAIL = N - (T - 1) * P
C = 256
H8 = 8
NEG = -1.0e30
SLOPE = 0.2
IDX = 4096
PADV = (IDX - 1) * IDX
G = 8
S2 = G // 2
EARLY = 2
AHEAD = 3
NBUF = 4
EW = 19
FFN_NODES = 16 * 128
EXP0, F0 = 4, 512
EXP1, F1 = 32, 64
SLOTS = (N + EXP1 * (P - 1)) // P
SB, TURN = 4, 8
assert SLOTS % TURN == 0
TB = 5
TOK = TB * P


class EdgeSet:

    def __init__(self, name, edges, tiles, j, c):
        self.name, self.edges, self.tiles, self.J = name, edges, tiles, j
        self.W = c + 16
        self.fold = 2 if tiles > 16 else 1
        self.sections = -(-tiles // self.fold)
        self.Q = 16 * j
        self.groups = -(-(-(-edges // (2 * P)) + tiles - 1) // S2)
        self.turns = -(-self.groups // NBUF) - 1
        self.steps = self.groups * S2
        assert self.Q * P >= edges + 2 * P
        self.L = j * P


MAIN = EdgeSet("m", 50000, T, 25, 256)
FFN = EdgeSet("f", 32768, FFN_NODES // P, 17, 16)
GATS = [(MAIN, 256), (MAIN, 256), (FFN, 16), (MAIN, 256)]
HEADS = (8, 1, 4, 8)

PASSES = [("prep_m", 12), ("wT", 8)]


def _passes():
    out = list(PASSES)
    for g, (es, c) in enumerate(GATS):
        out.append((f"xT{g}", T))
        if g == 0:
            out += [("q", 2 * TB * 2), ("kv", T), ]
        out.append((f"h{g}", T))
        if g == 0:
            out += [("mixo", T), ("aT", T), ("proj", T)]
        if g == 3:
            out += [("mix1o", T)]
        if g == 1:
            out += [("prep_f", 9)]
        out += [(f"sA{g}", -(-es.J // 4)), (f"sB{g}", -(-es.J // 4))]
    out += [("bnm", 1), ("bnv", 1), ("xT4", T), ("rt", T)]
    base, at = {}, 5
    for n, k in out:
        base[n] = (at, k)
        at += k
    return base


BASE = _passes()


def rounds_before(g):
    return sum(es.J for es, _ in GATS[:g])


def loads_before(g, b):
    return sum((es.J + 1 - b) // 2 for es, _ in GATS[:g])


def groups_before(g):
    return sum(es.groups for es, _ in GATS[:g])


def build(nc, A, out):
    ctx = ExitStack()
    with ctx:
        def sb(name, shape, dt=F32):
            return ctx.enter_context(nc.sbuf_tensor(name, shape, dt))

        def dram(name, shape, dt=F32):
            return nc.dram_tensor(name, shape, dt, kind="Internal").ap()

        sems = {}

        def S(name):
            if name not in sems:
                sems[name] = ctx.enter_context(nc.semaphore(name))
            return sems[name]

        arena = sb("arena", [P, 29904])
        R1 = arena[:, 0:6800]
        R2 = arena[:, 6800:13600]
        R4 = arena[:, 13600:21200]
        R3 = arena[:, 21200:29904]
        X = sb("X", [P, T, C])
        oneh = sb("oneh", [P, 2, G, P])
        onehB = sb("onehB", [P, 2, G, P], BF16)
        onehT = sb("onehT", [P, G, P], BF16)
        identB = sb("identB", [P, P], BF16)
        iotaB = sb("iotaB", [P, P], BF16)
        dS = sb("dS", [P, T, 3, H8], BF16)
        ident = sb("ident", [P, P])
        ones = sb("ones", [P, P])
        iota = sb("iota", [P, MAIN.Q])
        stage = sb("stage", [P, NBUF, G, EW])
        idx = sb("idx", [P, NBUF, G], I32)
        sProd = R1[:, 3200:4864]
        sMask = R1[:, 4864:5120].bitcast(BF16)
        idx_s = sb("idx_s", [P, 2, G], I32)
        dat_s = sb("dat_s", [P, 2, G], I32)
        padT = sb("padT", [P, 16], I32)
        zz = sb("zz", [P, G, 2, H8])
        zd = sb("zd", [P, G, H8])
        drel = sb("drel", [P, 2, G])
        Wn = sb("Wn", [P, 2, C + 16])
        brow = sb("brow", [P, 4, C])
        dsb = {e.name: sb("dsb_" + e.name, [P, 3, e.Q]) for e in (MAIN, FFN)}
        srcT = {e.name: sb("srcT_" + e.name, [P, e.Q], BF16) for e in (MAIN, FFN)}
        flagA = {e.name: sb("flagA_" + e.name, [P, e.L + 1], BF16) for e in (MAIN, FFN)}
        seam = {e.name: sb("seam_" + e.name, [1, 4, H8, 16]) for e in (MAIN, FFN)}
        t128 = {e.name: sb("t128_" + e.name, [P, e.steps]) for e in (MAIN, FFN)}
        steps = {e.name: sb("steps_" + e.name, [65, e.steps], I32) for e in (MAIN, FFN)}
        tI, tP, cI = ({k: v[32 * q:32 * q + 1, :] for k, v in steps.items()} for q in range(3))
        rowc = sb("rowc", [1, 3, H8, 16])
        chan = sb("chan", [P, 1])
        chan2 = sb("chan2", [P, 1])
        rowsum = sb("rowsum", [P, 200])
        small3 = oneh[:, :, :, :].rearrange("p a b c -> p (a b c)")[:, 0:4 * T * H8].rearrange(
            "p (q t h) -> p q t h", q=4, t=T)
        zeros = R4[:, 7168:7168 + C]
        small4 = onehT[:, :, :].rearrange("p a b -> p (a b)").bitcast(F32)
        carry = sb("carry", [P, 1])
        mv = sb("mv", [P, T, 2])
        st6 = sb("st6", [P, TB, 6])
        rstd = sb("rstd", [P, T])
        epsc = sb("epsc", [P, 1])
        BD = sb("BD", [P, 2, 132])
        mask = sb("mask", [P, 132])
        b1T = sb("b1T", [P, 16])
        rwT = sb("rwT", [P, 2, EXP1])
        gates = sb("gates", [P, T, EXP0])
        dcol = sb("dcol", [P, 8])
        PS = ctx.enter_context(nc.psum_tensor("PS", [P, 8, 512], F32))

        def Hv(c):
            return R2[:, 0:T * (c + 16)].rearrange("p (t w) -> p t w", t=T)

        def Av(c):
            return R1[:, 0:T * (c + 16)].rearrange("p (t w) -> p t w", t=T)

        def nodes(region):
            return region[:, 0:T * C].rearrange("p (t c) -> p t c", t=T)

        XT = R3[:, 0:2 * T * P].rearrange("p (k n) -> p k n", k=2)

        def EV(es):
            return R4[:, 0:es.Q * EW].rearrange("p (q w) -> p q w", w=EW)

        def rows(g):
            w = GATS[g][1] + 16
            return (R2[:, 1000:1000 + NBUF * G * w] if g == 2 else R3[:, 0:NBUF * G * w]).rearrange("p (b u w) -> p b u w", b=NBUF, u=G)

        def scan_bufs(g):
            L = GATS[g][0].L
            return (R1[:, 1000:1000 + L], R1[:, 3200:3200 + L]) if g == 2 else (R3[:, 5504:5504 + L], R1[:, 3200:3200 + L])

        lows = R3[:, 6400:8448].bitcast(BF16).rearrange("p (b e) -> p b e", b=2)
        place = [q.bitcast(BF16).rearrange("p (b e) -> p b e", b=2) for q in
                 (oneh[:, :, :, :].rearrange("p a b c -> p (a b c)"), R3[:, 4352:6400])]

        def s_parts(g):
            w = GATS[g][0].sections * HEADS[g]
            return onehT[:, :, :].rearrange("p a b -> p (a b)")[:, 0:3 * GATS[g][0].fold * w], w

        def s_cols(g):
            L = GATS[g][0].L
            return R4[:, 5200:5200 + L] if g == 2 else R1[:, 0:L]

        pk = {e.name: dram("pk_" + e.name, (e.Q * P + P,), I32) for e in (MAIN, FFN)}
        srt1 = dram("srt1", (FFN.edges, 1), I32)
        srt2 = dram("srt2", (FFN.edges, 1), I32)
        tab = [dram(f"tab{g}", (T * P, c + 8)) for g, (_, c) in enumerate(GATS)]
        lowQ = {e.name: dram("lowQ_" + e.name, (e.Q * P,), BF16) for e in (MAIN, FFN)}
        low = {e.name: dram("low_" + e.name, (e.Q * P,), BF16) for e in (MAIN, FFN)}

        SC = FFN.edges // P
        DIGITS = ((12, 64), (18, 32))
        sortO = (R3.bitcast(BF16), R4.bitcast(BF16))
        sortH = (arena[:, 0:64 * SC], R3)
        keep = (R4[:, 6400:7600], Wn[:, :, :].rearrange("p k c -> p (k c)"))
        srtV, srtI = ([k[:, q * SC:(q + 1) * SC].bitcast(I32) for k in keep] for q in range(2))
        ltri, offd = R4[:, 6912:7040], R4[:, 7040:7168]
        rest = R4[:, 4096:6400]
        srtT = rest[:, 0:SC].bitcast(I32)
        srtD = rest[:, SC:2 * SC]
        srtP = rest[:, 2 * SC:3 * SC]
        sGl, sCnt, sGex, sXo = (rest[:, 3 * SC + 64 * q:3 * SC + 64 * (q + 1)] for q in range(4))
        pkS = R3[0:125, 0:400].bitcast(I32)
        pkD = R3[0:125, 400:800].bitcast(I32)

        def prepv(es):
            nb = -(-es.Q // P)
            return [nb] + [R1[:, k * 512:k * 512 + nb * P].rearrange("p (b i) -> p b i", b=nb) for k in range(4)]

        sel0 = R1[:, 2048:2048 + 128]
        cmpT = R1[:, 2304:2304 + MAIN.Q]
        small = R1[:, 3000:3032]
        lowI = R1[:, 4300:4812].bitcast(I32)
        lowB = R1[:, 4812:5068].bitcast(BF16)
        tileI = R1[:, 5100:5500].bitcast(I32)
        tS = R1[:, 3200:3200 + 2 * MAIN.steps]
        pkA = R3[:, 0:3200]
        dA = R3[:, 3200:6400]
        fA = R4[:, 0:3200]

        wraw = R1[:, 0:2048].rearrange("p (o c) -> p o c", o=8)
        wT = R3[:, 6400:8448].rearrange("p (k o m) -> p k o m", k=2, o=8)
        qT = R4[:, 0:2 * T * P].rearrange("p (k n) -> p k n", k=2)
        K0 = nodes(R1)
        V0 = R2[:, 0:T * 258].rearrange("p (t a w) -> p t a w", t=T, a=2)
        AO = nodes(R1)
        eluT = oneh[:, :, :, :].rearrange("p a b c -> p (a b c)")
        K1, V1 = nodes(R1), nodes(R4)
        def att_row(g, q):
            late = oneh[:, :, :, :].rearrange("p a b c -> p (a b c)")[:, 1024:1536]
            return (brow[:, q, :] if g < 3 else late[:, q * C:(q + 1) * C])[:, 0:GATS[g][1]]

        W1e = R4[:, 0:4096].rearrange("p (e k f) -> p e k f", e=EXP0, k=2)
        W2e = R2[:, 0:4096].rearrange("p (e k f) -> p e k f", e=EXP0, k=4)
        hh = R1[:, 0:2 * 4 * TOK].rearrange("p (b f n) -> p b f n", b=2, f=4)
        b1e = R2[0:16, 4096:4224]
        b2e = R2[:, 4300:4300 + EXP0 * C]
        W2x = arena[0:65, 6800:6800 + EXP1 * C]
        W1x = arena[:, 15000:19096].rearrange("p (k m) -> p k m", k=2)
        lg = arena[:, 19100:19900].rearrange("p (t e) -> p t e", t=T)
        eq = arena[:, 19900:20700].rearrange("p (t e) -> p t e", t=T)
        b1r = arena[0:32, 20700:20764]
        rwr = arena[0:32, 20800:21056]
        b1c = R3[0:64, 6500:6532]
        before = R3[:, 0:(T + 1) * EXP1].rearrange("p (t e) -> p t e", e=EXP1)
        bins = R3[:, 1000:1000 + SLOTS * EXP1].rearrange("p (q e) -> p q e", e=EXP1)
        lower = R3[:, 3000:3128]
        used, upto, first = (R3[:, 3200 + 32 * q:3232 + 32 * q] for q in range(3))
        ints = onehT[:, :, :].rearrange("p a b -> p (a b)").bitcast(I32)
        slotI, w1_at, w2_at = ints[:, 0:T], ints[0:1, 32:32 + SLOTS], ints[0:1, 96:96 + SLOTS]
        xs = R3[:, 0:2048].rearrange("p (b k c) -> p b k c", b=2, k=SB)
        ys = R3[:, 2048:4096].rearrange("p (b k c) -> p b k c", b=2, k=SB)
        xsT = R3[:, 4096:4608].rearrange("p (b k n) -> p b k n", b=2, k=2)
        w1s = R3[:, 4608:4864].rearrange("p (b k f) -> p b k f", b=2, k=2)
        hs = R3[0:65, 4864:5120].rearrange("p (b n) -> p b n", b=2)
        xs_dram = dram("xs", (SLOTS * P, C))
        ys_dram = dram("ys", (SLOTS * P, C))

        block = ctx.enter_context(nc.Block())

        def offsets(engine, table, step, n, last):
            return nc.values_load_multi_w_load_instructions(
                table[:, at(step, n)], engines=(engine,), min_val=0, max_val=last, bass_reorder=False,
                skip_runtime_bounds_check_because="the tables are clamped when they are built")[1]

        def at(start, n):
            return slice(start, start + n) if isinstance(start, int) else bass.ds(start, n)

        def bank(b):
            return PS[:, b, :]

        class Chain:

            def __init__(self, eng, name):
                self.eng, self.sem, self.n, self.i, self.k0 = eng, S(name), 0, None, 0

            def value(self):
                return self.n if self.i is None else self.i * self.K + self.n

            def __call__(self, ins):
                ins.then_inc(self.sem, 1)
                self.n += 1
                self.eng.wait_ge(self.sem, self.value())

            def loop(self, count, per, body, first=0):
                self.n -= first * per
                n0 = self.n
                with self.eng.Fori(first, count) as i:
                    self.i, self.K = i, per
                    body(i)
                    assert self.n - n0 == per, (self.n - n0, per)
                    self.i = None
                self.n = n0 + per * count

        def consume(eng, name, fn):
            base, n = BASE[name]
            if n == T:
                with eng.Fori(0, T // TB) as i:
                    for k in range(TB):
                        t = i * TB + k
                        eng.wait_ge(S("bank_full"), t + (base - 4))
                        fn(t, k).then_inc(S("bank_free"), 1)
            else:
                for t in range(n):
                    eng.wait_ge(S("bank_full"), t + base - 4)
                    fn(t, t % TB).then_inc(S("bank_free"), 1)
            eng.wait_ge(S("bank_free"), base + n)

        def fill(eng, name, fn):
            base, n = BASE[name]
            eng.wait_ge(S("bank_free"), base)
            for t in range(n):
                if t >= TB:
                    eng.wait_ge(S("bank_free"), t + base - 4)
                fn(t, t % TB).then_inc(S("bank_full"), 1)

        @block.sync
        def _(sp):
            def load(dst, src, name):
                sp.dma_start(dst, src).then_inc(S(name), 16)

            load(pkS, A["src"].rearrange("(p c) -> p c", p=125), "ld_edges")
            load(pkD, A["dst"].rearrange("(p c) -> p c", p=125), "ld_edges")
            load(srtT, A["L0_ffn_edge_index"][0].rearrange("(p c) -> p c", p=P), "ld_fedges")
            load(srtV[0], A["L0_ffn_edge_index"][1].rearrange("(p c) -> p c", p=P), "ld_fedges")
            sp.wait_ge(S("x_cleared"), 1)
            load(X[:, 0:T - 1, :], A["x"][0:(T - 1) * P, :].rearrange("(t p) c -> p t c", p=P), "ld_x")
            load(X[0:TAIL, T - 1, :], A["x"][(T - 1) * P:N, :], "ld_x")
            sp.wait_ge(S("packed"), 1)
            sp.dma_start(pk["m"][0:50000].rearrange("(p c) -> p c", p=125), pkS).then_inc(S("pkm_st"), 16)
            for e in (MAIN, FFN):
                n = e.Q * P + P - e.edges
                w = n // 16
                assert n % 16 == 0 and w <= P or e is FFN
                for o in range(0, w, P):
                    k = min(P, w - o)
                    sp.dma_start(pk[e.name][e.edges + 16 * o:e.edges + 16 * (o + k)].rearrange("(p c) -> p c", c=16),
                                 padT[0:k, 0:16]).then_inc(S("pk_st"), 16)
            def load_prep(es, k):
                nb, a, b, _, _ = prepv(es)
                name = "ld_prep"
                for dst, off in ((a, 0), (b, 1)):
                    v = pk[es.name][off:off + es.Q * P].rearrange("(q i) -> q i", i=P)
                    load(dst[:, 0:nb - 1, :].bitcast(I32), v[0:(nb - 1) * P].rearrange("(b p) i -> p b i", p=P), name)
                    load(dst[0:16, nb - 1, :].bitcast(I32), v[(nb - 1) * P:es.Q], name)
                rws = pk[es.name][0:es.Q * P].rearrange("(r x) -> r x", r=16)
                load(pkA[:, 0:es.L].bitcast(I32), rws.unsqueeze(1).to_broadcast((16, H8, es.L)), name)

            def store_low(es, k):
                nb = prepv(es)[0]
                v = lowQ[es.name].rearrange("(q i) -> q i", i=P)
                low3 = lowB[:, 0:nb * P].rearrange("p (b i) -> p b i", b=nb)
                sp.wait_ge(S("low_ready"), k + 1)
                sp.dma_start(v[0:(nb - 1) * P].rearrange("(b p) i -> p b i", p=P), low3[:, 0:nb - 1, :]).then_inc(S("low_st"), 16)
                sp.dma_start(v[(nb - 1) * P:es.Q], low3[0:16, nb - 1, :]).then_inc(S("low_st"), 16)
                sp.wait_ge(S("low_st"), 32 * (k + 1))
                sp.dma_start(low[es.name].rearrange("(j r i) -> j r i", r=16, i=P),
                             lowQ[es.name].rearrange("(r j i) -> j r i", r=16, i=P)).then_inc(S("low_order"), 16)

            def load_lows(g, es):
                n0 = rounds_before(g)

                def one(r, b, first):
                    if not first:
                        sp.wait_ge(S("low_used"), r + (n0 - 1))
                    sp.dma_start(lows[:, b, :], low[es.name][at(r * 2048, 2048)].unsqueeze(0).to_broadcast((P, 2048))
                                 ).then_inc(S(f"ld_low{b}"), 16)
                sp.wait_ge(S("records"), g + 1)
                sp.wait_ge(S("low_order"), 32 if g else 16)
                one(0, 0, True)
                one(1, 1, True)
                with sp.Fori(1, es.J // 2) as i:
                    for b in range(2):
                        one(i * 2 + b, b, False)
                one(es.J - 1, 0, False)

            sp.wait_ge(S("pk_st"), 48)
            sp.wait_ge(S("pkm_st"), 16)
            sp.wait_ge(S("rank_ready"), 1)
            load_prep(MAIN, 0)
            store_low(MAIN, 0)
            sp.wait_ge(S("prep_done"), 1)
            for i, (w, n) in enumerate((("L0_mix_Wq", 2), ("L0_mix_Wkv", 4), ("L0_mix_Wproj", 2))):
                o = (0, 2, 6)[i]
                load(wraw[:, o:o + n, :], A[w].rearrange("(o p) c -> p o c", p=P), "ld_wraw")

            def row(i, name, sem):
                v = A[name]
                if len(v.shape) == 2:
                    v = v.rearrange("a b -> (a b)")
                if len(v.shape) == 3:
                    v = v.rearrange("a b c -> (a b c)")
                n = v.shape[0]
                load(brow[:, i, 0:n], v.unsqueeze(0).to_broadcast((P, n)), sem)

            wnames = [("L0_gnn_W1", "L0_gnn_att_src1", "L0_gnn_att_dst1"),
                      ("L0_gnn_W2", "L0_gnn_att_src2", "L0_gnn_att_dst2"),
                      ("L0_ffn_W_gat", "L0_ffn_att_src", "L0_ffn_att_dst"),
                      ("L1_gnn_W", "L1_gnn_att_src", "L1_gnn_att_dst")]
            for g, (es, c) in enumerate(GATS):
                if g:
                    sp.wait_ge(S("fin_done"), g)
                if g == 3:
                    row(0, "L1_mix_kln_weight", "ld_mix1")
                    row(1, "L1_mix_kln_bias", "ld_mix1")
                    row(2, "L1_mix_vln_weight", "ld_mix1")
                    row(3, "L1_mix_vln_bias", "ld_mix1")
                load(Wn[:, :, 0:c], A[wnames[g][0]].rearrange("(k p) c -> p k c", p=P), "ld_gw")
                for q in range(2):
                    load(att_row(g, q), A[wnames[g][q + 1]].rearrange("a b c -> (a b c)" if len(A[wnames[g][q + 1]].shape) == 3 else "a b -> (a b)").unsqueeze(0).to_broadcast((P, c)), "ld_gw")
                if g == 3:
                    sp.wait_ge(S("mix1_kv"), 1)
                if g == 0:
                    row(2, "L0_gnn_b1", "ld_b")
                    row(3, "L0_mix_bproj", "ld_b")
                    sp.dma_start(xs_dram.rearrange("(q p) c -> p q c", p=P),
                                 zeros[:, :].unsqueeze(1).to_broadcast((P, SLOTS, C))).then_inc(S("xs_clear"), 16)
                if g == 1:
                    row(2, "L0_gnn_b2", "ld_b")
                if g == 2:
                    row(2, "L0_ffn_b_gat", "ld_b")
                    row(3, "L0_ffn_ln_gamma", "ld_b")
                if g == 3:
                    row(2, "L1_gnn_bias", "ld_b")
                sp.wait_ge(S("h_copied"), g + 1)
                sp.dma_start(tab[g].rearrange("(t p) w -> p t w", p=P), Hv(c)[:, :, 0:c + 8]).then_inc(S("tab_st"), 16)
                if g == 0:
                    for b in range(2):
                        sp.wait_ge(S(f"scat{b}"), 8 * SC)
                    sp.wait_ge(S("sort_room"), 1)
                    load(srtV[1], srt1.rearrange("(p c) w -> p (c w)", p=P), "ld_sort1")
                if g == 1:
                    load_prep(FFN, 1)
                    store_low(FFN, 1)
                load_lows(g, es)
                if g == 0:
                    for b in range(2):
                        sp.wait_ge(S(f"scat{b}"), 16 * SC)
                    sp.dma_start(pk["f"][0:FFN.edges].rearrange("(p c) -> p c", p=P),
                                 srt2.rearrange("(p c) w -> p (c w)", p=P)).then_inc(S("pk_st"), 16)
                    sp.wait_ge(S("pk_st"), 64)
                if g == 2:
                    sp.wait_ge(S("att_used"), 3)
                    row(0, "L0_ffn_ln_beta", "ld_b2")
                    sp.wait_ge(S("fin_done"), 3)
                    load(W1e[:, :, :, :].rearrange("p e k f -> p (e k) f"), A["L0_ffn_W1"].rearrange("e (k p) f -> p (e k) f", p=P), "ld_moe")
                    load(W2e[:, :, :, :].rearrange("p e k f -> p (e k) f"), A["L0_ffn_W2"].rearrange("e (k p) f -> p (e k) f", p=P), "ld_moe")
                    load(b1e, A["L0_ffn_b1"].rearrange("e (k p) -> (e k) p", p=P), "ld_moe")
                    load(b2e, A["L0_ffn_b2"].rearrange("e c -> (e c)").unsqueeze(0).to_broadcast((P, EXP0 * C)), "ld_moe")
                if g == 3:
                    sp.wait_ge(S("att_used"), 4)
                    row(0, "L1_gnn_gamma", "ld_b2")
                    row(1, "L1_gnn_beta", "ld_b2")
            sp.wait_ge(S("fin_done"), 4)
            for k in range(2):
                load(W1x[:, k, :].rearrange("p (e f) -> p e f", e=EXP1),
                     A["L1_ffn_W1"][:, k * P:(k + 1) * P, :].rearrange("e p f -> p e f"), "ld_moe1")
            load(W2x[0:64, :].rearrange("f (e c) -> f e c", e=EXP1), A["L1_ffn_W2"].rearrange("e f c -> f e c"), "ld_moe1")
            load(W2x[64:65, :], A["L1_ffn_b2"].rearrange("e c -> (e c)").unsqueeze(0), "ld_moe1")
            load(b1r, A["L1_ffn_b1"], "ld_moe1")
            load(rwr, A["L1_ffn_router_w"], "ld_moe1")
            sp.wait_ge(S("bn_done"), 1)
            row(0, "L1_ffn_router_b", "ld_rb")
            xv = xs_dram.rearrange("(m k p) c -> m p k c", k=SB, p=P)
            yv = ys_dram.rearrange("(m k p) c -> m p k c", k=SB, p=P)

            def tiles_at(v, m):
                return (v[m] if isinstance(m, int) else v[bass.ds(m, 1)].rearrange("m p k c -> (m p) k c"))
            sp.sem_inc(S("ys_st0"), 16)
            sp.sem_inc(S("ys_st1"), 16)
            sp.wait_ge(S("xs_st"), 16 * T)
            sp.wait_ge(S("owners_ready"), 1)
            for b in range(2):
                sp.dma_start(xs[:, b, :, :], tiles_at(xv, b)).then_inc(S(f"ld_xs{b}"), 16)
            last = SLOTS // TURN - 1
            with sp.Fori(0, last) as i:
                for b in range(2):
                    sp.wait_ge(S("xs_ps"), i * TURN + SB * (b + 1))
                    sp.dma_start(xs[:, b, :, :], tiles_at(xv, i * 2 + (b + 2))).then_inc(S(f"ld_xs{b}"), 16)
                    sp.wait_ge(S("ys_copied"), i * TURN + (SB * (b + 1) + 2))
                    sp.dma_start(tiles_at(yv, i * 2 + b), ys[:, b, :, :]).then_inc(S(f"ys_st{b}"), 16)
            for b in range(2):
                sp.wait_ge(S("ys_copied"), last * TURN + SB * (b + 1) + 2)
                sp.dma_start(tiles_at(yv, last * 2 + b), ys[:, b, :, :]).then_inc(S(f"ys_st{b}"), 16)
            for b in range(T // TB):
                sp.wait_ge(S("out_done"), b + 1)
                t0, t1 = b * TB, min((b + 1) * TB, T - 1)
                sp.dma_start(out[t0 * P:t1 * P, :].rearrange("(t p) c -> p t c", p=P), X[:, t0:t1, :]).then_inc(S("st_out"), 16)
            sp.dma_start(out[(T - 1) * P:N, :], X[0:TAIL, T - 1, :]).then_inc(S("st_out"), 16)
            sp.wait_ge(S("st_out"), 16 * (T // TB + 1))


        @block.gpsimd
        def _(pool):
            L = Chain(pool, "pool_chain")
            L(pool.memset(ident[:, :], 0.0))
            L(pool.affine_select(out=ident[:, :], in_=ident[:, :], compare_op=ALU.not_equal, fill=1.0,
                                 base=0, pattern=[[-1, P]], channel_multiplier=1))
            L(pool.tensor_copy(identB[:, :], ident[:, :]))
            L(pool.memset(ones[:, :], 1.0))
            L(pool.affine_select(out=ltri, in_=ones[:, :], compare_op=ALU.is_gt, fill=0.0,
                                 base=0, pattern=[[1, P]], channel_multiplier=-1))
            L(pool.affine_select(out=offd, in_=ones[:, :], compare_op=ALU.not_equal, fill=0.0,
                                 base=0, pattern=[[-1, P]], channel_multiplier=1))
            L(pool.iota(iota[:, :], [[1, MAIN.Q]], base=0, channel_multiplier=0,
                        allow_small_or_imprecise_dtypes=True))
            L(pool.tensor_copy(iotaB[:, :], iota[:, 0:P]))
            L(pool.iota(chan[:, :], [[0, 1]], base=0, channel_multiplier=1, allow_small_or_imprecise_dtypes=True))
            L(pool.memset(mask[:, :], 1.0))
            for v, pat, neg in ((mask[:, 0:P].rearrange("p (h e) -> p h e", h=4), [[-32, 4], [0, 32]], [[32, 4], [0, 32]]),
                                (mask[:, P:P + 4], [[-32, 4]], [[32, 4]])):
                L(pool.affine_select(out=v, in_=v, compare_op=ALU.is_ge, fill=0.0, base=0,
                                     pattern=pat, channel_multiplier=1))
                L(pool.affine_select(out=v, in_=v, compare_op=ALU.is_gt, fill=0.0, base=32,
                                     pattern=neg, channel_multiplier=-1))
            pool.sem_inc(S("consts"), 1)

            for p in range(2):
                pool.wait_ge(S("rank_ready"), p + 1)
                dst = (srt1, srt2)[p]

                def body(i, p=p, dst=dst):
                    for b in range(2):
                        if not isinstance(i, int) or p:
                            pool.wait_ge(S(f"scat{b}"), i * P + p * 8 * SC)
                        L(pool.tensor_copy(idx_s[:, b, :], srtI[p][:, at(i * 16 + 8 * b, 8)]))
                        L(pool.tensor_copy(dat_s[:, b, :], srtV[p][:, at(i * 16 + 8 * b, 8)]))
                        pool.sem_inc(S("pool_turn"), 1)
                        for u in range(G):
                            pool.indirect_dma_start(
                                out=dst, out_offset=bass.IndirectOffsetOnAxis(ap=idx_s[:, b, u:u + 1], axis=0),
                                in_=dat_s[:, b, u:u + 1], in_offset=None).then_inc(S(f"scat{b}"), 16)
                body(0)
                L.loop(SC // 16, 4, body, first=1)

            for g, (es, c) in enumerate(GATS):
                sp_rows = rows(g)
                pool.wait_ge(S("tab_st"), 16 * (g + 1))
                def gather(b, g=g, c=c, sp_rows=sp_rows):
                    pool.sem_inc(S("pool_turn"), 1)
                    for u in range(G):
                        pool.indirect_dma_start(
                            out=sp_rows[:, b, u, 0:c + 8], out_offset=None, in_=tab[g],
                            in_offset=bass.IndirectOffsetOnAxis(ap=idx[:, b, u:u + 1], axis=0),
                        ).then_inc(S(f"gat{b}"), 16)
                for b in range(NBUF):
                    if b == 0:
                        pool.wait_ge(S("first_idx"), g + 1)
                    if b == EARLY:
                        pool.wait_ge(S("rows_free"), g + 1)
                    if b >= EARLY:
                        pool.wait_ge(S("staged"), b + 1 + groups_before(g))
                    gather(b)
                with pool.Fori(1, es.turns) as i:
                    for b in range(NBUF):
                        pool.wait_ge(S("staged"), i * NBUF + (b + 1 + groups_before(g)))
                        gather(b)
                for n in range(es.turns * NBUF, es.groups):
                    pool.wait_ge(S("staged"), n + 1 + groups_before(g))
                    gather(n % NBUF)

            XN = nodes(R1)
            pool.wait_ge(S("slots_ready"), 1)
            pool.sem_inc(S("pool_turn"), 1)
            for t in range(T):
                k = P if t < T - 1 else TAIL
                pool.indirect_dma_start(
                    out=xs_dram, out_offset=bass.IndirectOffsetOnAxis(ap=slotI[0:k, t:t + 1], axis=0),
                    in_=XN[0:k, t, :], in_offset=None).then_inc(S("xs_st"), 16)
            for b in range(2):
                pool.wait_ge(S(f"ys_st{b}"), 16 * (SLOTS // TURN + 1))
            pool.sem_inc(S("pool_turn"), 1)
            for t in range(T):
                k = P if t < T - 1 else TAIL
                pool.indirect_dma_start(
                    out=XN[0:k, t, :], out_offset=None, in_=ys_dram,
                    in_offset=bass.IndirectOffsetOnAxis(ap=slotI[0:k, t:t + 1], axis=0),
                ).then_inc(S(f"ys_got{t // TB}"), 16)

        @block.vector
        def _(v):
            L = Chain(v, "dve_chain")
            tt, ts, stt = v.tensor_tensor, v.tensor_scalar, v.scalar_tensor_tensor

            def tell(name, k=1):
                v.sem_inc(S(name), k)

            def scan(out_, d0, d1, init, o0, o1):
                return v.tensor_tensor_scan(out_, d0, d1, init, o0, o1)

            tell("bank_free", TB)
            tell("step_done", 4)
            tell("group_done", NBUF)
            tell("moe_free", 4)
            tell("pair_done", 2)
            tell("s_free", 2)
            L(v.memset(X[:, T - 1, :], 0.0))
            L(v.memset(zeros, 0.0))
            tell("x_cleared")
            v.wait_ge(S("consts"), 1)
            L(ts(chan2[:, :], chan[:, :], float(P), None, ALU.add))
            L(v.memset(padT[:, :], PADV))
            L(v.memset(epsc[:, :], 1e-5))
            v.wait_ge(S("ld_edges"), 32)
            L(ts(pkD, pkD, 12, None, ALU.logical_shift_left))
            L(tt(pkS, pkS, pkD, ALU.bitwise_or))
            tell("packed")
            v.wait_ge(S("ld_fedges"), 32)
            L(ts(srtV[0], srtV[0], 12, None, ALU.logical_shift_left))
            L(tt(srtV[0], srtV[0], srtT, ALU.bitwise_or))

            def sort_pass(p):
                sh, B = DIGITS[p]
                if p:
                    tell("sort_room")
                    v.wait_ge(S("ld_sort1"), 16)
                V, I, O_, H_ = srtV[p], srtI[p], sortO[p][:, 0:B * SC], sortH[p][:, 0:B * SC]
                O = O_.rearrange("p (b c) -> p b c", b=B)
                Hc = H_.rearrange("p (b c) -> p b c", b=B)
                L(ts(srtT, V, sh, B - 1, ALU.logical_shift_right, ALU.bitwise_and))
                L(v.tensor_copy(srtD, srtT))
                L(tt(O, srtD.unsqueeze(1).to_broadcast((P, B, SC)),
                     iota[:, 0:B].unsqueeze(2).to_broadcast((P, B, SC)), ALU.is_equal))
                L(scan(H_, O_, O_, 0.0, ALU.add, ALU.max))
                L(v.tensor_copy(sGl[:, 0:B], Hc[:, :, SC - 1]))
                L(v.memset(sGex[:, 0:1], 0.0))
                L(v.tensor_copy(sGex[:, 1:B], sGl[:, 0:B - 1]))
                L(tt(sCnt[:, 0:B], sGl[:, 0:B], sGex[:, 0:B], ALU.subtract))
                tell("counts_ready")
                v.wait_ge(S("offsets"), p + 1)
                L(ts(sXo[:, 0:B], bank(7)[:, 0:B], -1.0, None, ALU.add))
                L(tt(Hc, Hc, sXo[:, 0:B].unsqueeze(2).to_broadcast((P, B, SC)), ALU.add))
                L(tt(Hc, Hc, O, ALU.mult))
                L(v.tensor_reduce(srtP, Hc.rearrange("p b c -> p c b"), AX, ALU.add))
                L(v.tensor_copy(I, srtP))
                tell("rank_ready")

            v.wait_ge(S("consts"), 1)
            v.wait_ge(S("pkm_st"), 16)
            sort_pass(0)

            def consts_of(es, k):
                nb, a, b, c, d = prepv(es)
                nm = es.name
                v.wait_ge(S("ld_prep"), 80 * (k + 1))
                v.wait_ge(S("low_st"), 32 * k) if k else None
                last = [(slice(0, P), slice(0, nb - 1)), (slice(0, 16), slice(nb - 1, nb))]
                for ps_, bs in last:
                    A_, B_, C_, D_ = (q[ps_, bs, :] for q in (a, b, c, d))
                    Ai, Bi = A_.bitcast(I32), B_.bitcast(I32)
                    L(ts(D_.bitcast(I32), Ai, IDX - 1, None, ALU.bitwise_and))
                    L(v.tensor_copy(C_, D_.bitcast(I32)))
                    l3 = (q[:, 0:nb * P].rearrange("p (b i) -> p b i", b=nb)[ps_, bs, :] for q in (lowI, lowB))
                    li, lb = l3
                    L(ts(li, D_.bitcast(I32), es.fold * P - 1, None, ALU.bitwise_and))
                    L(v.tensor_copy(lb, li))
                    L(ts(Ai, Ai, 12, None, ALU.logical_shift_right))
                    L(ts(Bi, Bi, 12, None, ALU.logical_shift_right))
                    L(v.tensor_copy(D_, Ai))
                    L(v.tensor_copy(A_, Bi))
                    L(tt(B_, A_, D_, ALU.not_equal))
                    L(v.tensor_copy(A_, D_))
                tell("low_ready")
                tell("prep_rows")
                Ll = es.L
                L(ts(fA[:, 0:Ll].bitcast(I32), pkA[:, 0:Ll].bitcast(I32), 12, None, ALU.logical_shift_right))
                L(v.tensor_copy(dA[:, 0:Ll], fA[:, 0:Ll].bitcast(I32)))
                L(tt(fA[:, 1:Ll], dA[:, 1:Ll], dA[:, 0:Ll - 1], ALU.not_equal))
                L(ts(flagA[nm][:, 1:Ll], fA[:, 1:Ll], NEG, None, ALU.mult))
                L(v.memset(flagA[nm][:, 0:1], 0.0))
                L(v.memset(flagA[nm][:, Ll:Ll + 1], 0.0))
                tell("prep_scan")
                consume(v, "prep_" + nm, lambda t, kk: v.tensor_copy(
                    dsb[nm][:, t // nb, (t % nb) * P:min((t % nb + 1) * P, es.Q)],
                    bank(kk)[:, 0:min(P, es.Q - (t % nb) * P)]))
                L(v.tensor_copy(tileI[:, 0:es.Q], dsb[nm][:, 1, :]))
                L(ts(tileI[:, 0:es.Q], tileI[:, 0:es.Q], 6 + es.fold, None, ALU.logical_shift_right))
                L(v.tensor_copy(srcT[nm][:, :].rearrange("p (j r) -> p r j", r=16),
                                tileI[:, 0:es.Q].rearrange("p (r j) -> p r j", r=16)))
                v.wait_ge(S("ends_ps"), k + 1)
                L(v.tensor_copy(rowc[0:1, 0:2, :, :], bank(7)[0:1, 0:256].rearrange("p (k r h) -> p k h r", k=2, h=H8)))
                f_, l_ = rowc[0:1, 0, :, :], rowc[0:1, 1, :, :]
                sm = seam[nm]
                L(v.memset(sm[:, :, :, :], 1.0))
                L(tt(sm[:, 0, :, 1:16], f_[:, :, 1:16], f_[:, :, 0:15], ALU.not_equal))
                L(tt(sm[:, 1, :, 1:16], f_[:, :, 1:16], l_[:, :, 0:15], ALU.not_equal))
                L(tt(sm[:, 2, :, 0:15], l_[:, :, 1:16], l_[:, :, 0:15], ALU.not_equal))
                L(tt(sm[:, 3, :, 0:15], f_[:, :, 1:16], l_[:, :, 0:15], ALU.not_equal))
                L(ts(sm[:, :, :, :], sm[:, :, :, :], NEG, None, ALU.mult))
                n = es.tiles - 1
                L(v.memset(sel0, 0.0))
                L(v.memset(sel0[0:1, :], 1.0))
                tell("sel0_ready")
                v.wait_ge(S("firsts_ps"), k + 1)
                thr, cnt = small[:, 0:1], small[:, 1:2]
                L(ts(thr, chan[:, :], 128.0, 128.0, ALU.mult, ALU.add))
                L(ts(cmpT[0:n, 0:es.Q // 2], bank(6)[0:n, 0:es.Q:2], thr[0:n, :], None, ALU.is_lt))
                L(v.tensor_reduce(cnt[0:n, :], cmpT[0:n, 0:es.Q // 2], AX, ALU.add))
                L(stt(out=cnt[0:n, :], in0=cnt[0:n, :], scalar=1.0, in1=chan[0:n, :], op0=ALU.max, op1=ALU.add))
                L(ts(cmpT[0:n, 0:es.steps], iota[0:n, 0:es.steps], cnt[0:n, :], None, ALU.is_ge))
                tell("leave_ready")
                v.wait_ge(S("tiles_ps"), k + 1)
                L(v.tensor_copy(tS[:, 0:es.steps], bank(5)[:, 0:es.steps]))
                L(ts(t128[nm][:, :], tS[:, 0:es.steps], 128.0, None, ALU.mult))
                for tb, w, q in ((tI, es.W, 0), (tP, 3 * H8, 32)):
                    L(ts(tS[:, MAIN.steps:MAIN.steps + es.steps], tS[:, 0:es.steps], float(w), None, ALU.mult))
                    L(v.tensor_copy(tb[nm], tS[q:q + 1, MAIN.steps:MAIN.steps + es.steps]))
                L(tt(cmpT[:, 0:es.steps], iota[:, 0:es.steps], tS[:, 0:es.steps], ALU.subtract))
                L(ts(cmpT[:, 0:es.steps], cmpT[:, 0:es.steps], float(es.Q // 2 - 1), 2.0 * EW, ALU.min, ALU.mult))
                L(v.tensor_copy(cI[nm], cmpT[64:65, 0:es.steps]))
                tell("prep_done")

            consts_of(MAIN, 0)

            def norm(k, dst):
                for t in range(T):
                    L(v.bn_stats(st6[:, t % TB, :], X[:, t, :]))
                    L(v.bn_aggr(mv[:, t, :], st6[:, t % TB, :]))
                tell("var_ready")
                v.wait_ge(S("std_ready"), k + 1)
                L(v.reciprocal(rstd[:, :], rstd[:, :]))
                L(tt(dst, X[:, :, :], mv[:, :, 0:1].to_broadcast((P, T, C)), ALU.subtract))
                L(tt(dst, dst, rstd[:, :].unsqueeze(2).to_broadcast((P, T, C)), ALU.mult))
                tell("xn_ready")

            def elu1(region, name):
                for q in range(4):
                    L(ts(eluT[:, 0:1600], region[:, q * 1600:(q + 1) * 1600], 0.0, None, ALU.min))
                    tell("elu_min")
                    v.wait_ge(S("elu_exp"), 4 * (name == "k") + q + 1)
                    L(stt(out=region[:, q * 1600:(q + 1) * 1600], in0=region[:, q * 1600:(q + 1) * 1600], scalar=0.0,
                          in1=eluT[:, 0:1600], op0=ALU.max, op1=ALU.add))

            def lrelu(x):
                L(stt(out=x, in0=x, scalar=SLOPE, in1=x, op0=ALU.mult, op1=ALU.max))

            def score_weights(g, es, c):
                heads = HEADS[g]
                rep = 8 // heads
                tmp = small3[:, :, :, :].rearrange("p q t h -> p (q t h)")[:, 0:2 * c].rearrange("p (k c) -> p k c", k=2)
                v.wait_ge(S("ld_gw"), 16 * 3 * (g + 1))
                for q in range(2):
                    L(tt(tmp, Wn[:, :, 0:c], att_row(g, q).unsqueeze(1).to_broadcast((P, 2, c)), ALU.mult))
                    sc = rowsum[:, 0:2 * heads]
                    L(v.tensor_reduce(sc, tmp.rearrange("p k (h e) -> p (k h) e", h=heads), AX, ALU.add))
                    sc = sc.rearrange("p (k h) -> p k h", k=2)
                    for r in range(rep):
                        L(v.tensor_copy(Wn[:, :, c + 8 * q:c + 8 * q + 8].rearrange("p k (h r) -> p k h r", r=rep)[:, :, :, r], sc))
                tell("att_used")

            def split_scores(g, es, c):
                H = Hv(c)
                heads = HEADS[g]
                rep = 8 // heads
                rest = small3[:, 0, :, :]
                L(v.tensor_copy(rest, H[:, :, c + 8:c + 16]))
                for q in range(3):
                    L(v.tensor_copy(dS[:, :, q, :], rest))
                    if q < 2:
                        L(tt(rest, rest, dS[:, :, q, :], ALU.subtract))
                parts, w = s_parts(g)
                parts = parts.rearrange("p (k f t h) -> p k f t h", k=3, f=es.fold, h=heads)
                n = es.fold * es.sections * heads
                flat = small3[:, :, :, :].rearrange("p q t h -> p (q t h)")[:, 0:n]
                L(v.memset(flat, 0.0))
                L(v.tensor_copy(flat[:, 0:es.tiles * heads].rearrange("p (t h) -> p t h", h=heads),
                                H[:, 0:es.tiles, c:c + 8].rearrange("p t (h r) -> p t h r", r=rep)[:, :, :, 0]))
                rest = flat.rearrange("p (t f h) -> p f t h", f=es.fold, h=heads)
                for q in range(3):
                    for f in range(es.fold):
                        L(v.tensor_copy(parts[:, q, f, :, :], rest[:, f, :, :]))
                        if q < 2:
                            L(tt(rest[:, f, :, :], rest[:, f, :, :], parts[:, q, f, :, :], ALU.subtract))
                tell("parts_ready")

            def fetch_s(g, es):
                heads, nt = HEADS[g], es.sections
                rep = 8 // heads
                n0 = rounds_before(g)
                found = s_cols(g) if rep == 1 else R1[:, 5200:5200 + es.Q * heads]
                mask3 = sMask[:, 0:32 * nt].rearrange("p (b u t) -> p b u t", b=2, u=16)
                prod = sProd[:, 0:16 * nt * heads].rearrange("p (u t h) -> p u t h", u=16, t=nt)

                def onehots(r, b, turn):
                    v.wait_ge(S(f"ld_low{b}"), turn * 16 + 16 * (loads_before(g, b) + 1))
                    for f in range(es.fold):
                        ins = ts(place[f][:, b, :], lows[:, b, :], (chan, chan2)[f][:, :], None, ALU.is_equal)
                    ins.then_inc(S("low_used"), 1)
                    L(tt(mask3[:, b, :, :], iotaB[:, 0:nt].unsqueeze(1).to_broadcast((P, 16, nt)),
                         srcT[es.name][:, at(r * 16, 16)].unsqueeze(2).to_broadcast((P, 16, nt)), ALU.is_equal))

                def take(r, b):
                    v.wait_ge(S("s_ps"), r + (n0 + 1))
                    ps = PS[:, 4 * b:4 * b + 4, :].rearrange("p b (a w) -> p (b a) w", a=4)[:, :, 0:nt * heads]
                    tt(prod, ps.rearrange("p u (t h) -> p u t h", h=heads),
                       mask3[:, b, :, :].unsqueeze(3).to_broadcast((P, 16, nt, heads)),
                       ALU.mult).then_inc(S("s_free"), 1)
                    v.wait_ge(S("s_free"), r + (n0 + 3))
                    w = 16 * heads
                    L(v.tensor_reduce(found[:, at(r * w, w)].rearrange("p (u h) -> p u h", u=16),
                                      prod.rearrange("p u t h -> p u h t"), AX, ALU.add))

                onehots(0, 0, 0)

                def body(i):
                    onehots(i * 2 + 1, 1, i)
                    take(i * 2, 0)
                    onehots(i * 2 + 2, 0, i + 1)
                    take(i * 2 + 1, 1)
                L.loop(es.J // 2, 4, body)
                take(es.J - 1, 0)
                v.wait_ge(S("low_used"), n0 + es.J)
                if rep > 1:
                    L(v.tensor_copy(s_cols(g).rearrange("p (q r) -> p q r", r=rep),
                                    found.unsqueeze(2).to_broadcast((P, es.Q * heads, rep))))
                tell("s_ready")

            def scan_max(g, es):
                SA, MA = scan_bufs(g)
                fl = flagA[es.name]
                sm = seam[es.name]
                L(v.tensor_copy(EV(es).rearrange("p (r j) w -> p j r w", j=es.J)[:, :, :, 0:8],
                                s_cols(g).rearrange("p (j r h) -> p j r h", r=16, h=H8)))
                v.wait_ge(S("bank_free"), BASE[f"sA{g}"][0] + BASE[f"sA{g}"][1])
                Ll = es.L

                def seams(n, resets, seam_, end, shift, rev):
                    tell("end_ready")
                    v.wait_ge(S("end_row"), 2 * g + n + 1)
                    T_ = bank(7)[0:1, 0:P].rearrange("p (r h) -> p h r", h=H8)
                    e_, i_ = rowc[0:1, 0, :, :], rowc[0:1, 1, :, :]
                    L(v.memset(e_, NEG))
                    if rev:
                        L(tt(e_[:, :, 0:15], T_[:, :, 1:16], seam_[:, :, 0:15], ALU.add))
                    else:
                        L(tt(e_[:, :, 1:16], T_[:, :, 0:15], seam_[:, :, 1:16], ALU.add))
                    a_, b_, o_ = (q.rearrange("p h r -> p (h r)") for q in (resets, e_, i_))
                    if rev:
                        a_, b_, o_ = a_[:, ::-1], b_[:, ::-1], o_[:, ::-1]
                    L(scan(o_, a_, b_, NEG, ALU.add, ALU.max))
                    L(v.tensor_copy(rowc[0:1, 2, :, :].rearrange("p h r -> p (h r)").rearrange("p (r h) -> p h r", h=H8), i_))
                    tell("carry_row")
                    v.wait_ge(S("carry_ps"), 2 * g + n + 1)
                    L(v.tensor_copy(carry[:, :], bank(7)[:, 256:257]))

                L(scan(MA, fl[:, 0:Ll], SA, NEG, ALU.add, ALU.max))
                L(v.tensor_copy(dcol[:, 0:1], MA[:, Ll - 1:Ll]))
                seams(0, sm[:, 0, :, :], sm[:, 1, :, :], None, 1, False)
                L(scan(MA, fl[:, 0:Ll], SA, carry[:, 0:1], ALU.add, ALU.max))
                bk = fl[:, 1:Ll + 1][:, ::-1]
                L(scan(SA[:, ::-1], bk, MA[:, ::-1], NEG, ALU.add, ALU.max))
                L(v.tensor_copy(dcol[:, 0:1], SA[:, 0:1]))
                seams(1, sm[:, 2, :, :], sm[:, 3, :, :], None, -1, True)
                L(scan(SA[:, ::-1], bk, MA[:, ::-1], carry[:, 0:1], ALU.add, ALU.max))
                tell("max_ready")

            def edges(g, es, c):
                nm = es.name
                R, A_ = rows(g), Av(c)
                gb = groups_before(g)
                sb_ = gb * S2
                base, k = BASE[f"sB{g}"]
                L(v.memset(R1[:, 0:T * (c + 16)], 0.0))
                v.wait_ge(S("bank_free"), base + k)
                tell("rows_free")


                def onehots(n, b):
                    v.wait_ge(S("staged"), n + (gb + 1))
                    tt(drel[:, b % 2, :].rearrange("p (k a) -> p k a", a=2),
                       stage[:, b, :, 16].rearrange("p (k a) -> p k a", a=2),
                       t128[nm][:, at(n * S2, S2)].unsqueeze(2).to_broadcast((P, S2, 2)),
                       ALU.subtract).then_inc(S("rel_done"), 1)
                    v.wait_ge(S("rel_done"), n + (gb + 1))
                    for u in range(G):
                        ins = ts(onehB[:, b % 2, u, :], iotaB[:, :], drel[:, b % 2, u:u + 1], None, ALU.is_equal)
                    ins.then_inc(S("oneh_ready"), 1)

                def group(n, b, more):
                    if more:
                        onehots(n + 1, (b + 1) % NBUF)
                    v.wait_ge(S("d_ready"), n + (gb + 1))
                    v.tensor_reduce(zd[:, :, :], bank(6)[:, 0:3 * G * H8].rearrange("p (u k h) -> p u h k", u=G, k=3),
                                    AX, ALU.add).then_inc(S("z_done"), 1)
                    v.wait_ge(S("z_done"), n * 4 + (4 * gb + 1))
                    tt(zz[:, :, :, :], stage[:, b, :, 0:16].rearrange("p u (k h) -> p u k h", k=2),
                       zd[:, :, :].unsqueeze(2).to_broadcast((P, G, 2, H8)), ALU.add).then_inc(S("z_done"), 1)
                    v.wait_ge(S("z_done"), n * 4 + (4 * gb + 2))
                    stt(out=zz[:, :, :, :], in0=zz[:, :, :, :], scalar=SLOPE, in1=zz[:, :, :, :], op0=ALU.mult,
                        op1=ALU.max).then_inc(S("z_done"), 1)
                    v.wait_ge(S("z_done"), n * 4 + (4 * gb + 3))
                    tt(zd[:, :, :], zz[:, :, 0, :], zz[:, :, 1, :], ALU.subtract).then_inc(S("z_done"), 1)
                    v.wait_ge(S("z_done"), n * 4 + (4 * gb + 4))
                    ts(zd[:, :, :], zd[:, :, :], 0.0, None, ALU.min).then_inc(S("z_ready"), 1)
                    tt(R[:, b, :, c + 8:c + 16], stage[:, b, :, 8:16],
                       stage[:, b, :, 18:19].to_broadcast((P, G, H8)), ALU.mult)
                    if not isinstance(n, int) or n:
                        add_up(n - 1)
                    v.wait_ge(S("w_ready"), n + (gb + 1))
                    for u in range(0, G, 2):
                        r = R[:, b, u:u + 2, 0:c].rearrange("p u (h e) -> p u h e", h=H8)
                        tt(r, r, R[:, b, u:u + 2, c:c + 8].unsqueeze(3).to_broadcast((P, 2, H8, c // 8)),
                           ALU.mult).then_inc(S("scaled"), 1)

                def add_up(n):
                    offs = offsets(mybir.EngineType.DVE, tI[nm], n * S2, S2, (es.tiles - 1) * es.W)
                    for k in range(S2):
                        v.wait_ge(S("summed"), n * S2 + (sb_ + k + 1))
                        v.wait_ge(S("step_done"), n * S2 + (sb_ + k + 4))
                        a = R1[:, bass.ds(offs[k], c + 16)]
                        tt(a, a, bank(k)[:, 0:c + 16], ALU.add).then_inc(S("step_done"), 1)
                    v.wait_ge(S("step_done"), n * S2 + (sb_ + S2 + 4))
                    v.sem_inc(S("group_done"), 1)

                onehots(0, 0)
                group(0, 0, True)
                rounds = (es.groups - 1) // NBUF
                with v.Fori(0, rounds) as i:
                    for j in range(NBUF):
                        group(i * NBUF + (j + 1), (j + 1) % NBUF, True)
                for n in range(1 + rounds * NBUF, es.groups):
                    group(n, n % NBUF, n < es.groups - 1)
                add_up(es.groups - 1)

            def finish(g, es, c, told=None):
                H, A_ = Hv(c), Av(c)
                s_, d_ = H[:, :, c:c + 8], H[:, :, c + 8:c + 16]
                den, mx = A_[:, :, c:c + 8], A_[:, :, c + 8:c + 16]
                n3 = [small3[:, q, :, :] for q in range(4)]
                L(ts(n3[0], den, 0.5, NEG, ALU.is_lt, ALU.mult))
                L(tt(mx, mx, n3[0], ALU.add))
                L(tt(mx, mx, d_, ALU.add))
                L(tt(s_, s_, d_, ALU.add))
                lrelu(mx)
                lrelu(s_)
                L(tt(n3[0], mx, s_, ALU.max))
                L(tt(n3[1], mx, n3[0], ALU.subtract))
                L(tt(n3[2], s_, n3[0], ALU.subtract))
                tell("fin_z")
                v.wait_ge(S("fin_e"), g + 1)
                L(tt(den, den, n3[1], ALU.mult))
                L(tt(den, den, n3[2], ALU.add))
                if g != 3:
                    L(ts(den, den, 1e-16, None, ALU.add))
                L(v.reciprocal(n3[0], den))
                L(tt(n3[1], n3[1], n3[0], ALU.mult))
                L(tt(n3[2], n3[2], n3[0], ALU.mult))
                a_ = A_[:, :, 0:c].rearrange("p t (h e) -> p t h e", h=H8)
                h_ = H[:, :, 0:c].rearrange("p t (h e) -> p t h e", h=H8)
                L(tt(a_, a_, n3[1].unsqueeze(3).to_broadcast((P, T, H8, c // 8)), ALU.mult))
                L(tt(h_, h_, n3[2].unsqueeze(3).to_broadcast((P, T, H8, c // 8)), ALU.mult))
                v.wait_ge(S("ld_b"), (32, 48, 80, 96)[g])
                blocks = T // TB if told else 1
                for b in range(blocks):
                    n = T // blocks
                    q = slice(b * n, (b + 1) * n)
                    L(tt(A_[:, q, 0:c], A_[:, q, 0:c], H[:, q, 0:c], ALU.add))
                    L(tt(A_[:, q, 0:c], A_[:, q, 0:c], brow[:, 2, 0:c].unsqueeze(1).to_broadcast((P, n, c)), ALU.add))
                    if told == "xn_ready" and g == 0:
                        L(ts(A_[:, q, 0:c], A_[:, q, 0:c], 0.0, None, ALU.max))
                    if told:
                        tell(told)

            def fill_records(es):
                v.wait_ge(S("xs_clear"), 16)
                L(v.tensor_copy(EV(es)[:, :, 16:19], dsb[es.name][:, :, :].rearrange("p k q -> p q k")))
                tell("records")

            v.wait_ge(S("ld_x"), 32)
            score_weights(0, *GATS[0])
            norm(0, nodes(R2))
            v.wait_ge(S("q_copied"), 1)
            elu1(R4[:, 0:2 * T * P], "q")
            tell("q_ready")
            v.wait_ge(S("kv_copied"), 1)
            elu1(R1[:, 0:T * C], "k")
            L(v.memset(V0[:, :, :, 128:129], 1.0))
            tell("k_ready")
            v.wait_ge(S("ctx_ps"), 1)
            for a in range(2):
                L(v.tensor_copy(dcol[:, a:a + 1], bank(6 + a)[:, 128:129]))
                L(tt(BD[:, a, 0:P], bank(6 + a)[:, 0:P], mask[:, 0:P], ALU.mult))
                L(ts(BD[:, a, P:P + 4], mask[:, P:P + 4], dcol[:, a:a + 1], None, ALU.mult))
            tell("ctx_ready")
            v.wait_ge(S("h_copied"), 1)
            split_scores(0, *GATS[0])

            base, _ = BASE["mixo"]

            def mixo(i):
                for k in range(TB):
                    v.wait_ge(S("bank_full"), i * TB + (k + base - 4))
                    pv = bank(k)[:, 0:264].rearrange("p (a w) -> p a w", a=2)
                    dn = dcol[:, 0:8].rearrange("p (a w) -> p a w", a=2)
                    L(ts(dn, pv[:, :, P:P + 4], 1e-6, None, ALU.max))
                    L(v.reciprocal(dn, dn))
                    L(tt(AO[:, bass.ds(i * TB + k, 1), :].rearrange("p o (a h e) -> p (o a) h e", a=2, h=4),
                         pv[:, :, 0:P].rearrange("p a (h e) -> p a h e", h=4),
                         dn.unsqueeze(3).to_broadcast((P, 2, 4, 32)), ALU.mult))
                    v.sem_inc(S("bank_free"), 1)
            L.loop(T // TB, 3 * TB, mixo)
            v.wait_ge(S("bank_free"), base + T)
            tell("ao_ready")
            consume(v, "proj", lambda t, k: tt(X[:, bass.ds(t, 1), :].rearrange("p a c -> p (a c)"),
                                               X[:, bass.ds(t, 1), :].rearrange("p a c -> p (a c)"),
                                               bank(k)[:, 0:C], ALU.add))
            v.wait_ge(S("ld_b"), 32)
            L(tt(X[:, :, :], X[:, :, :], brow[:, 3, :].unsqueeze(1).to_broadcast((P, T, C)), ALU.add))
            sort_pass(1)
            fill_records(MAIN)
            fetch_s(0, MAIN)
            scan_max(0, MAIN)
            edges(0, *GATS[0])
            finish(0, *GATS[0], told="xn_ready")
            tell("fin_done")
            score_weights(1, *GATS[1])
            v.wait_ge(S("h_copied"), 2)
            split_scores(1, *GATS[1])
            consts_of(FFN, 1)
            fill_records(MAIN)
            fetch_s(1, MAIN)
            scan_max(1, MAIN)
            edges(1, *GATS[1])
            finish(1, *GATS[1])
            L(tt(X[:, :, :], X[:, :, :], Av(C)[:, :, 0:C], ALU.add))
            tell("fin_done")

            norm(1, nodes(R2))
            score_weights(2, *GATS[2])
            v.wait_ge(S("h_copied"), 3)
            split_scores(2, *GATS[2])
            fill_records(FFN)
            fetch_s(2, FFN)
            scan_max(2, FFN)
            edges(2, *GATS[2])
            finish(2, *GATS[2])
            O16 = Av(16)[:, :, 0:16]
            m1, m2 = rowsum[:, 0:T], rowsum[:, T:2 * T]
            L(v.tensor_reduce(m1, O16, AX, ALU.add))
            L(ts(m1, m1, 1.0 / 16, None, ALU.mult))
            L(tt(O16, O16, m1.unsqueeze(2).to_broadcast((P, T, 16)), ALU.subtract))
            sq = small4[:, 0:T * 16].rearrange("p (t c) -> p t c", t=T)
            L(tt(sq, O16, O16, ALU.mult))
            L(v.tensor_reduce(m2, sq, AX, ALU.add))
            L(ts(rstd[:, :], m2, 1.0 / 16, None, ALU.mult))
            tell("rvar_ready")
            v.wait_ge(S("rstd_ready"), 1)
            L(v.reciprocal(rstd[:, :], rstd[:, :]))
            L(tt(O16, O16, rstd[:, :].unsqueeze(2).to_broadcast((P, T, 16)), ALU.mult))
            v.wait_ge(S("ld_b2"), 16)
            L(tt(O16, O16, brow[:, 3, 0:16].unsqueeze(1).to_broadcast((P, T, 16)), ALU.mult))
            L(tt(O16, O16, brow[:, 0, 0:16].unsqueeze(1).to_broadcast((P, T, 16)), ALU.add))
            sc = small4[:, 400:400 + 4 * T].rearrange("p (t e) -> p t e", t=T)
            L(v.tensor_reduce(sc, O16.rearrange("p t (h e) -> p t e h", h=4), AX, ALU.add))
            L(ts(sc, sc, 0.25, None, ALU.mult))
            cmp4 = small4[:, 0:T * 4].rearrange("p (t e) -> p t e", t=T)
            rk = small4[:, 100:100 + T * 4].rearrange("p (t e) -> p t e", t=T)
            L(v.memset(rk, 0.0))
            for j in range(EXP0):
                sj = sc[:, :, j:j + 1].to_broadcast((P, T, EXP0))
                L(tt(cmp4, sj, sc, ALU.is_gt))
                L(tt(rk, rk, cmp4, ALU.add))
                if j < EXP0 - 1:
                    w = EXP0 - 1 - j
                    L(tt(cmp4[:, :, 0:w], sc[:, :, j:j + 1].to_broadcast((P, T, w)), sc[:, :, j + 1:EXP0], ALU.is_equal))
                    L(tt(rk[:, :, j + 1:EXP0], rk[:, :, j + 1:EXP0], cmp4[:, :, 0:w], ALU.add))
            L(v.tensor_reduce(m1, sc, AX, ALU.max))
            L(tt(gates[:, :, :], sc, m1.unsqueeze(2).to_broadcast((P, T, EXP0)), ALU.subtract))
            tell("gate_z")
            v.wait_ge(S("gate_e"), 1)
            L(stt(out=gates[:, :, :], in0=rk, scalar=1.5, in1=gates[:, :, :], op0=ALU.is_lt, op1=ALU.mult))
            L(v.tensor_reduce(m1, gates[:, :, :], AX, ALU.add))
            L(v.reciprocal(m1, m1))
            L(tt(gates[:, :, :], gates[:, :, :], m1.unsqueeze(2).to_broadcast((P, T, EXP0)), ALU.mult))
            tell("fin_done")
            v.wait_ge(S("ld_moe"), 64)
            nE = EXP0 * TB
            with v.Fori(0, T // TB) as i:
                for e in range(EXP0):
                    for k in range(TB):
                        o = e * TB + k
                        if e:
                            v.wait_ge(S("moe_free"), i * nE + (o - TB + 1 + 4))
                        x = X[:, bass.ds(i * TB + k, 1), :].rearrange("p a c -> p (a c)")
                        stt(out=x, in0=b2e[:, e * C:(e + 1) * C],
                            scalar=gates[:, bass.ds(i * TB + k, 1), e:e + 1].rearrange("p a c -> p (a c)"),
                            in1=x, op0=ALU.mult, op1=ALU.add).then_inc(S("bias_done"), 1)
                        v.wait_ge(S("bias_done"), i * nE + (o + 1))
                        v.wait_ge(S("moe_full"), i * nE + (o + 1 + 2 * TB))
                        stt(out=x, in0=bank(o % 4)[:, 0:C],
                            scalar=gates[:, bass.ds(i * TB + k, 1), e:e + 1].rearrange("p a c -> p (a c)"),
                            in1=x, op0=ALU.mult, op1=ALU.add).then_inc(S("moe_free"), 1)
            v.wait_ge(S("moe_free"), 4 + nE * (T // TB))
            tell("moe0_done")

            XN = nodes(R2)
            score_weights(3, *GATS[3])
            norm(2, XN)
            L(stt(out=X[:, :, :], in0=XN, scalar=2.0, in1=X[:, :, :], op0=ALU.mult, op1=ALU.add))
            g3 = lambda r: r[:, 0:T * C].rearrange("p (q e) -> p q e", e=32)
            mean, std = rowsum[:, 0:200], small4[:, 0:200]
            L(v.tensor_reduce(mean, g3(R2), AX, ALU.add))
            L(ts(mean, mean, 1.0 / 32, None, ALU.mult))
            L(tt(g3(R1), g3(R2), mean.unsqueeze(2).to_broadcast((P, 200, 32)), ALU.subtract))
            tell("centered")
            L(tt(g3(R4), g3(R1), g3(R1), ALU.mult))
            L(v.tensor_reduce(std, g3(R4), AX, ALU.add))
            tell("hvar_ready")
            v.wait_ge(S("hstd_ready"), 1)
            L(ts(std, std, 1e-5, None, ALU.add))
            L(v.reciprocal(std, std))
            L(tt(g3(R1), g3(R1), std.unsqueeze(2).to_broadcast((P, 200, 32)), ALU.mult))
            v.wait_ge(S("ld_mix1"), 64)
            bc = lambda q: brow[:, q, :].unsqueeze(1).to_broadcast((P, T, C))
            L(tt(V1, K1, bc(2), ALU.mult))
            L(tt(V1, V1, bc(3), ALU.add))
            L(tt(K1, K1, bc(0), ALU.mult))
            L(tt(K1, K1, bc(1), ALU.add))
            tell("mix1_kv")
            v.wait_ge(S("ctx_ps"), 2)
            for a in range(2):
                L(stt(out=BD[:, a, 0:P], in0=bank(6 + a)[:, 0:P], scalar=1.0 / N, in1=mask[:, 0:P], op0=ALU.mult,
                      op1=ALU.mult))
            tell("ctx_ready")
            consume(v, "mix1o", lambda t, k: tt(X[:, bass.ds(t, 1), :].rearrange("p a c -> p (a c)"),
                                                X[:, bass.ds(t, 1), :].rearrange("p a c -> p (a c)"),
                                                bank(k)[:, 0:C], ALU.add))
            v.wait_ge(S("h_copied"), 4)
            split_scores(3, *GATS[3])
            fill_records(MAIN)
            fetch_s(3, MAIN)
            scan_max(3, MAIN)
            edges(3, *GATS[3])
            finish(3, *GATS[3], told="bn_in")
            out3 = Av(C)[:, :, 0:C]
            meanS, varS = R2[:, 0:C], R2[:, C:2 * C]
            base, _ = BASE["bnm"]
            v.wait_ge(S("bank_full"), base - 4)
            ts(meanS, bank(0)[:, 0:C], 1.0 / N, None, ALU.mult).then_inc(S("bank_free"), 1)
            v.wait_ge(S("bank_free"), base + 1)
            L(tt(out3, out3, meanS.unsqueeze(1).to_broadcast((P, T, C)), ALU.subtract))
            for b in range(T // TB):
                q = slice(b * TB, (b + 1) * TB)
                L(tt(nodes(R4)[:, q, :], out3[:, q, :], out3[:, q, :], ALU.mult))
                tell("bn_in")
            v.wait_ge(S("bank_full"), base - 3)
            ts(varS, bank(0)[:, 0:C], 1.0 / N, None, ALU.mult).then_inc(S("bank_free"), 1)
            v.wait_ge(S("bank_free"), base + 2)
            tell("bn_var")
            v.wait_ge(S("bn_std"), 1)
            L(v.reciprocal(varS, varS))
            v.wait_ge(S("ld_b2"), 48)
            L(tt(varS, varS, brow[:, 0, :], ALU.mult))
            L(tt(out3, out3, varS.unsqueeze(1).to_broadcast((P, T, C)), ALU.mult))
            L(tt(out3, out3, bc(1), ALU.add))
            L(tt(X[:, :, :], X[:, :, :], out3, ALU.add))
            tell("fin_done")
            tell("bn_done")

            norm(3, nodes(R1))
            v.wait_ge(S("ld_rb"), 16)
            base, _ = BASE["rt"]
            v.wait_ge(S("xt_used"), 1)
            consume(v, "rt", lambda t, k: tt(lg[:, bass.ds(t, 1), :].rearrange("p a e -> p (a e)"), bank(k)[:, 0:32],
                                             brow[:, 0, 0:32], ALU.add))
            mx = rowsum[:, 0:T]
            L(v.tensor_reduce(mx, lg, AX, ALU.max))
            L(tt(eq, lg, mx.unsqueeze(2).to_broadcast((P, T, 32)), ALU.is_equal))
            rev = small4[:, 0:32]
            L(ts(rev, iota[:, 0:32], -1.0, 32.0, ALU.mult, ALU.add))
            L(tt(eq, eq, rev.unsqueeze(1).to_broadcast((P, T, 32)), ALU.mult))
            L(v.tensor_reduce(mx, eq, AX, ALU.max))
            L(tt(lg, eq, mx.unsqueeze(2).to_broadcast((P, T, 32)), ALU.is_equal))
            real = dcol[:, 0:1]
            L(ts(real, chan[:, :], float(TAIL), None, ALU.is_lt))
            L(ts(lg[:, T - 1, :], lg[:, T - 1, :], real, None, ALU.mult))
            L(ts(lower, iota[:, 0:P], chan[:, :], None, ALU.is_gt))
            L(v.memset(before[:, 0, :], 0.0))
            for t in range(T):
                L(tt(before[:, t + 1, :], before[:, t, :], lg[:, t, :], ALU.add))
            tell("choice")
            v.wait_ge(S("places_ps"), 1)
            L(ts(first, iota[:, 0:32], 128.0, None, ALU.mult))
            cmp_ = bins[:, 0:32, 0:T]
            L(v.tensor_copy(used, bank(7)[:, 0:32]))
            L(tt(cmp_, used.unsqueeze(2).to_broadcast((P, 32, T)), first[:, 0:T].unsqueeze(1).to_broadcast((P, 32, T)),
                 ALU.is_gt))
            L(v.tensor_reduce(used, cmp_, AX, ALU.add))
            L(scan(upto, used, used, 0.0, ALU.add, ALU.max))
            L(tt(first, upto, used, ALU.subtract))
            L(ts(first, first, float(P), None, ALU.mult))
            for hf, (t0, t1) in enumerate(((0, 13), (13, T))):
                L(tt(eq[:, t0:t1, :], bank(5 + hf)[:, 0:(t1 - t0) * 32].rearrange("p (t e) -> p t e", e=32),
                     first.unsqueeze(1).to_broadcast((P, t1 - t0, 32)), ALU.add))
            L(tt(eq, eq, lg, ALU.mult))
            L(v.tensor_reduce(mx, eq, AX, ALU.add))
            L(v.tensor_copy(slotI, mx))
            tell("slots_ready")
            L(tt(bins, upto.unsqueeze(1).to_broadcast((P, SLOTS, 32)),
                 iota[:, 0:SLOTS].unsqueeze(2).to_broadcast((P, SLOTS, 32)), ALU.is_le))
            own = rowsum[:, 32:32 + SLOTS]
            L(v.tensor_reduce(own, bins, AX, ALU.add))
            L(ts(own, own, float(EXP1 - 1), float(F1), ALU.min, ALU.mult))
            L(v.tensor_copy(w1_at, own[0:1, :]))
            L(ts(own, own, float(C // F1), None, ALU.mult))
            L(v.tensor_copy(w2_at, own[0:1, :]))
            L(v.memset(hs[64:65, :, :], 1.0))
            tell("owners_ready")

            tell("xs_copied", 2)
            tell("ys_copied", 2)

            def turned(n, b):
                v.wait_ge(S("xs_ps"), n + 1)
                v.wait_ge(S("up_ps"), n + 1)
                v.tensor_copy(xsT[:, b, :, :], bank(b)[:, 0:C].rearrange("p (k n) -> p k n", k=2)
                              ).then_inc(S("xs_copied"), 1)

            def result(n, k, i):
                v.wait_ge(S("down_ps"), n + 3)
                if k % SB == 0:
                    v.wait_ge(S(f"ys_st{k // SB}"), i * 16 + 16)
                v.tensor_copy(ys[:, k // SB, k % SB, :], bank(4 + k % 2)[:, 0:C]).then_inc(S("ys_copied"), 1)

            def turn8(i, end):
                for k in range(TURN):
                    if k + 2 < TURN or not end:
                        turned(i * TURN + (k + 2), k % 2)
                    result(i * TURN + k, k, i)
            turned(0, 0)
            turned(1, 1)
            last = SLOTS // TURN - 1
            with v.Fori(0, last) as i:
                turn8(i, False)
            turn8(last, True)
            XN = nodes(R1)
            for b in range(T // TB):
                v.wait_ge(S(f"ys_got{b}"), 16 * TB)
                q = slice(b * TB, (b + 1) * TB)
                L(stt(out=X[:, q, :], in0=XN[:, q, :], scalar=0.0, in1=X[:, q, :], op0=ALU.max, op1=ALU.add))
                tell("out_done")

        @block.scalar
        def _(s):
            L = Chain(s, "act_chain")
            act = s.activation

            def copy(out_, in_):
                return act(out_, in_, ACT.Copy)

            def tell(name, k=1):
                s.sem_inc(S(name), k)

            def to_xt(g):
                consume(s, f"xT{g}", lambda t, k: copy(XT[:, :, bass.ds(t * P, P)],
                                                       bank(k)[:, 0:2 * P].rearrange("p (a n) -> p a n", a=2)))
                tell("xt_ready")

            def std(src, dst, bias):
                L(act(dst, src, ACT.Sqrt, bias=bias))

            def gat(g, es, c):
                E = EV(es)
                nm = es.name
                s.wait_ge(S("records"), g + 1)
                for b in range(EARLY):
                    offs = offsets(mybir.EngineType.Activation, cI[nm], b * S2, S2, (es.Q - 2) * EW)
                    for k in range(S2):
                        L(copy(idx[:, b, 2 * k:2 * k + 2],
                               R4[:, bass.ds(offs[k], 2 * EW)].rearrange("p (u w) -> p u w", u=2)[:, :, 17]))
                tell("first_idx")
                SA, _ = scan_bufs(g)

                def down(t, k):
                    w = min(4, es.J - 4 * t) * P
                    return copy(SA[:, 4 * t * P:4 * t * P + w], bank(k)[:, 0:w])
                consume(s, f"sA{g}", down)
                Er = E.rearrange("p (r j) w -> p j r w", j=es.J)

                def up(t, k):
                    w = min(4, es.J - 4 * t)
                    for q in range(w):
                        ins = copy(Er[:, 4 * t + q, :, 8:16], bank(k)[:, q * P:(q + 1) * P].rearrange("p (r h) -> p r h", h=H8))
                    return ins
                consume(s, f"sB{g}", up)

                gb = groups_before(g)
                R = rows(g)

                def stage_in(n, b):
                    s.wait_ge(S("group_done"), n + (gb + 1))
                    offs = offsets(mybir.EngineType.Activation, cI[nm], n * S2, S2, (es.Q - 2) * EW)
                    for k in range(S2):
                        ins = copy(stage[:, b, 2 * k:2 * k + 2, :].rearrange("p u w -> p (u w)"),
                                   R4[:, bass.ds(offs[k], 2 * EW)])
                    ins.then_inc(S("rec_done"), 1)
                    s.wait_ge(S("rec_done"), n + (gb + 1))
                    if isinstance(n, int) and n < EARLY:
                        tell("staged")
                    else:
                        copy(idx[:, b, :], stage[:, b, :, 17]).then_inc(S("staged"), 1)

                def turned(n, b):
                    s.wait_ge(S("turned_ps"), n + (gb + 1))
                    copy(onehT[:, :, :], bank(4).bitcast(BF16).rearrange("p (u e) -> p u e", u=G)).then_inc(S("turned"), 1)
                    if gb or not isinstance(n, int) or n > 1:
                        s.wait_ge(S("group_done"), n + (gb + NBUF - 1))
                    copy(oneh[:, b % 2, :, :], onehB[:, b % 2, :, :]).then_inc(S("oneh_copied"), 1)

                def group(n, b, more, more3):
                    s.wait_ge(S("z_ready"), n + (gb + 1))
                    k = n // NBUF if isinstance(n, int) else None
                    gathered(n, b, k)
                    act(R[:, b, :, c:c + 8], zd[:, :, :], ACT.Exp).then_inc(S("w_ready"), 1)
                    if more:
                        turned(n + 1, b + 1)
                    if more3:
                        stage_in(n + AHEAD, (b + AHEAD) % NBUF)

                def gathered(n, b, k):
                    q = k if k is not None else cur[0]
                    fills = sum((e.groups - b + NBUF - 1) // NBUF for e, _ in GATS[:g])
                    s.wait_ge(S(f"gat{b}"), q * P + (P * fills + P))

                cur = [None]
                for b in range(AHEAD):
                    stage_in(b, b)
                turned(0, 0)
                with s.Fori(0, es.turns - 1) as i:
                    cur[0] = i
                    for b in range(NBUF):
                        group(i * NBUF + b, b, True, True)
                for n in range((es.turns - 1) * NBUF, es.groups):
                    group(n, n % NBUF, n + 1 < es.groups, n + AHEAD < es.groups)
                s.wait_ge(S("fin_z"), g + 1)
                L(act(small3[:, 1:3, :, :], small3[:, 1:3, :, :], ACT.Exp))
                tell("fin_e")

            def to_h(g, c):
                consume(s, f"h{g}", lambda t, k: copy(Hv(c)[:, bass.ds(t, 1), :].rearrange("p a c -> p (a c)"),
                                                      bank(k)[:, 0:c + 16]))
                tell("h_copied")

            def node_std(k):
                s.wait_ge(S("var_ready"), k + 1)
                std(mv[:, :, 1], rstd[:, :], epsc[:, 0:1])
                tell("std_ready")

            consume(s, "wT", lambda t, k: copy(wT[:, :, t, :], bank(k)[:, 0:2 * P].rearrange("p (a n) -> p a n", a=2)))
            tell("wT_ready")
            node_std(0)
            to_xt(0)
            consume(s, "q", lambda t, k: copy(qT[:, t // 10, (t % 10) * 320:(t % 10 + 1) * 320], bank(k)[:, 0:320]))
            tell("q_copied")

            def kv(t, k):
                copy(K0[:, bass.ds(t, 1), :].rearrange("p a c -> p (a c)"), bank(k)[:, 0:C])
                return copy(V0[:, bass.ds(t, 1), :, 0:P].rearrange("p o a w -> p (o a) w"),
                            bank(k)[:, C:2 * C].rearrange("p (a w) -> p a w", a=2))
            for q in range(4):
                s.wait_ge(S("elu_min"), q + 1)
                L(act(eluT[:, 0:1600], eluT[:, 0:1600], ACT.Exp))
                tell("elu_exp")
            consume(s, "kv", kv)
            tell("kv_copied")
            for q in range(4, 8):
                s.wait_ge(S("elu_min"), q + 1)
                L(act(eluT[:, 0:1600], eluT[:, 0:1600], ACT.Exp))
                tell("elu_exp")
            to_h(0, C)
            s.wait_ge(S("ao_ready"), 1)
            consume(s, "aT", lambda t, k: copy(XT[:, :, bass.ds(t * P, P)],
                                               bank(k)[:, 0:2 * P].rearrange("p (a n) -> p a n", a=2)))
            tell("aT_ready")
            gat(0, *GATS[0])
            to_xt(1)
            to_h(1, C)
            gat(1, *GATS[1])
            node_std(1)
            to_xt(2)
            to_h(2, 16)
            gat(2, *GATS[2])
            s.wait_ge(S("rvar_ready"), 1)
            std(rstd[:, :], rstd[:, :], epsc[:, 0:1])
            tell("rstd_ready")
            s.wait_ge(S("gate_z"), 1)
            L(act(gates[:, :, :], gates[:, :, :], ACT.Exp))
            tell("gate_e")
            s.wait_ge(S("b1_ps"), 1)
            L(copy(b1T[:, :], bank(7)[:, 0:16]))
            tell("b1_ready")
            with s.Fori(0, T // TB) as i:
                for e in range(EXP0):
                    s.wait_ge(S("moe_full"), i * (EXP0 * TB) + (e + 1) * TB)
                    for f in range(4):
                        for hf in range(2):
                            m = (e * 4 + f) * 2 + hf
                            s.wait_ge(S("hid_full"), i * 32 + (m + 1))
                            col = e * 4 + f
                            act(hh[:, e % 2, f, hf * 320:(hf + 1) * 320], bank(4 + m % 4)[:, 0:320], ACT.Gelu,
                                bias=b1T[:, col:col + 1]).then_inc(S("hid_free"), 1)
            node_std(2)
            s.wait_ge(S("hvar_ready"), 1)
            L(act(small4[:, 0:200], small4[:, 0:200], ACT.Sqrt, scale=1.0 / 31))
            tell("hstd_ready")
            to_xt(3)
            s.wait_ge(S("centered"), 1)
            to_h(3, C)
            gat(3, *GATS[3])
            s.wait_ge(S("bn_var"), 1)
            std(R2[:, C:2 * C], R2[:, C:2 * C], epsc[:, 0:1])
            tell("bn_std")
            node_std(3)
            s.wait_ge(S("b1_ps"), 2)
            L(copy(b1c, bank(7)[0:64, 0:32]))
            L(copy(rwT[:, :, :], bank(7)[:, 64:128].rearrange("p (k e) -> p k e", k=2)))
            tell("b1_ready")
            to_xt(4)
            tell("xt_used")
            s.wait_ge(S("owners_ready"), 1)
            tell("hs_ready", 2)

            def turn8(i, end):
                w1 = offsets(mybir.EngineType.Activation, w1_at, i * TURN, TURN, (EXP1 - 1) * F1)
                for k in range(TURN):
                    n, b = i * TURN + k, k % 2
                    s.wait_ge(S("up_ps"), n + 1)
                    copy(w1s[:, b, :, :], W1x[:, :, bass.ds(w1[k], F1)]).then_inc(S("w1_ready"), 1)
                    s.wait_ge(S("up_ps"), n + 3)
                    s.wait_ge(S("down_ps"), n + 1)
                    act(hs[0:64, b, :], bank(2 + b)[0:64, 0:P], ACT.Relu,
                        bias=b1c[:, bass.ds(w1[k] // F1, 1)]).then_inc(S("hs_ready"), 1)
            last = SLOTS // TURN - 1
            with s.Fori(0, last) as i:
                turn8(i, False)
            turn8(last, True)

        @block.tensor
        def _(pe):
            mm = pe.matmul

            def turn(out_, in_, k=P):
                return pe.transpose(out_, in_, ident[0:k, 0:k])

            pe.wait_ge(S("consts"), 1)
            def sort_offsets(p):
                B = DIGITS[p][1]
                pe.wait_ge(S("counts_ready"), p + 1)
                mm(bank(7)[:, 0:B], ltri, sCnt[:, 0:B], start=True, stop=False)
                mm(bank(7)[:, 0:B], offd, sGex[:, 0:B], start=False, stop=True).then_inc(S("offsets"), 1)
            sort_offsets(0)

            def prepare(es, k):
                nb, a, b, c, d = prepv(es)
                pe.wait_ge(S("prep_rows"), k + 1)

                def chunk_cols(t, kk):
                    w = min(P, es.Q - (t % nb) * P)
                    src = (a, c, b)[t // nb]
                    return turn(bank(kk)[:, 0:w], src[0:w, t % nb, :], w)
                fill(pe, "prep_" + es.name, chunk_cols)
                pe.wait_ge(S("prep_scan"), k + 1)
                for q, col in enumerate((0, es.L - 1)):
                    ins = mm(bank(7)[0:1, q * P:(q + 1) * P], dA[:, col:col + 1], ident[:, :], start=True, stop=True)
                ins.then_inc(S("ends_ps"), 1)
                pe.wait_ge(S("sel0_ready"), k + 1)
                n = es.tiles - 1
                mm(bank(6)[0:n, 0:es.Q], sel0[:, 0:n], dsb[es.name][:, 0, :], start=True, stop=True).then_inc(S("firsts_ps"), 1)
                pe.wait_ge(S("leave_ready"), k + 1)
                mm(bank(5)[:, 0:es.steps], ones[0:n, :], cmpT[0:n, 0:es.steps], start=True, stop=True).then_inc(S("tiles_ps"), 1)

            prepare(MAIN, 0)

            pe.wait_ge(S("ld_wraw"), 48)

            def w_turn(t, kk):
                for k in range(2):
                    ins = turn(bank(kk)[:, k * P:(k + 1) * P], wraw[:, t, k * P:(k + 1) * P])
                return ins
            fill(pe, "wT", w_turn)

            def x_turn(name, src, blocks_from=None):
                def one(t, kk):
                    if blocks_from is not None and t % TB == 0:
                        pe.wait_ge(S("xn_ready"), blocks_from + t // TB)
                    for k in range(2):
                        ins = turn(bank(kk)[:, k * P:(k + 1) * P],
                                   src[:, t, k * P:(k + 1) * P])
                    return ins
                fill(pe, name, one)

            def product(name, rhs, n):
                def one(t, kk):
                    for k in range(2):
                        ins = mm(bank(kk)[:, 0:n], XT[:, k, t * P:(t + 1) * P], rhs(k), start=(k == 0), stop=(k == 1))
                    return ins
                fill(pe, name, one)

            def gat(g, es, c):
                pe.wait_ge(S("parts_ready"), g + 1)
                parts, w = s_parts(g)
                n0 = rounds_before(g)

                def find(r, b):
                    pe.wait_ge(S("low_used"), r + (n0 + 1))
                    pe.wait_ge(S("s_free"), r + (n0 + 1))
                    for u in range(16):
                        for q in range(3 * es.fold):
                            f, k = q // 3, q % 3
                            ins = mm(bank(4 * b + u // 4)[:, (u % 4) * P:(u % 4) * P + w],
                                     place[f][:, b, u * P:(u + 1) * P],
                                     parts[:, (k * es.fold + f) * w:(k * es.fold + f + 1) * w],
                                     start=(q == 0), stop=(q == 3 * es.fold - 1))
                    ins.then_inc(S("s_ps"), 1)
                with pe.Fori(0, es.J // 2) as i:
                    for b in range(2):
                        find(i * 2 + b, b)
                find(es.J - 1, 0)
                pe.wait_ge(S("s_ready"), g + 1)
                SA, MA = scan_bufs(g)

                def down(t, kk):
                    for q in range(min(4, es.J - 4 * t)):
                        ins = turn(bank(kk)[:, q * P:(q + 1) * P], s_cols(g)[:, (4 * t + q) * P:(4 * t + q + 1) * P])
                    return ins
                fill(pe, f"sA{g}", down)
                for n in range(2):
                    pe.wait_ge(S("end_ready"), 2 * g + n + 1)
                    mm(bank(7)[0:1, 0:P], dcol[:, 0:1], ident[:, :], start=True, stop=True).then_inc(S("end_row"), 1)
                    pe.wait_ge(S("carry_row"), 2 * g + n + 1)
                    mm(bank(7)[:, 256:257], rowc[0:1, 2, :, :].rearrange("p h r -> p (h r)"), ones[0:1, 0:1],
                       start=True, stop=True).then_inc(S("carry_ps"), 1)
                pe.wait_ge(S("max_ready"), g + 1)

                def up(t, kk):
                    for q in range(min(4, es.J - 4 * t)):
                        j = 4 * t + q
                        ins = turn(bank(kk)[:, q * P:(q + 1) * P], SA[:, j * P:(j + 1) * P])
                    return ins
                fill(pe, f"sB{g}", up)
                base, k = BASE[f"sB{g}"]
                pe.wait_ge(S("bank_free"), base + k)

                nm, H, R = es.name, Hv(c), rows(g)
                gb = groups_before(g)
                sb_ = gb * S2

                def turns(n, b):
                    pe.wait_ge(S("oneh_ready"), n + (gb + 1))
                    pe.wait_ge(S("turned"), n + gb) if gb or not isinstance(n, int) or n else None
                    for u in range(G):
                        ins = pe.transpose(bank(4).bitcast(BF16)[:, u * P:(u + 1) * P], onehB[:, b % 2, u, :], identB[:, :])
                    ins.then_inc(S("turned_ps"), 1)

                def fetch(n):
                    pe.wait_ge(S("turned"), n + (gb + 1))
                    if gb or not isinstance(n, int) or n:
                        pe.wait_ge(S("z_ready"), n + gb)
                    offs = offsets(mybir.EngineType.PE, tP[nm], n * S2, S2, (es.tiles - 1) * 3 * H8)
                    dcols = dS[:, :, :, :].rearrange("p t k h -> p (t k h)")
                    for u in range(G):
                        ins = mm(bank(6)[:, u * 24:(u + 1) * 24], onehT[:, u, :], dcols[:, bass.ds(offs[u // 2], 24)],
                                 start=True, stop=True)
                    ins.then_inc(S("d_ready"), 1)

                def group(n, b, more):
                    if more:
                        turns(n + 1, b + 1)
                    pe.wait_ge(S("oneh_copied"), n + (gb + 1))
                    for k in range(S2):
                        if k == S2 // 2 and more:
                            fetch(n + 1)
                        pe.wait_ge(S("scaled"), n * S2 + (sb_ + k + 1))
                        pe.wait_ge(S("step_done"), n * S2 + (sb_ + k + 1))
                        for u in (2 * k, 2 * k + 1):
                            ins = mm(bank(k)[:, 0:c + 16], oneh[:, b % 2, u, :], R[:, b, u, 0:c + 16],
                                     start=(u % 2 == 0), stop=(u % 2 == 1))
                        ins.then_inc(S("summed"), 1)

                turns(0, 0)
                fetch(0)
                with pe.Fori(0, es.turns) as i:
                    for b in range(NBUF):
                        group(i * NBUF + b, b, True)
                for n in range(es.turns * NBUF, es.groups):
                    group(n, n % NBUF, n + 1 < es.groups)

            pe.wait_ge(S("xn_ready"), 1)
            x_turn("xT0", nodes(R2))
            pe.wait_ge(S("wT_ready"), 1)
            pe.wait_ge(S("xt_ready"), 1)

            def q_rows(t, kk):
                for k in range(2):
                    ins = mm(bank(kk)[:, 0:320], wT[:, k, t // 10, :], XT[:, k, (t % 10) * 320:(t % 10 + 1) * 320],
                             start=(k == 0), stop=(k == 1))
                return ins
            fill(pe, "q", q_rows)
            product("kv", lambda k: wT[:, k, 2:6, :].rearrange("p o m -> p (o m)"), 512)

            def context(Kv, rhs):
                for a in range(2):
                    for t in range(T):
                        kk = P if t < T - 1 else TAIL
                        r = rhs(a, t, kk)
                        ins = mm(bank(6 + a)[:, 0:r.shape[-1]], Kv[0:kk, t, a * P:(a + 1) * P], r,
                                 start=(t == 0), stop=(t == T - 1))
                ins.then_inc(S("ctx_ps"), 1)

            pe.wait_ge(S("k_ready"), 1)
            context(K0, lambda a, t, kk: V0[0:kk, t, a, :])
            pe.wait_ge(S("ctx_ready"), 1)
            pe.wait_ge(S("att_used"), 1)
            product("h0", lambda k: Wn[:, k, :], C + 16)

            def mixo(t, kk):
                for a in range(2):
                    ins = mm(bank(kk)[:, a * 132:(a + 1) * 132], qT[:, a, t * P:(t + 1) * P], BD[:, a, :],
                             start=True, stop=True)
                return ins
            fill(pe, "mixo", mixo)
            pe.wait_ge(S("ao_ready"), 1)
            x_turn("aT", AO)
            pe.wait_ge(S("aT_ready"), 1)
            product("proj", lambda k: wT[:, k, 6:8, :].rearrange("p o m -> p (o m)"), C)
            sort_offsets(1)
            gat(0, *GATS[0])
            x_turn("xT1", Av(C)[:, :, 0:C], 2)
            pe.wait_ge(S("att_used"), 2)
            pe.wait_ge(S("xt_ready"), 2)
            product("h1", lambda k: Wn[:, k, :], C + 16)
            prepare(FFN, 1)
            gat(1, *GATS[1])
            pe.wait_ge(S("xn_ready"), 7)
            x_turn("xT2", nodes(R2))
            pe.wait_ge(S("att_used"), 3)
            pe.wait_ge(S("xt_ready"), 3)
            product("h2", lambda k: Wn[:, k, 0:32], 32)
            gat(2, *GATS[2])

            pe.wait_ge(S("ld_moe"), 64)
            turn(bank(7)[:, 0:16], b1e, 16).then_inc(S("b1_ps"), 1)
            pe.wait_ge(S("b1_ready"), 1)
            pe.wait_ge(S("fin_done"), 3)
            pe.sem_inc(S("hid_free"), 4)
            pe.sem_inc(S("moe_full"), 2 * TB)

            with pe.Fori(0, T // TB) as i:
                def up_proj(e):
                    for f in range(4):
                        for hf in range(2):
                            m = (e * 4 + f) * 2 + hf
                            pe.wait_ge(S("hid_free"), i * 32 + (m + 1))
                            for k in range(2):
                                ins = mm(bank(4 + m % 4)[:, 0:320], W1e[:, e, k, f * P:(f + 1) * P],
                                         XT[:, k, bass.ds(i * TOK + hf * 320, 320)], start=(k == 0), stop=(k == 1))
                            ins.then_inc(S("hid_full"), 1)

                def down_proj(e):
                    pe.wait_ge(S("hid_free"), i * 32 + (4 + 8 * (e + 1)))
                    for k in range(TB):
                        o = e * TB + k
                        pe.wait_ge(S("moe_free"), i * (EXP0 * TB) + (o + 1))
                        for f in range(4):
                            ins = mm(bank(o % 4)[:, 0:C], hh[:, e % 2, f, k * P:(k + 1) * P], W2e[:, e, f, :],
                                     start=(f == 0), stop=(f == 3))
                        ins.then_inc(S("moe_full"), 1)

                up_proj(0)
                for e in range(EXP0):
                    if e < EXP0 - 1:
                        up_proj(e + 1)
                    down_proj(e)

            pe.wait_ge(S("xn_ready"), 8)
            pe.wait_ge(S("moe0_done"), 1)
            x_turn("xT3", nodes(R2))
            pe.wait_ge(S("xt_ready"), 4)
            pe.wait_ge(S("att_used"), 4)
            product("h3", lambda k: Wn[:, k, :], C + 16)
            pe.wait_ge(S("mix1_kv"), 1)
            context(K1, lambda a, t, kk: V1[0:kk, t, a * P:(a + 1) * P])
            pe.wait_ge(S("ctx_ready"), 2)

            def mix1o(t, kk):
                for a in range(2):
                    ins = mm(bank(kk)[:, a * P:(a + 1) * P], XT[:, a, t * P:(t + 1) * P], BD[:, a, 0:P],
                             start=True, stop=True)
                return ins
            fill(pe, "mix1o", mix1o)
            gat(3, *GATS[3])

            for n, src in enumerate((Av(C), nodes(R4))):
                for t in range(T):
                    if t % TB == 0:
                        pe.wait_ge(S("bn_in"), n * (T // TB) + t // TB + 1)
                    kk = P if t < T - 1 else TAIL
                    ins = mm(bank(0)[:, 0:C], ones[0:kk, :], src[0:kk, t, 0:C], start=(t == 0), stop=(t == T - 1))
                ins.then_inc(S("bank_full"), 1)

            pe.wait_ge(S("ld_moe1"), 16 * 6)
            turn(bank(7)[0:64, 0:32], b1r, 32)
            for k in range(2):
                ins = turn(bank(7)[:, 64 + 32 * k:96 + 32 * k], rwr[:, k * P:(k + 1) * P], 32)
            ins.then_inc(S("b1_ps"), 1)
            pe.wait_ge(S("xn_ready"), 9)
            x_turn("xT4", nodes(R1))
            pe.wait_ge(S("xt_ready"), 5)
            pe.wait_ge(S("b1_ready"), 2)
            product("rt", lambda k: rwT[:, k, :], 32)
            pe.wait_ge(S("choice"), 1)
            for hf, (t0, t1) in enumerate(((0, 13), (13, T))):
                mm(bank(5 + hf)[:, 0:(t1 - t0) * 32], lower, lg[:, t0:t1, :].rearrange("p t e -> p (t e)"),
                   start=True, stop=False)
                mm(bank(5 + hf)[:, 0:(t1 - t0) * 32], ones[:, :], before[:, t0:t1, :].rearrange("p t e -> p (t e)"),
                   start=False, stop=True)
            mm(bank(7)[:, 0:32], ones[:, :], before[:, T, :], start=True, stop=True).then_inc(S("places_ps"), 1)
            pe.wait_ge(S("owners_ready"), 1)
            pe.sem_inc(S("up_ps"), 2)
            pe.sem_inc(S("down_ps"), 2)

            def turn_x(n, k, i):
                if k % SB == 0:
                    pe.wait_ge(S(f"ld_xs{k // SB % 2}"), i * 16 + 16)
                pe.wait_ge(S("xs_copied"), n + 1)
                for h in range(2):
                    ins = turn(bank(k % 2)[:, h * P:(h + 1) * P], xs[:, k // SB % 2, k % SB, h * P:(h + 1) * P])
                ins.then_inc(S("xs_ps"), 1)

            def up(n, b):
                pe.wait_ge(S("xs_copied"), n + 3)
                pe.wait_ge(S("w1_ready"), n + 1)
                pe.wait_ge(S("hs_ready"), n + 1)
                for h in range(2):
                    ins = mm(bank(2 + b)[0:64, 0:P], w1s[:, b, h, :], xsT[:, b, h, :], start=(h == 0), stop=(h == 1))
                ins.then_inc(S("up_ps"), 1)

            def down(n, b, at_):
                pe.wait_ge(S("hs_ready"), n + 3)
                pe.wait_ge(S("ys_copied"), n + 1)
                mm(bank(4 + b)[:, 0:C], hs[:, b, :], W2x[:, bass.ds(at_, C)], start=True, stop=True).then_inc(S("down_ps"), 1)

            def turn8(i, end):
                w2 = offsets(mybir.EngineType.PE, w2_at, i * TURN, TURN, (EXP1 - 1) * C)
                for k in range(TURN):
                    if k + 2 < TURN or not end:
                        turn_x(i * TURN + (k + 2), k + 2 if k + 2 < TURN else k + 2 - TURN, i if k + 2 < TURN else i + 1)
                    if k + 1 < TURN or not end:
                        up(i * TURN + (k + 1), (k + 1) % 2)
                    down(i * TURN + k, k % 2, w2[k])
            turn_x(0, 0, 0)
            turn_x(1, 1, 0)
            up(0, 0)
            last = SLOTS // TURN - 1
            with pe.Fori(0, last) as i:
                turn8(i, False)
            turn8(last, True)


_OUTS = [((N, C), "float32")]
_INS = ['x', 'src', 'dst', 'L0_gnn_W1', 'L0_gnn_att_src1', 'L0_gnn_att_dst1', 'L0_gnn_b1', 'L0_gnn_W2',
        'L0_gnn_att_src2', 'L0_gnn_att_dst2', 'L0_gnn_b2', 'L0_mix_Wq', 'L0_mix_Wkv', 'L0_mix_Wproj',
        'L0_mix_bproj', 'L0_ffn_W_gat', 'L0_ffn_att_src', 'L0_ffn_att_dst', 'L0_ffn_b_gat', 'L0_ffn_ln_gamma',
        'L0_ffn_ln_beta', 'L0_ffn_W1', 'L0_ffn_b1', 'L0_ffn_W2', 'L0_ffn_b2', 'L0_ffn_edge_index', 'L1_gnn_W',
        'L1_gnn_att_src', 'L1_gnn_att_dst', 'L1_gnn_bias', 'L1_gnn_gamma', 'L1_gnn_beta', 'L1_mix_kln_weight',
        'L1_mix_kln_bias', 'L1_mix_vln_weight', 'L1_mix_vln_bias', 'L1_ffn_router_w', 'L1_ffn_router_b',
        'L1_ffn_W1', 'L1_ffn_b1', 'L1_ffn_W2', 'L1_ffn_b2']


def kernel(**inputs):
    import concourse.bacc as _bacc
    from concourse.bass_utils import run_bass_kernel_spmd as _run

    nc = _bacc.Bacc("TRN2", target_bir_lowering=False, num_devices=1)
    arrays, aps = {}, {}
    for name in _INS:
        a = np.ascontiguousarray(inputs[name])
        arrays[f"in_{name}"] = a
        aps[name] = nc.dram_tensor(f"in_{name}", a.shape, mybir.dt.from_np(a.dtype), kind="ExternalInput").ap()
    res = nc.dram_tensor("out_0", (N, C), F32, kind="ExternalOutput").ap()
    build(nc, aps, res)
    r = _run(nc, [arrays], core_ids=[0])
    return r.results[0]["out_0"]
```
